# Optimizing a Trainium2 kernel written in Bass

```python
import numpy as np
import jax
import jax.numpy as jnp

def _softmax(x, axis=-1):
    return jax.nn.softmax(x, axis=axis)
def _gelu(x):
    return jax.nn.gelu(x, approximate=True)
def _silu(x):
    return jax.nn.silu(x)
def _sigmoid(x):
    return jax.nn.sigmoid(x)
def _layernorm(x, axis=-1, eps=1e-5):
    m = jnp.mean(x, axis=axis, keepdims=True)
    v = jnp.var(x, axis=axis, keepdims=True)
    return (x - m) / jnp.sqrt(v + eps)
def _scatter_add(tgt, idx, src, axis=0):
    return tgt.at[idx].add(src)
def _segment_sum(src, seg, n):
    return jax.ops.segment_sum(src, seg, n)

kernel_name = 'mk_conv_preact_d4_conv_nchw256_e988b3'

def setup_inputs(seed: int = 0):
    np.random.seed(seed)
    _w = jnp.asarray
    def _rec_inputs():
        import jax
        import jax.numpy as jnp
        _gk = jax.random.key(seed)
        x = -0.0002928 + 1 * jax.random.normal(jax.random.fold_in(_gk, 1), (4, 256, 64, 64), jnp.float32)
        return x
    x = _rec_inputs()
    def _L0_conv_setup():
        import jax, jax.numpy as jnp
        from jax import lax
        import numpy as np
        N, C, H, W = (4, 256, 64, 64)
        K, PAD, DIL, G = (3, 6, 6, 4)
        GC = C // G
        P = K * K
        SLOPE = 0.01
        EPS = 1e-05

        def _bn(x, g, b, m, v, axis):
            sh = [1] * x.ndim
            sh[axis] = -1
            inv = g / jnp.sqrt(v + EPS)
            return x * inv.reshape(sh) + (b - m * inv).reshape(sh)

        def _grid_sample(img, grid):
            B, Cc, Hi, Wi = img.shape
            gx = (grid[..., 0] + 1.0) * (Wi * 0.5) - 0.5
            gy = (grid[..., 1] + 1.0) * (Hi * 0.5) - 0.5
            x0 = jnp.floor(gx).astype(jnp.int32)
            y0 = jnp.floor(gy).astype(jnp.int32)
            wx = gx - x0
            wy = gy - y0
            flat = img.reshape(B, Cc, Hi * Wi)

            def tap(xi, yi, w):
                valid = (xi >= 0) & (xi < Wi) & (yi >= 0) & (yi < Hi)
                idx = jnp.clip(yi, 0, Hi - 1) * Wi + jnp.clip(xi, 0, Wi - 1)
                v = jnp.take_along_axis(flat, idx.reshape(B, 1, -1), axis=2)
                v = v.reshape(B, Cc, *xi.shape[1:])
                return v * (w * valid.astype(img.dtype))[:, None]
            return tap(x0, y0, (1 - wx) * (1 - wy)) + tap(x0 + 1, y0, wx * (1 - wy)) + tap(x0, y0 + 1, (1 - wx) * wy) + tap(x0 + 1, y0 + 1, wx * wy)

        def _forward(x, conv_w, bn1_g, bn1_b, bn1_m, bn1_v, dw_w, dw_b, dwbn_g, dwbn_b, dwbn_m, dwbn_v, off_w, off_b, mask_w, mask_b, inproj_w, inproj_b, outproj_w, outproj_b, bn2_g, bn2_b, bn2_m, bn2_v, se_down_w, se_down_b, se_up_w, se_up_b, fc1_w, fc1_b, fc2_w, fc2_b):
            n = x.shape[0]
            y = jnp.einsum('nchw,oc->nohw', x, conv_w)
            y = jax.nn.leaky_relu(_bn(y, bn1_g, bn1_b, bn1_m, bn1_v, 1), SLOPE)
            inp = y.transpose(0, 2, 3, 1)
            xp = jnp.einsum('nhwc,oc->nhwo', inp, inproj_w) + inproj_b
            t = lax.conv_general_dilated(y, dw_w, (1, 1), [((K - 1) // 2,) * 2] * 2, dimension_numbers=('NCHW', 'OIHW', 'NCHW'), feature_group_count=C) + dw_b[None, :, None, None]
            t = jax.nn.leaky_relu(_bn(t, dwbn_g, dwbn_b, dwbn_m, dwbn_v, 1), SLOPE)
            t = t.transpose(0, 2, 3, 1)
            offset = jnp.einsum('nhwc,oc->nhwo', t, off_w) + off_b
            mlog = jnp.einsum('nhwc,oc->nhwo', t, mask_w) + mask_b
            mask = jax.nn.softmax(mlog.reshape(n, H, W, G, P), -1).reshape(n, H, W, G * P)
            xpad = jnp.pad(xp, ((0, 0), (PAD, PAD), (PAD, PAD), (0, 0)))
            Hp, Wp = (H + 2 * PAD, W + 2 * PAD)
            base = DIL * (K - 1) // 2 + 0.5
            ref_x = (base + jnp.arange(W, dtype=x.dtype)) / Wp
            ref_y = (base + jnp.arange(H, dtype=x.dtype)) / Hp
            ref = jnp.stack(jnp.broadcast_arrays(ref_x[None, :], ref_y[:, None]), -1)
            d = jnp.arange(K, dtype=x.dtype) * DIL - DIL * (K - 1) // 2
            gxx, gyy = jnp.meshgrid(d / Wp, d / Hp, indexing='ij')
            dil_grid = jnp.tile(jnp.stack([gxx, gyy], -1).reshape(1, P, 2), (G, 1, 1)).reshape(G * P, 2)
            loc = (ref[:, :, None, :] + dil_grid[None, None]).reshape(1, H, W, G * P * 2)
            norm = jnp.tile(jnp.array([Wp, Hp], x.dtype), G * P)
            sg = 2.0 * (loc + offset / norm) - 1.0
            sg = sg.reshape(n, H * W, G, P, 2).transpose(0, 2, 1, 3, 4).reshape(n * G, H * W, P, 2)
            img = xpad.transpose(0, 3, 1, 2).reshape(n * G, GC, Hp, Wp)
            samp = _grid_sample(img, sg)
            mr = mask.reshape(n, H * W, G, P).transpose(0, 2, 1, 3).reshape(n * G, 1, H * W, P)
            dout = (samp * mr).sum(-1).reshape(n, G * GC, H * W).transpose(0, 2, 1).reshape(n, H, W, C)
            dout = jnp.einsum('nhwc,oc->nhwo', dout, outproj_w) + outproj_b
            x2 = _bn(inp + dout, bn2_g, bn2_b, bn2_m, bn2_v, 3)
            s = x2.mean((1, 2))
            s = jax.nn.relu(s @ se_down_w.T + se_down_b)
            s = jax.nn.sigmoid(s @ se_up_w.T + se_up_b)
            x3 = x2 * s[:, None, None, :]
            hmid = jax.nn.leaky_relu(jnp.einsum('nhwc,oc->nhwo', x3, fc1_w) + fc1_b, SLOPE)
            m = jnp.einsum('nhwc,oc->nhwo', hmid, fc2_w) + fc2_b
            return (inp + m).transpose(0, 3, 1, 2)
        key = jax.random.key(seed)
        ks = jax.random.split(key, 40)
        f = jnp.float32
        nrm = lambda k, sh, sc: jax.random.normal(k, sh, f) * sc
        uni = lambda k, sh: jax.random.uniform(k, sh, f, 0.5, 1.5)
        s = 1.0 / float(np.sqrt(C))
        return {'x': nrm(ks[0], (N, C, H, W), 1.0), 'conv_w': nrm(ks[1], (C, C), s), 'bn1_g': uni(ks[2], (C,)), 'bn1_b': nrm(ks[3], (C,), 0.1), 'bn1_m': nrm(ks[4], (C,), 0.1), 'bn1_v': uni(ks[5], (C,)), 'dw_w': nrm(ks[6], (C, 1, K, K), 1.0 / 3.0), 'dw_b': nrm(ks[7], (C,), 0.05), 'dwbn_g': uni(ks[8], (C,)), 'dwbn_b': nrm(ks[9], (C,), 0.1), 'dwbn_m': nrm(ks[10], (C,), 0.1), 'dwbn_v': uni(ks[11], (C,)), 'off_w': nrm(ks[12], (G * P * 2, C), s), 'off_b': nrm(ks[13], (G * P * 2,), 0.02), 'mask_w': nrm(ks[14], (G * P, C), s), 'mask_b': nrm(ks[15], (G * P,), 0.02), 'inproj_w': nrm(ks[16], (C, C), s), 'inproj_b': nrm(ks[17], (C,), 0.02), 'outproj_w': nrm(ks[18], (C, C), s), 'outproj_b': nrm(ks[19], (C,), 0.02), 'bn2_g': uni(ks[20], (C,)), 'bn2_b': nrm(ks[21], (C,), 0.1), 'bn2_m': nrm(ks[22], (C,), 0.1), 'bn2_v': uni(ks[23], (C,)), 'se_down_w': nrm(ks[24], (C // 4, C), s), 'se_down_b': nrm(ks[25], (C // 4,), 0.02), 'se_up_w': nrm(ks[26], (C, C // 4), 1.0 / float(np.sqrt(C // 4))), 'se_up_b': nrm(ks[27], (C,), 0.02), 'fc1_w': nrm(ks[28], (4 * C, C), s), 'fc1_b': nrm(ks[29], (4 * C,), 0.02), 'fc2_w': nrm(ks[30], (C, 4 * C), 1.0 / float(np.sqrt(4 * C))), 'fc2_b': nrm(ks[31], (C,), 0.02)}
    _L0_conv_all = _L0_conv_setup()
    _L0_conv_in = {k: v for k, v in _L0_conv_all.items() if k in ('conv_w', 'bn1_g', 'bn1_b', 'bn1_m', 'bn1_v', 'dw_w', 'dw_b', 'dwbn_g', 'dwbn_b', 'dwbn_m', 'dwbn_v', 'off_w', 'off_b', 'mask_w', 'mask_b', 'inproj_w', 'inproj_b', 'outproj_w', 'outproj_b', 'bn2_g', 'bn2_b', 'bn2_m', 'bn2_v', 'se_down_w', 'se_down_b', 'se_up_w', 'se_up_b', 'fc1_w', 'fc1_b', 'fc2_w', 'fc2_b', )}
    del _L0_conv_all

    def _L1_conv_setup():
        import jax, jax.numpy as jnp
        import numpy as np
        import math

        def _rotate_one(kernel, angle):
            kH, kW = (kernel.shape[2], kernel.shape[3])
            cy, cx = ((kH - 1) / 2.0, (kW - 1) / 2.0)
            y = jnp.arange(kH, dtype=kernel.dtype) - cy
            x = jnp.arange(kW, dtype=kernel.dtype) - cx
            yy, xx = jnp.meshgrid(y, x, indexing='ij')
            c, s = (jnp.cos(angle), jnp.sin(angle))
            x_rot = xx * c + yy * s + cx
            y_rot = -xx * s + yy * c + cy
            x0 = jnp.clip(jnp.floor(x_rot), 0, kW - 2)
            y0 = jnp.clip(jnp.floor(y_rot), 0, kH - 2)
            x1 = x0 + 1
            y1 = y0 + 1
            w00 = (x1 - x_rot) * (y1 - y_rot)
            w01 = (x1 - x_rot) * (y_rot - y0)
            w10 = (x_rot - x0) * (y1 - y_rot)
            w11 = (x_rot - x0) * (y_rot - y0)
            x0i = x0.astype(jnp.int32)
            y0i = y0.astype(jnp.int32)
            x1i = x1.astype(jnp.int32)
            y1i = y1.astype(jnp.int32)
            return w00 * kernel[..., y0i, x0i] + w01 * kernel[..., y1i, x0i] + w10 * kernel[..., y0i, x1i] + w11 * kernel[..., y1i, x1i]
        key = jax.random.key(seed)
        ks = jax.random.split(key, 6)
        B, C, H, W = (16, 256, 64, 64)
        G, Cg, K = (8, 32, 3)
        HID = C // 4
        fan_out = Cg * K * K
        return {'x': jax.random.normal(ks[0], (B, C, H, W), jnp.float32), 'base_kernel': jax.random.normal(ks[1], (G, Cg, Cg, K, K), jnp.float32) * np.sqrt(2.0 / fan_out), 'ap_w1': jax.random.normal(ks[2], (HID, C), jnp.float32) * np.sqrt(1.0 / C), 'ap_b1': jnp.zeros((HID,), jnp.float32), 'ap_w2': jax.random.normal(ks[3], (G, HID), jnp.float32) * np.sqrt(1.0 / HID), 'ap_b2': jnp.zeros((G,), jnp.float32), 'meta_w1': jax.random.normal(ks[4], (HID, C), jnp.float32) * np.sqrt(1.0 / C), 'meta_b1': jnp.zeros((HID,), jnp.float32), 'meta_w2': jax.random.normal(ks[5], (C, HID), jnp.float32) * np.sqrt(1.0 / HID), 'meta_b2': jnp.zeros((C,), jnp.float32)}
    _L1_conv_all = _L1_conv_setup()
    _L1_conv_in = {k: v for k, v in _L1_conv_all.items() if k in ('base_kernel', 'ap_w1', 'ap_b1', 'ap_w2', 'ap_b2', 'meta_w1', 'meta_b1', 'meta_w2', 'meta_b2', )}
    del _L1_conv_all

    def _L2_conv_setup():
        import jax, jax.numpy as jnp
        import numpy as np
        DIM = 256
        HEADS = 8
        DIM_HEAD = 64
        HIDDEN = HEADS * DIM_HEAD
        SCALE = DIM_HEAD ** (-0.5)
        BN_EPS = 1e-05
        key = jax.random.key(seed)
        k1, k2, k3, k4 = jax.random.split(key, 4)
        x = jax.random.normal(k1, (32, DIM, 32, 32), dtype=jnp.float32)
        w_qkv = jax.random.normal(k2, (3 * HIDDEN, DIM), dtype=jnp.float32) * DIM ** (-0.5)
        w_out = jax.random.normal(k3, (DIM, HIDDEN), dtype=jnp.float32) * HIDDEN ** (-0.5)
        b_out = jax.random.normal(k4, (DIM,), dtype=jnp.float32) * 0.02
        gamma = jnp.ones((DIM,), dtype=jnp.float32)
        beta = jnp.zeros((DIM,), dtype=jnp.float32)
        return {'x': x, 'w_qkv': w_qkv, 'w_out': w_out, 'b_out': b_out, 'gamma': gamma, 'beta': beta}
    _L2_conv_all = _L2_conv_setup()
    _L2_conv_in = {k: v for k, v in _L2_conv_all.items() if k in ('w_qkv', 'w_out', 'b_out', 'gamma', 'beta', )}
    del _L2_conv_all

    def _L3_conv_setup():
        import jax, jax.numpy as jnp
        import numpy as np
        GC = 64
        GROUPS = GC // 4
        BIT = 4
        QN, QP = (-2 ** (BIT - 1), 2 ** (BIT - 1) - 1)

        def fake_quant(w, s):
            r = w / s
            r_ste = r + jax.lax.stop_gradient(jnp.round(r) - r)
            return jnp.clip(r_ste, QN, QP) * s

        def qconv(x, w, b, s, padding):
            w_q = fake_quant(w, s)
            y = jax.lax.conv_general_dilated(x, w_q, window_strides=(1, 1), padding=padding, dimension_numbers=('NCHW', 'OIHW', 'NCHW'), feature_group_count=GROUPS)
            return y + b[None, :, None, None]
        key = jax.random.key(seed)
        ks = jax.random.split(key, 7)
        x = jax.random.normal(ks[0], (64, 256, 64, 64), dtype=jnp.float32)
        w_hw = jax.random.normal(ks[1], (GC, 4, 3, 3), dtype=jnp.float32) * 0.1
        w_w = jax.random.normal(ks[2], (GC, 4, 1, 11), dtype=jnp.float32) * 0.1
        w_h = jax.random.normal(ks[3], (GC, 4, 11, 1), dtype=jnp.float32) * 0.1
        b_hw = jax.random.normal(ks[4], (GC,), dtype=jnp.float32) * 0.01
        b_w = jax.random.normal(ks[5], (GC,), dtype=jnp.float32) * 0.01
        b_h = jax.random.normal(ks[6], (GC,), dtype=jnp.float32) * 0.01
        s_hw = jnp.max(jnp.abs(w_hw)) / QP
        s_w = jnp.max(jnp.abs(w_w)) / QP
        s_h = jnp.max(jnp.abs(w_h)) / QP
        return {'x': x, 'w_hw': w_hw, 'b_hw': b_hw, 's_hw': s_hw, 'w_w': w_w, 'b_w': b_w, 's_w': s_w, 'w_h': w_h, 'b_h': b_h, 's_h': s_h}
    _L3_conv_all = _L3_conv_setup()
    _L3_conv_in = {k: v for k, v in _L3_conv_all.items() if k in ('w_hw', 'b_hw', 's_hw', 'w_w', 'b_w', 's_w', 'w_h', 'b_h', 's_h', )}
    del _L3_conv_all

    return {
        "x": x,
        "L0_conv_conv_w": _L0_conv_in["conv_w"],
        "L0_conv_bn1_g": _L0_conv_in["bn1_g"],
        "L0_conv_bn1_b": _L0_conv_in["bn1_b"],
        "L0_conv_bn1_m": _L0_conv_in["bn1_m"],
        "L0_conv_bn1_v": _L0_conv_in["bn1_v"],
        "L0_conv_dw_w": _L0_conv_in["dw_w"],
        "L0_conv_dw_b": _L0_conv_in["dw_b"],
        "L0_conv_dwbn_g": _L0_conv_in["dwbn_g"],
        "L0_conv_dwbn_b": _L0_conv_in["dwbn_b"],
        "L0_conv_dwbn_m": _L0_conv_in["dwbn_m"],
        "L0_conv_dwbn_v": _L0_conv_in["dwbn_v"],
        "L0_conv_off_w": _L0_conv_in["off_w"],
        "L0_conv_off_b": _L0_conv_in["off_b"],
        "L0_conv_mask_w": _L0_conv_in["mask_w"],
        "L0_conv_mask_b": _L0_conv_in["mask_b"],
        "L0_conv_inproj_w": _L0_conv_in["inproj_w"],
        "L0_conv_inproj_b": _L0_conv_in["inproj_b"],
        "L0_conv_outproj_w": _L0_conv_in["outproj_w"],
        "L0_conv_outproj_b": _L0_conv_in["outproj_b"],
        "L0_conv_bn2_g": _L0_conv_in["bn2_g"],
        "L0_conv_bn2_b": _L0_conv_in["bn2_b"],
        "L0_conv_bn2_m": _L0_conv_in["bn2_m"],
        "L0_conv_bn2_v": _L0_conv_in["bn2_v"],
        "L0_conv_se_down_w": _L0_conv_in["se_down_w"],
        "L0_conv_se_down_b": _L0_conv_in["se_down_b"],
        "L0_conv_se_up_w": _L0_conv_in["se_up_w"],
        "L0_conv_se_up_b": _L0_conv_in["se_up_b"],
        "L0_conv_fc1_w": _L0_conv_in["fc1_w"],
        "L0_conv_fc1_b": _L0_conv_in["fc1_b"],
        "L0_conv_fc2_w": _L0_conv_in["fc2_w"],
        "L0_conv_fc2_b": _L0_conv_in["fc2_b"],
        "L1_conv_base_kernel": _L1_conv_in["base_kernel"],
        "L1_conv_ap_w1": _L1_conv_in["ap_w1"],
        "L1_conv_ap_b1": _L1_conv_in["ap_b1"],
        "L1_conv_ap_w2": _L1_conv_in["ap_w2"],
        "L1_conv_ap_b2": _L1_conv_in["ap_b2"],
        "L1_conv_meta_w1": _L1_conv_in["meta_w1"],
        "L1_conv_meta_b1": _L1_conv_in["meta_b1"],
        "L1_conv_meta_w2": _L1_conv_in["meta_w2"],
        "L1_conv_meta_b2": _L1_conv_in["meta_b2"],
        "L2_conv_w_qkv": _L2_conv_in["w_qkv"],
        "L2_conv_w_out": _L2_conv_in["w_out"],
        "L2_conv_b_out": _L2_conv_in["b_out"],
        "L2_conv_gamma": _L2_conv_in["gamma"],
        "L2_conv_beta": _L2_conv_in["beta"],
        "L3_conv_w_hw": _L3_conv_in["w_hw"],
        "L3_conv_b_hw": _L3_conv_in["b_hw"],
        "L3_conv_s_hw": _L3_conv_in["s_hw"],
        "L3_conv_w_w": _L3_conv_in["w_w"],
        "L3_conv_b_w": _L3_conv_in["b_w"],
        "L3_conv_s_w": _L3_conv_in["s_w"],
        "L3_conv_w_h": _L3_conv_in["w_h"],
        "L3_conv_b_h": _L3_conv_in["b_h"],
        "L3_conv_s_h": _L3_conv_in["s_h"],
    }

def reference(x, L0_conv_conv_w, L0_conv_bn1_g, L0_conv_bn1_b, L0_conv_bn1_m, L0_conv_bn1_v, L0_conv_dw_w, L0_conv_dw_b, L0_conv_dwbn_g, L0_conv_dwbn_b, L0_conv_dwbn_m, L0_conv_dwbn_v, L0_conv_off_w, L0_conv_off_b, L0_conv_mask_w, L0_conv_mask_b, L0_conv_inproj_w, L0_conv_inproj_b, L0_conv_outproj_w, L0_conv_outproj_b, L0_conv_bn2_g, L0_conv_bn2_b, L0_conv_bn2_m, L0_conv_bn2_v, L0_conv_se_down_w, L0_conv_se_down_b, L0_conv_se_up_w, L0_conv_se_up_b, L0_conv_fc1_w, L0_conv_fc1_b, L0_conv_fc2_w, L0_conv_fc2_b, L1_conv_base_kernel, L1_conv_ap_w1, L1_conv_ap_b1, L1_conv_ap_w2, L1_conv_ap_b2, L1_conv_meta_w1, L1_conv_meta_b1, L1_conv_meta_w2, L1_conv_meta_b2, L2_conv_w_qkv, L2_conv_w_out, L2_conv_b_out, L2_conv_gamma, L2_conv_beta, L3_conv_w_hw, L3_conv_b_hw, L3_conv_s_hw, L3_conv_w_w, L3_conv_b_w, L3_conv_s_w, L3_conv_w_h, L3_conv_b_h, L3_conv_s_h):
    import jax
    import jax.numpy as jnp
    def _L0_conv_ref(x, conv_w, bn1_g, bn1_b, bn1_m, bn1_v, dw_w, dw_b, dwbn_g, dwbn_b, dwbn_m, dwbn_v, off_w, off_b, mask_w, mask_b, inproj_w, inproj_b, outproj_w, outproj_b, bn2_g, bn2_b, bn2_m, bn2_v, se_down_w, se_down_b, se_up_w, se_up_b, fc1_w, fc1_b, fc2_w, fc2_b):
        import jax, jax.numpy as jnp
        from jax import lax
        import numpy as np
        N, C, H, W = (4, 256, 64, 64)
        K, PAD, DIL, G = (3, 6, 6, 4)
        GC = C // G
        P = K * K
        SLOPE = 0.01
        EPS = 1e-05

        def _bn(x, g, b, m, v, axis):
            sh = [1] * x.ndim
            sh[axis] = -1
            inv = g / jnp.sqrt(v + EPS)
            return x * inv.reshape(sh) + (b - m * inv).reshape(sh)

        def _grid_sample(img, grid):
            B, Cc, Hi, Wi = img.shape
            gx = (grid[..., 0] + 1.0) * (Wi * 0.5) - 0.5
            gy = (grid[..., 1] + 1.0) * (Hi * 0.5) - 0.5
            x0 = jnp.floor(gx).astype(jnp.int32)
            y0 = jnp.floor(gy).astype(jnp.int32)
            wx = gx - x0
            wy = gy - y0
            flat = img.reshape(B, Cc, Hi * Wi)

            def tap(xi, yi, w):
                valid = (xi >= 0) & (xi < Wi) & (yi >= 0) & (yi < Hi)
                idx = jnp.clip(yi, 0, Hi - 1) * Wi + jnp.clip(xi, 0, Wi - 1)
                v = jnp.take_along_axis(flat, idx.reshape(B, 1, -1), axis=2)
                v = v.reshape(B, Cc, *xi.shape[1:])
                return v * (w * valid.astype(img.dtype))[:, None]
            return tap(x0, y0, (1 - wx) * (1 - wy)) + tap(x0 + 1, y0, wx * (1 - wy)) + tap(x0, y0 + 1, (1 - wx) * wy) + tap(x0 + 1, y0 + 1, wx * wy)

        def _forward(x, conv_w, bn1_g, bn1_b, bn1_m, bn1_v, dw_w, dw_b, dwbn_g, dwbn_b, dwbn_m, dwbn_v, off_w, off_b, mask_w, mask_b, inproj_w, inproj_b, outproj_w, outproj_b, bn2_g, bn2_b, bn2_m, bn2_v, se_down_w, se_down_b, se_up_w, se_up_b, fc1_w, fc1_b, fc2_w, fc2_b):
            n = x.shape[0]
            y = jnp.einsum('nchw,oc->nohw', x, conv_w)
            y = jax.nn.leaky_relu(_bn(y, bn1_g, bn1_b, bn1_m, bn1_v, 1), SLOPE)
            inp = y.transpose(0, 2, 3, 1)
            xp = jnp.einsum('nhwc,oc->nhwo', inp, inproj_w) + inproj_b
            t = lax.conv_general_dilated(y, dw_w, (1, 1), [((K - 1) // 2,) * 2] * 2, dimension_numbers=('NCHW', 'OIHW', 'NCHW'), feature_group_count=C) + dw_b[None, :, None, None]
            t = jax.nn.leaky_relu(_bn(t, dwbn_g, dwbn_b, dwbn_m, dwbn_v, 1), SLOPE)
            t = t.transpose(0, 2, 3, 1)
            offset = jnp.einsum('nhwc,oc->nhwo', t, off_w) + off_b
            mlog = jnp.einsum('nhwc,oc->nhwo', t, mask_w) + mask_b
            mask = jax.nn.softmax(mlog.reshape(n, H, W, G, P), -1).reshape(n, H, W, G * P)
            xpad = jnp.pad(xp, ((0, 0), (PAD, PAD), (PAD, PAD), (0, 0)))
            Hp, Wp = (H + 2 * PAD, W + 2 * PAD)
            base = DIL * (K - 1) // 2 + 0.5
            ref_x = (base + jnp.arange(W, dtype=x.dtype)) / Wp
            ref_y = (base + jnp.arange(H, dtype=x.dtype)) / Hp
            ref = jnp.stack(jnp.broadcast_arrays(ref_x[None, :], ref_y[:, None]), -1)
            d = jnp.arange(K, dtype=x.dtype) * DIL - DIL * (K - 1) // 2
            gxx, gyy = jnp.meshgrid(d / Wp, d / Hp, indexing='ij')
            dil_grid = jnp.tile(jnp.stack([gxx, gyy], -1).reshape(1, P, 2), (G, 1, 1)).reshape(G * P, 2)
            loc = (ref[:, :, None, :] + dil_grid[None, None]).reshape(1, H, W, G * P * 2)
            norm = jnp.tile(jnp.array([Wp, Hp], x.dtype), G * P)
            sg = 2.0 * (loc + offset / norm) - 1.0
            sg = sg.reshape(n, H * W, G, P, 2).transpose(0, 2, 1, 3, 4).reshape(n * G, H * W, P, 2)
            img = xpad.transpose(0, 3, 1, 2).reshape(n * G, GC, Hp, Wp)
            samp = _grid_sample(img, sg)
            mr = mask.reshape(n, H * W, G, P).transpose(0, 2, 1, 3).reshape(n * G, 1, H * W, P)
            dout = (samp * mr).sum(-1).reshape(n, G * GC, H * W).transpose(0, 2, 1).reshape(n, H, W, C)
            dout = jnp.einsum('nhwc,oc->nhwo', dout, outproj_w) + outproj_b
            x2 = _bn(inp + dout, bn2_g, bn2_b, bn2_m, bn2_v, 3)
            s = x2.mean((1, 2))
            s = jax.nn.relu(s @ se_down_w.T + se_down_b)
            s = jax.nn.sigmoid(s @ se_up_w.T + se_up_b)
            x3 = x2 * s[:, None, None, :]
            hmid = jax.nn.leaky_relu(jnp.einsum('nhwc,oc->nhwo', x3, fc1_w) + fc1_b, SLOPE)
            m = jnp.einsum('nhwc,oc->nhwo', hmid, fc2_w) + fc2_b
            return (inp + m).transpose(0, 3, 1, 2)
        return _forward(x, conv_w, bn1_g, bn1_b, bn1_m, bn1_v, dw_w, dw_b, dwbn_g, dwbn_b, dwbn_m, dwbn_v, off_w, off_b, mask_w, mask_b, inproj_w, inproj_b, outproj_w, outproj_b, bn2_g, bn2_b, bn2_m, bn2_v, se_down_w, se_down_b, se_up_w, se_up_b, fc1_w, fc1_b, fc2_w, fc2_b)

    def _L1_conv_ref(x, base_kernel, ap_w1, ap_b1, ap_w2, ap_b2, meta_w1, meta_b1, meta_w2, meta_b2):
        import jax, jax.numpy as jnp
        import numpy as np
        import math

        def _rotate_one(kernel, angle):
            kH, kW = (kernel.shape[2], kernel.shape[3])
            cy, cx = ((kH - 1) / 2.0, (kW - 1) / 2.0)
            y = jnp.arange(kH, dtype=kernel.dtype) - cy
            x = jnp.arange(kW, dtype=kernel.dtype) - cx
            yy, xx = jnp.meshgrid(y, x, indexing='ij')
            c, s = (jnp.cos(angle), jnp.sin(angle))
            x_rot = xx * c + yy * s + cx
            y_rot = -xx * s + yy * c + cy
            x0 = jnp.clip(jnp.floor(x_rot), 0, kW - 2)
            y0 = jnp.clip(jnp.floor(y_rot), 0, kH - 2)
            x1 = x0 + 1
            y1 = y0 + 1
            w00 = (x1 - x_rot) * (y1 - y_rot)
            w01 = (x1 - x_rot) * (y_rot - y0)
            w10 = (x_rot - x0) * (y1 - y_rot)
            w11 = (x_rot - x0) * (y_rot - y0)
            x0i = x0.astype(jnp.int32)
            y0i = y0.astype(jnp.int32)
            x1i = x1.astype(jnp.int32)
            y1i = y1.astype(jnp.int32)
            return w00 * kernel[..., y0i, x0i] + w01 * kernel[..., y1i, x0i] + w10 * kernel[..., y0i, x1i] + w11 * kernel[..., y1i, x1i]
        B, C, H, W = x.shape
        G, Cg = (base_kernel.shape[0], base_kernel.shape[1])
        K = base_kernel.shape[-1]
        pad = (K - 1) // 2
        pooled = x.mean(axis=(2, 3))
        h = jax.nn.relu(pooled @ ap_w1.T + ap_b1)
        angles = jnp.tanh(h @ ap_w2.T + ap_b2) * (math.pi / 4)
        rot = jax.vmap(jax.vmap(_rotate_one), in_axes=(None, 0))(base_kernel, angles)
        w = rot.reshape(B * C, Cg, K, K)
        out = jax.lax.conv_general_dilated(x.reshape(1, B * C, H, W), w, window_strides=(1, 1), padding=[(pad, pad), (pad, pad)], dimension_numbers=('NCHW', 'OIHW', 'NCHW'), feature_group_count=B * G)
        feat = out.reshape(B, C, H, W)
        m = jax.nn.relu(pooled @ meta_w1.T + meta_b1)
        mod = jax.nn.sigmoid(m @ meta_w2.T + meta_b2)
        return feat * mod[:, :, None, None]

    def _L2_conv_ref(x, w_qkv, w_out, b_out, gamma, beta):
        import jax, jax.numpy as jnp
        import numpy as np
        DIM = 256
        HEADS = 8
        DIM_HEAD = 64
        HIDDEN = HEADS * DIM_HEAD
        SCALE = DIM_HEAD ** (-0.5)
        BN_EPS = 1e-05
        b, c, h, w = x.shape
        n = h * w
        xf = x.reshape(b, c, n)
        qkv = jnp.einsum('oc,bcn->bon', w_qkv, xf)
        q, k, v = jnp.split(qkv, 3, axis=1)
        q = q.reshape(b, HEADS, DIM_HEAD, n)
        k = k.reshape(b, HEADS, DIM_HEAD, n)
        v = v.reshape(b, HEADS, DIM_HEAD, n)
        q = jax.nn.softmax(q, axis=2) * SCALE
        k = jax.nn.softmax(k, axis=3)
        v = v / n
        context = jnp.einsum('bhdn,bhen->bhde', k, v)
        out = jnp.einsum('bhde,bhdn->bhen', context, q)
        out = out.reshape(b, HIDDEN, n)
        out = jnp.einsum('oc,bcn->bon', w_out, out) + b_out[None, :, None]
        mean = out.mean(axis=(0, 2), keepdims=True)
        var = out.var(axis=(0, 2), keepdims=True)
        out = (out - mean) * jax.lax.rsqrt(var + BN_EPS)
        out = out * gamma[None, :, None] + beta[None, :, None]
        return out.reshape(b, c, h, w)

    def _L3_conv_ref(x, w_hw, b_hw, s_hw, w_w, b_w, s_w, w_h, b_h, s_h):
        import jax, jax.numpy as jnp
        import numpy as np
        GC = 64
        GROUPS = GC // 4
        BIT = 4
        QN, QP = (-2 ** (BIT - 1), 2 ** (BIT - 1) - 1)

        def fake_quant(w, s):
            r = w / s
            r_ste = r + jax.lax.stop_gradient(jnp.round(r) - r)
            return jnp.clip(r_ste, QN, QP) * s

        def qconv(x, w, b, s, padding):
            w_q = fake_quant(w, s)
            y = jax.lax.conv_general_dilated(x, w_q, window_strides=(1, 1), padding=padding, dimension_numbers=('NCHW', 'OIHW', 'NCHW'), feature_group_count=GROUPS)
            return y + b[None, :, None, None]
        c = x.shape[1]
        id_c = c - 3 * GC
        x_id = x[:, :id_c]
        x_h = x[:, id_c:id_c + GC]
        x_w = x[:, id_c + GC:id_c + 2 * GC]
        x_hw = x[:, id_c + 2 * GC:]
        y_h = qconv(x_h, w_h, b_h, s_h, [(5, 5), (0, 0)])
        y_w = qconv(x_w, w_w, b_w, s_w, [(0, 0), (5, 5)])
        y_hw = qconv(x_hw, w_hw, b_hw, s_hw, [(1, 1), (1, 1)])
        return jnp.concatenate((x_id, y_h, y_w, y_hw), axis=1)

    def _gn(v, G=32, eps=1e-5):
        B_, C_, H_, W_ = v.shape
        g = v.reshape(B_, G, C_ // G, H_, W_)
        m = jnp.mean(g, axis=(2, 3, 4), keepdims=True)
        s = jnp.var(g, axis=(2, 3, 4), keepdims=True)
        return ((g - m) / jnp.sqrt(s + eps)).reshape(v.shape)

    def _ln_c(v, eps=1e-6):
        m = jnp.mean(v, axis=1, keepdims=True)
        s = jnp.var(v, axis=1, keepdims=True)
        return (v - m) / jnp.sqrt(s + eps)

    def _ln_t(v, eps=1e-5):
        m = jnp.mean(v, axis=-1, keepdims=True)
        s = jnp.var(v, axis=-1, keepdims=True)
        return (v - m) / jnp.sqrt(s + eps)

    def _to_tokens(v):
        B_, C_, H_, W_ = v.shape
        return v.reshape(B_, C_, H_ * W_).transpose(0, 2, 1)
    def _from_tokens(t, like):
        B_, C_, H_, W_ = like.shape
        return t.transpose(0, 2, 1).reshape(B_, C_, H_, W_)

    x = x + _L0_conv_ref(_gn(x), L0_conv_conv_w, L0_conv_bn1_g, L0_conv_bn1_b, L0_conv_bn1_m, L0_conv_bn1_v, L0_conv_dw_w, L0_conv_dw_b, L0_conv_dwbn_g, L0_conv_dwbn_b, L0_conv_dwbn_m, L0_conv_dwbn_v, L0_conv_off_w, L0_conv_off_b, L0_conv_mask_w, L0_conv_mask_b, L0_conv_inproj_w, L0_conv_inproj_b, L0_conv_outproj_w, L0_conv_outproj_b, L0_conv_bn2_g, L0_conv_bn2_b, L0_conv_bn2_m, L0_conv_bn2_v, L0_conv_se_down_w, L0_conv_se_down_b, L0_conv_se_up_w, L0_conv_se_up_b, L0_conv_fc1_w, L0_conv_fc1_b, L0_conv_fc2_w, L0_conv_fc2_b)
    x = x + _L1_conv_ref(_gn(x), L1_conv_base_kernel, L1_conv_ap_w1, L1_conv_ap_b1, L1_conv_ap_w2, L1_conv_ap_b2, L1_conv_meta_w1, L1_conv_meta_b1, L1_conv_meta_w2, L1_conv_meta_b2)
    x = x + _L2_conv_ref(_gn(x), L2_conv_w_qkv, L2_conv_w_out, L2_conv_b_out, L2_conv_gamma, L2_conv_beta)
    x = x + _L3_conv_ref(_gn(x), L3_conv_w_hw, L3_conv_b_hw, L3_conv_s_hw, L3_conv_w_w, L3_conv_b_w, L3_conv_s_w, L3_conv_w_h, L3_conv_b_h, L3_conv_s_h)
    return x


_drawn_inputs = setup_inputs


def setup_inputs(seed=0):
    import zlib

    import numpy as np

    out = dict(_drawn_inputs(seed))
    spreads = {'L1_conv_ap_b1': (0.0, 0.308),
     'L1_conv_ap_b2': (0.0, 0.1),
     'L1_conv_meta_b1': (0.0, 0.408),
     'L1_conv_meta_b2': (0.0, 0.358),
     'L2_conv_gamma': (1.0, 0.6),
     'L2_conv_beta': (0.0, 0.1)}
    factors = {'L0_conv_dw_b': 8.0,
     'L0_conv_dwbn_g': 3.103,
     'L0_conv_dwbn_b': 6.603,
     'L0_conv_dwbn_m': 6.357,
     'L0_conv_dwbn_v': 5.729,
     'L0_conv_off_b': 8.0,
     'L0_conv_inproj_b': 8.0,
     'L0_conv_outproj_b': 8.0,
     'L0_conv_se_down_b': 8.0,
     'L0_conv_se_up_b': 8.0,
     'L0_conv_fc1_b': 5.188,
     'L0_conv_fc2_b': 3.062,
     'L2_conv_w_qkv': 8.0,
     'L2_conv_w_out': 8.0,
     'L2_conv_b_out': 64.0,
     'L3_conv_b_hw': 23.111,
     'L3_conv_b_w': 8.0,
     'L3_conv_b_h': 8.0}
    for name, (base, spread) in spreads.items():
        noise = np.random.default_rng([zlib.crc32(name.encode()), seed]).standard_normal(out[name].shape)
        drawn = base * np.exp(spread * noise) if base else spread * noise
        out[name] = jnp.asarray(drawn.astype(out[name].dtype))
    for name, factor in factors.items():
        out[name] = (out[name] * factor).astype(out[name].dtype)
    return out
```

```python
from contextlib import ExitStack

import concourse.bass as bass
from concourse import mybir

ALU = mybir.AluOpType
ACT = mybir.ActivationFunctionType
AX_X = mybir.AxisListType.X
F32 = mybir.dt.float32
U32 = mybir.dt.uint32

B, C, H, W = 4, 256, 64, 64
P = 128
KC = C // P
HW = H * W
CHUNK = 512
ROWS = CHUNK // W
CHUNKS = HW // CHUNK
PAIRS = CHUNKS // 2
SUBS = CHUNK // P
TILES = HW // P
G, K2 = 4, 9
GC = C // G
PTS = G * K2
CORNERS = 4
DIL = 6
FC = 4 * C // P
HEADS, DH = 8, 64
HID = HEADS * DH
KH = HID // P
CG = 32
EPS = 1e-5
SLOPE = 0.01
MAGIC = 12582912.0
TAB_FRONT = W + 1
TAB_ROWS = HW + P
YPITCH = W + 2
YPLANE = (H + 2) * YPITCH
P0_PITCH, P0_ROWS = W, H + 10
P1_PITCH, P1_ROWS = W + 10, H + 2
P1_BASE = P0_PITCH * P0_ROWS
IMG2 = P1_BASE + P1_PITCH * P1_ROWS + 28
L3_TAPS0 = [(dy, 0) for dy in range(-5, 6)]
L3_TAPS1 = [(0, dx) for dx in range(-5, 6)] + [(dy, dx) for dy in (-1, 1) for dx in (-1, 0, 1)]
L3_TAPS = len(L3_TAPS0) + len(L3_TAPS1)
START = 2

VECS = [("bn1_g", 2), ("bn1_b", 2), ("bn1_m", 2), ("bn1_v", 2),
        ("dwbn_g", 2), ("dwbn_b", 2), ("dwbn_m", 2), ("dwbn_v", 2), ("dw_b", 2),
        ("bn2_g", 2), ("bn2_b", 2), ("bn2_m", 2), ("bn2_v", 2),
        ("outproj_b", 2), ("fc1_b", 8), ("fc2_b", 2), ("se_down_b", 1), ("se_up_b", 2),
        ("ap_b1", 1), ("ap_b2", 2), ("meta_b1", 1), ("meta_b2", 2),
        ("b_out", 2), ("gamma", 2), ("beta", 2), ("l3_b", 2), ("l3_s", 2),
        ("inproj_row", 256), ("om_row", 3 * PTS), ("ident", P), ("gavg", P),
        ("gx_base", PTS), ("gy_base", TILES * K2), ("g_base", G)]
COL, _at = {}, 0
for _name, _width in VECS:
    COL[_name] = (_at, _width)
    _at += _width
NPAR = _at

A_CONV, A_INP, A_OM, A_DW = 0, 512, 1024, 1024 + 2 * 3 * PTS
A_SIZE = A_DW + KC * K2 * P
F_OUT, F_FC1, F_FC2 = 0, 512, 512 + KC * 4 * C
F_DOWN = F_FC2 + FC * C
F_UP = F_DOWN + KC * 64
F_SIZE = F_UP + C
R_BASE = 0
R_AP1 = KC * K2 * CG
R_ME1 = R_AP1 + KC * 64
R_AP2 = R_ME1 + KC * 64
R_ME2 = R_AP2 + C
R_SIZE = R_ME2 + C
Q_Q, Q_K, Q_V, Q_O = 0, KC * HID, 2 * KC * HID, 3 * KC * HID
Q_SIZE = Q_O + KH * C
WA_SIZE = R_SIZE + KC * K2 * P
WB_SIZE = Q_SIZE + 3 * 1024 + 512


class Own:

    def __init__(self, eng, sem):
        self.eng, self.sem, self.n, self.at, self.k = eng, sem, 0, 0, 0

    def enter(self, it, per):
        self.at, self.per, self.k = it * per, per, 0

    def leave(self, times):
        assert self.k == self.per, (self.k, self.per)
        self.n += self.per * times
        self.at, self.k = 0, 0

    def link(self, ins):
        self.k += 1
        ins.then_inc(self.sem, 1)
        self.eng.wait_ge(self.sem, self.at + (self.n + self.k))

    def settle(self):
        self.n, self.k = self.n + self.k, 0


def network_kernel(nc, x, par, wa, wr, wf, wq, w3, out):
    ctx = ExitStack()
    with ctx:
        def sb(name, shape, dt=F32):
            return ctx.enter_context(nc.sbuf_tensor(name, shape, dt))

        def dram(name, shape):
            return nc.dram_tensor(name, shape, F32, kind="Internal").ap()

        sems = {}

        def sem(name):
            if name not in sems:
                sems[name] = ctx.enter_context(nc.semaphore(name))
            return sems[name]

        y_dram = dram("y_dram", [B, P, KC, HW])
        tab = [dram(f"table{b}", [G * TAB_ROWS, CORNERS * GC]) for b in range(B)]
        w_dram = dram("w_dram", [B, P, TILES * PTS * CORNERS])
        idx_dram = nc.dram_tensor("idx_dram", [B, P, TILES * PTS], U32, kind="Internal").ap()
        d_dram = dram("d_dram", [B, TILES, P, C])
        q_dram = dram("q_dram", [B, P, CHUNKS, KH, CHUNK])
        o_dram = dram("o_dram", [B, P, KC, HW])
        x2_dram = dram("x2_dram", [B, P, KC, HW])

        params = sb("params", [P, NPAR])
        wa_sb = sb("wa_sb", [P, WA_SIZE])
        wb_sb = sb("wb_sb", [P, WB_SIZE])
        ring = sb("ring", [P, G, K2 * CORNERS * GC])
        idx = sb("idx", [P, TILES * PTS], U32)
        idx_stage = sb("idx_stage", [P, 2, PTS], U32)
        wt = sb("wt", [P, TILES * PTS * CORNERS])
        dbuf = sb("dbuf", [P, 4, C])
        img1 = sb("img1", [P, KC * HW])
        img2 = sb("img2", [P, IMG2])
        cb = sb("cb", [P, 4 * 1024])
        stats = sb("stats", [P, KC * CHUNKS * 6])
        ostats = sb("ostats", [P, KC * B * CHUNKS * 6])
        sm = sb("sm", [P, 420])
        PS = ctx.enter_context(nc.psum_tensor("PS", [P, 8, 512], F32))

        def v(name, k=None, rows=P):
            a, w = COL[name]
            return params[0:rows, a:a + w] if k is None else params[0:rows, a + k:a + k + 1]

        used = [0]

        def small(n):
            a = used[0]
            used[0] += n
            return sm[:, a:a + n]

        mv, ms, gm = small(4), small(4), small(4)
        gvar, gsd, gn_s, gn_t, gsq = small(2), small(2), small(2), small(2), small(4)
        eps_c, zero_c, one_c, nhalf = small(1), small(1), small(1), small(1)
        bnv, bninv, bnsh = small(6), small(6), small(6)
        cb1 = small(2)
        rsum, xmean, s_hid, s_z, s_e, s_g, s_ga, s_gc = (small(2) for _ in range(8))
        fb = small(8)
        a_hid, m_hid, ang, sin_c, cos_c, mod = small(1), small(1), small(2), small(2), small(2), small(2)
        mz = small(2)
        U, V_ = small(18), small(18)
        BX, AY = small(54), small(54)
        kmax, cmax, knew, kneg, kdif, kalpha, ksum, esum = (small(KH) for _ in range(8))
        qmax, qsum = small(32), small(32)
        pooled = small(2)
        o_mv, o_sc, o_sh, o_sd, o_rs = small(4), small(2), small(2), small(2), small(1)
        assert used[0] <= 420, used[0]

        coef = cb[:, 0:KC * K2 * K2]

        ych = [cb[:, h * 1024:(h + 1) * 1024] for h in range(2)]
        xpt = [cb[:, (2 + h) * 1024:(3 + h) * 1024] for h in range(2)]
        i2 = [img2[:, j * 1024:(j + 1) * 1024] for j in range(9)]

        def seg(t, start, n):
            return t[:, bass.ds(start, n)]

        def chunk_of(t, k, c):
            return seg(t, c * CHUNK + k * HW, CHUNK)

        def padded(k, c, dy, dx):
            return seg(img2, c * (ROWS * YPITCH) + (k * YPLANE + dy * YPITCH + dx), ROWS * YPITCH)\
                .rearrange("p (r x) -> p r x", x=YPITCH)[:, :, 0:W]

        def padded3(k, c, dy, dx):
            pitch, base = ((P0_PITCH, 0), (P1_PITCH, P1_BASE))[k]
            return seg(img2, c * (ROWS * pitch) + (base + dy * pitch + dx), ROWS * pitch)\
                .rearrange("p (r x) -> p r x", x=pitch)[:, :, 0:W]

        def rows(ap):
            return ap.rearrange("p (r x) -> p r x", x=W)

        def wseg(region, a, n):
            return region[:, a:a + n]

        x_img = x.rearrange("b (k p) h w -> b p k (h w)", p=P)
        out_img = out.rearrange("b (k p) h w -> b p k (h w)", p=P)

        def done(eng, name, n):
            eng.wait_ge(sem(name), n + (START + 1))

        def room(eng, name, n):
            eng.wait_ge(sem(name), n + 1)

        two_deep = ["aZ", "aY", "aC", "aP", "aX", "aXE", "dZ", "dT", "dD", "dO", "dE",
                    "fT", "fC", "fO", "fR", "gH", "gZ", "gB", "gD", "gX", "lC", "lX",
                    "cKs", "bP", "bO", "bS", "eC", "eX"]
        store_sems = [f"{name}{h}" for name in ("y_stored", "t_stored", "o_stored", "out_stored") for h in range(2)] \
            + ["d_stored", "q_stored"]
        block = ctx.enter_context(nc.Block())
        ENG = ("sp", "pe", "act", "dve")

        class Barrier:

            def __init__(self, eng, me):
                self.eng, self.me, self.n = eng, me, 0

            def __call__(self):
                self.n += 1
                if self.me == "sp":
                    self.eng.sem_inc(sem("sp_phase"), 1)
                else:
                    self.eng.drain().then_inc(sem(self.me + "_phase"), 1)
                for e in ENG:
                    if e != self.me:
                        self.eng.wait_ge(sem(e + "_phase"), self.n)

        plan = [("A", 0, None)] + [("A", b, 0) for b in range(1, B)] + [("REST", None, 0)]
        for k in range(1, B):
            plan += [("F", k - 1, k), ("L1", k - 1, k), ("L2", k - 1, k), ("REST", None, k)]
        plan += [("F", B - 1, None), ("L1", B - 1, None), ("L2", B - 1, None), ("L3", None, None)]
        TURNS = {"A1": 1, "A2": 1, "F1": 1, "F2": 2, "L1": 1, "L2a": 3, "L2b": 1}

        class Stream:

            def __init__(self, unit, turned=None):
                self.unit, self.turned, self.taken, self.left = unit, turned, {}, []

            def begin(self, part, gi, i):
                self.left = []
                if gi is not None:
                    n = TURNS[part]
                    self.left = [(gi, i * n + (self.taken.get(gi, 0) + j), g, j) for j in range(n) for g in range(G)]
                self.share = len(self.left)

            def give(self, part_of=1, whole=1):
                for _ in range(min(len(self.left), -(-self.share * part_of // whole))):
                    self.unit(*self.left.pop(0))

            def finish(self):
                while self.left:
                    self.unit(*self.left.pop(0))

            def ended(self, part, gi):
                if gi is not None:
                    self.taken[gi] = self.taken.get(gi, 0) + TURNS[part] * PAIRS

            def rest(self, eng, gi, after=None):
                first = self.taken.get(gi, 0)
                if first < TILES:
                    with eng.Fori(0, TILES - first) as i:
                        for g in range(G):
                            self.unit(gi, i + first, g, 0)
                        if after:
                            after(gi, i + first, 1)
                self.taken[gi] = TILES

        @block.gpsimd
        def _(pool):
            def unit(b, t, g, stage):
                pool.wait_ge(sem("ring_free"), t * G + (b * TILES * G + g + 1))
                if g == 0:
                    pool.wait_ge(sem("idx_staged"), t + (b * TILES + 1))
                pool.sem_inc(sem("unit_begun"), 1)
                for p in range(K2):
                    nc.gpsimd.indirect_dma_start(
                        out=ring[:, g, p * CORNERS * GC:(p + 1) * CORNERS * GC], out_offset=None,
                        in_=tab[b], in_offset=bass.IndirectOffsetOnAxis(
                            ap=idx_stage[:, stage, g * K2 + p:g * K2 + p + 1], axis=0),
                    ).then_inc(sem(f"gathered{g}"), 16)

            def pair(b, i, last):
                for h in range(2):
                    t = i * 2 + h
                    for g in range(G):
                        if g == G - 1 and not (last and h == 1):
                            pool.wait_ge(sem("ring_free"), t * G + (b * TILES * G + g + 1))
                            nc.gpsimd.tensor_copy(idx_stage[:, 1 - h, :], seg(idx, t * PTS + PTS, PTS))\
                                .then_inc(sem("idx_staged"), 1)
                        unit(b, t, g, h)

            for b in range(B):
                pool.wait_ge(sem("idx_loaded"), 16 * (b + 1))
                nc.gpsimd.tensor_copy(idx_stage[:, 0, :], idx[:, 0:PTS]).then_inc(sem("idx_staged"), 1)
                with pool.Fori(0, TILES // 2 - 1) as i:
                    pair(b, i, False)
                pair(b, TILES // 2 - 1, True)

        @block.sync
        def _(sp):
            for name in two_deep:
                sp.sem_inc(sem(name), START)
            for name in ("cQC", "cET", "cXT", "cS", "cQT"):
                sp.sem_inc(sem(name), 1)
            sp.sem_inc(sem("ring_free"), G)
            barrier = Barrier(sp, "sp")
            loads = {"wa": 0, "wb": 0}

            def store_sums(b, first, n):
                for j in range(n):
                    t = first + j
                    sp.wait_ge(sem("ring_free"), t * G + ((b * TILES + 1) * G + G))
                    sp.dma_start(d_dram[b][bass.ds(t, 1)].rearrange("a p c -> (a p) c"), dbuf[:, j, :])\
                        .then_inc(sem("d_stored"), 16)

            stream = Stream(lambda *u: None)

            def begin_gathers(b):
                sp.dma_start(idx[:], idx_dram[b]).then_inc(sem("idx_loaded"), 16)
                sp.dma_start(wt[:], w_dram[b]).then_inc(sem("wt_loaded"), 16)

            def load_pack(region, tile_, pack):
                loads[region] += 1
                sp.dma_start(tile_[:, 0:pack.shape[1]], pack).then_inc(sem(region + "_loaded"), 16)

            def chunks(part, gi, body):
                with sp.Fori(0, PAIRS) as i:
                    body(i)
                    if gi is not None:
                        store_sums(gi, i * TURNS[part] + stream.taken.get(gi, 0), TURNS[part])
                stream.ended(part, gi)

            def A(b, gi):
                if b == 0:
                    sp.dma_start(params[:], par).then_inc(sem("par_loaded"), 16)
                load_pack("wa", wa_sb, wa)
                for k in range(KC):
                    sp.dma_start(img1[:, k * HW:(k + 1) * HW], x_img[b][:, k, :]).then_inc(sem("x_loaded"), 16)
                if b == B - 1:
                    load_pack("wb", wb_sb, wf)
                if b == 0:
                    sp.wait_ge(sem("zeros"), 1)
                    pieces = [(t, first) for t in tab for first in (0, P // 2, HW, HW + P // 2)]
                    for (t, first), name in zip(pieces, store_sems + ["pads_stored"] * (len(pieces) - len(store_sems))):
                        sp.dma_start(t.rearrange("(g r) c -> r g c", g=G)[first:first + P // 2],
                                     dbuf[0:P // 2, 0, :].unsqueeze(1).to_broadcast([P // 2, G, C])).then_inc(sem(name), 16)
                    for name in store_sems:
                        sp.wait_ge(sem(name), 16)
                    sp.wait_ge(sem("pads_stored"), 16 * (len(pieces) - len(store_sems)))
                barrier()
                table = tab[b].rearrange("(g r) c -> r g c", g=G)

                def body(i):
                    for h in range(2):
                        n, c = i * 2 + (b * CHUNKS + h), i * 2 + h
                        done(sp, "aY", n)
                        for k in range(KC):
                            sp.dma_start(y_dram[b][:, k, bass.ds(c * CHUNK, CHUNK)], ych[h][:, k * CHUNK:(k + 1) * CHUNK])\
                                .then_inc(sem(f"y_stored{h}"), 16)
                    for h in range(2):
                        n, c = i * 2 + (b * CHUNKS + h), i * 2 + h
                        done(sp, "aXE", n)
                        src = xpt[h].rearrange("p (s g c) -> p s g c", s=SUBS, g=G)
                        for s in range(SUBS):
                            for j, back in enumerate((0, 1, W, W + 1)):
                                first = c * CHUNK + (TAB_FRONT - back + s * P)
                                sp.dma_start(table[bass.ds(first, P), :, j * GC:(j + 1) * GC], src[:, s])\
                                    .then_inc(sem(f"t_stored{h}"), 16)
                chunks("A1", gi, body)
                for h in range(2):
                    sp.wait_ge(sem(f"y_stored{h}"), 16 * KC * PAIRS * (b + 1) + 16)
                    sp.wait_ge(sem(f"t_stored{h}"), 16 * 16 * PAIRS * (b + 1) + 16)
                barrier()
                chunks("A2", gi, lambda i: None)
                barrier()
                sp.wait_ge(sem("idx_made"), b + 1)
                sp.wait_ge(sem("w_made"), b + 1)
                sp.dma_start(w_dram[b], img2[:, 0:TILES * PTS * CORNERS]).then_inc(sem("w_stored"), 16)
                sp.dma_start(idx_dram[b], img1[:, 0:TILES * PTS].bitcast(U32)).then_inc(sem("w_stored"), 16)
                sp.wait_ge(sem("w_stored"), 32 * (b + 1))
                if b == 0:
                    begin_gathers(0)
                barrier()

            def F(b, gi):
                load_pack("wa", wa_sb, wr)

                def f1(i):
                    for h in range(2):
                        n, c = i * 2 + (b * CHUNKS + h), i * 2 + h
                        room(sp, "fT", n)
                        sp.dma_start(i2[h].rearrange("p (s c) -> p s c", s=SUBS),
                                     d_dram[b][bass.ds(c * SUBS, SUBS)].rearrange("s p c -> p s c"))\
                            .then_inc(sem(f"fD{h}"), 16)
                        room(sp, "fR", n)
                        sp.dma_start(i2[2 + h].rearrange("p (k n) -> p k n", k=KC), y_dram[b][:, :, bass.ds(c * CHUNK, CHUNK)])\
                            .then_inc(sem(f"fY{h}"), 16)
                chunks("F1", gi, f1)
                barrier()
                barrier()

                def f2(i):
                    for h in range(2):
                        n, c = i * 2 + (b * CHUNKS + h), i * 2 + h
                        room(sp, "gX", n)
                        sp.dma_start(i2[h].rearrange("p (k n) -> p k n", k=KC), y_dram[b][:, :, bass.ds(c * CHUNK, CHUNK)])\
                            .then_inc(sem(f"gYl{h}"), 16)
                        sp.dma_start(i2[2 + h].rearrange("p (k n) -> p k n", k=KC), x_img[b][:, :, bass.ds(c * CHUNK, CHUNK)])\
                            .then_inc(sem(f"gXl{h}"), 16)
                chunks("F2", gi, f2)
                barrier()

            def L1(b, gi):
                load_pack("wb", wb_sb, wq)
                barrier()
                chunks("L1", gi, lambda i: None)
                barrier()

            def L2(b, gi):
                barrier()
                sp.dma_start(x2_dram[b].rearrange("p k n -> p (k n)"), img1[:]).then_inc(sem("x2_stored"), 16)

                def a(i):
                    for h in range(2):
                        n, c = i * 2 + (b * CHUNKS + h), i * 2 + h
                        sp.wait_ge(sem("cQC"), n + 2)
                        sp.dma_start(q_dram[b][:, bass.ds(c, 1)].rearrange("p a m n -> p (a m n)"), img2[:, 6144:8192])\
                            .then_inc(sem("q_stored"), 16)
                chunks("L2a", gi, a)
                sp.wait_ge(sem("q_stored"), 16 * CHUNKS * (b + 1) + 16)
                barrier()
                barrier()

                def o(i):
                    for h in range(2):
                        n, c = i * 2 + (b * CHUNKS + h), i * 2 + h
                        room(sp, "bP", n)
                        sp.dma_start(img2[:, h * 2048:(h + 1) * 2048], q_dram[b][:, bass.ds(c, 1)].rearrange("p a m n -> p (a m n)"))\
                            .then_inc(sem(f"q_loaded{h}"), 16)
                    for h in range(2):
                        n, c = i * 2 + (b * CHUNKS + h), i * 2 + h
                        done(sp, "bO", n)
                        sp.dma_start(o_dram[b][:, :, bass.ds(c * CHUNK, CHUNK)], i2[4 + h].rearrange("p (k n) -> p k n", k=KC))\
                            .then_inc(sem(f"o_stored{h}"), 16)
                chunks("L2b", gi, o)
                for h in range(2):
                    sp.wait_ge(sem(f"o_stored{h}"), 16 * PAIRS * (b + 1) + 16)
                sp.wait_ge(sem("x2_stored"), 16 * (b + 1))
                barrier()

            def L3():
                load_pack("wb", wb_sb, w3)
                rf = ring[:].rearrange("p g c -> p (g c)")
                barrier()
                for b in range(B):
                    sp.dma_start(img1[:], x2_dram[b].rearrange("p k n -> p (k n)")).then_inc(sem("e_loaded"), 16)
                    sp.dma_start(rf[:, 0:KC * HW], o_dram[b].rearrange("p k n -> p (k n)")).then_inc(sem("e_loaded"), 16)
                    barrier()
                    with sp.Fori(0, PAIRS) as i:
                        for h in range(2):
                            n, c = i * 2 + (b * CHUNKS + h), i * 2 + h
                            done(sp, "eX", n)
                            sp.dma_start(out_img[b][:, :, bass.ds(c * CHUNK, CHUNK)], ych[h].rearrange("p (k n) -> p k n", k=KC))\
                                .then_inc(sem(f"out_stored{h}"), 16)
                    for h in range(2):
                        sp.wait_ge(sem(f"out_stored{h}"), 16 * PAIRS * (b + 1) + 16)
                    barrier()

            for phase, b, gi in plan:
                if phase == "REST":
                    if gi:
                        load_pack("wb", wb_sb, wf)
                    stream.rest(sp, gi, store_sums)
                    sp.wait_ge(sem("d_stored"), 16 * TILES * (gi + 1) + 16)
                    if gi + 1 < B:
                        begin_gathers(gi + 1)
                    barrier()
                elif phase == "L3":
                    L3()
                else:
                    {"A": A, "F": F, "L1": L1, "L2": L2}[phase](b, gi)

        @block.tensor
        def _(pe):
            barrier = Barrier(pe, "pe")
            count = {"wa": 0, "wb": 0, "gn": 0}

            def mm(o, l, r, start, stop, **kw):
                return nc.tensor.matmul(o, l, r, start=start, stop=stop, **kw)

            def loaded(region):
                count[region] += 1
                pe.wait_ge(sem(region + "_loaded"), 16 * count[region])

            def group_average():
                count["gn"] += 1
                pe.wait_ge(sem("gn_moments"), count["gn"])
                mm(PS[:, 7, 0:4], v("gavg"), ms, True, True).then_inc(sem("gn_grouped"), 1)

            def loop(body):
                with pe.Fori(0, PAIRS) as i:
                    body(i)

            def A(b):
                loaded("wa")
                conv = wseg(wa_sb, A_CONV, 512)
                inp, om = wseg(wa_sb, A_INP, 512), wseg(wa_sb, A_OM, 6 * PTS)
                if b == 0:
                    pe.wait_ge(sem("par_loaded"), 16)
                group_average()
                pe.wait_ge(sem("gn_ready"), count["gn"])
                for oc in range(KC):
                    for k in range(KC):
                        last = mm(PS[:, 6, oc:oc + 1], conv[:, k * C + oc * P:k * C + (oc + 1) * P], gn_t[:, k:k + 1],
                                  k == 0, k == KC - 1)
                last.then_inc(sem("a_bias"), 1)
                barrier()

                def a1(i):
                    for h in range(2):
                        n, c = i * 2 + (b * CHUNKS + h), i * 2 + h
                        room(pe, "aZ", n)
                        for oc in range(KC):
                            for k in range(KC):
                                last = mm(PS[:, 2 * h + oc, :], conv[:, k * C + oc * P:k * C + (oc + 1) * P],
                                          chunk_of(img1, k, c), k == 0, k == KC - 1)
                        last.then_inc(sem("aC"), 1)
                    for h in range(2):
                        n = i * 2 + (b * CHUNKS + h)
                        done(pe, "aY", n)
                        room(pe, "aXE", n)
                        for s in range(SUBS):
                            for k in range(KC):
                                last = mm(PS[:, 4 + 2 * h + s // 2, (s % 2) * C:(s % 2 + 1) * C],
                                          ych[h][:, k * CHUNK + s * P:k * CHUNK + (s + 1) * P], inp[:, k * C:(k + 1) * C],
                                          k == 0, k == KC - 1)
                        last.then_inc(sem("aX"), 1)
                loop(a1)
                barrier()

                def a2(i):
                    for h in range(2):
                        n, c = i * 2 + (b * CHUNKS + h), i * 2 + h
                        room(pe, "dZ", n)
                        for k in range(KC):
                            for tap in range(K2):
                                at = A_DW + (k * K2 + tap) * P
                                last = mm(PS[:, 2 * h + k, :].rearrange("p (r x) -> p r x", x=W), wseg(wa_sb, at, P),
                                          padded(k, c, tap // 3, tap % 3), tap == 0, tap == K2 - 1)
                        last.then_inc(sem("dD"), 1)
                    for h in range(2):
                        n = i * 2 + (b * CHUNKS + h)
                        done(pe, "dT", n)
                        room(pe, "dE", n)
                        for s in range(SUBS):
                            for k in range(KC):
                                last = mm(PS[:, 4 + h, s * 3 * PTS:(s + 1) * 3 * PTS],
                                          ych[h][:, k * CHUNK + s * P:k * CHUNK + (s + 1) * P],
                                          om[:, k * 3 * PTS:(k + 1) * 3 * PTS], k == 0, k == KC - 1)
                        last.then_inc(sem("dO"), 1)
                loop(a2)
                barrier()
                barrier()

            def F(b):
                loaded("wb")
                outp, fc1, fc2 = wseg(wb_sb, F_OUT, 512), wseg(wb_sb, F_FC1, KC * 4 * C), wseg(wb_sb, F_FC2, FC * C)

                def f1(i):
                    for h in range(2):
                        n, m = i * 2 + (b * CHUNKS + h), i + b * PAIRS
                        pe.wait_ge(sem(f"fD{h}"), m * 16 + 16)
                        room(pe, "fC", n)
                        for k in range(KC):
                            for s in range(SUBS):
                                last = nc.tensor.transpose(PS[:, 2 * h + k, s * P:(s + 1) * P],
                                                           i2[h][:, s * C + k * P:s * C + (k + 1) * P], v("ident"))
                        last.then_inc(sem("fT"), 1)
                    for h in range(2):
                        n = i * 2 + (b * CHUNKS + h)
                        done(pe, "fC", n)
                        room(pe, "fR", n)
                        for oc in range(KC):
                            for k in range(KC):
                                last = mm(PS[:, 4 + 2 * h + oc, :], outp[:, k * C + oc * P:k * C + (oc + 1) * P],
                                          i2[4 + h][:, k * CHUNK:(k + 1) * CHUNK], k == 0, k == KC - 1)
                        last.then_inc(sem("fO"), 1)
                loop(f1)
                barrier()
                pe.wait_ge(sem("se_mean"), b + 1)
                for k in range(KC):
                    last = mm(PS[0:64, 7, 0:1], wseg(wb_sb, F_DOWN, KC * 64)[:, k * 64:(k + 1) * 64], xmean[:, k:k + 1],
                              k == 0, k == KC - 1)
                last.then_inc(sem("se_down"), 1)
                pe.wait_ge(sem("se_hidden"), b + 1)
                for oc in range(KC):
                    last = mm(PS[:, 6, oc:oc + 1], wb_sb[0:64, F_UP + oc * P:F_UP + (oc + 1) * P], s_hid[0:64, 0:1], True, True)
                last.then_inc(sem("se_up"), 1)
                pe.wait_ge(sem("se_gate"), b + 1)
                for hc in range(FC):
                    for k in range(KC):
                        last = mm(PS[:, 5, hc:hc + 1], fc1[:, k * 4 * C + hc * P:k * 4 * C + (hc + 1) * P], s_gc[:, k:k + 1],
                                  k == 0, k == KC - 1)
                last.then_inc(sem("fc1_shift"), 1)
                barrier()

                def f2(i):
                    for h in range(2):
                        n, c = i * 2 + (b * CHUNKS + h), i * 2 + h

                        def up(q):
                            room(pe, "gZ", n * 4 + q)
                            for j in range(2):
                                for k in range(KC):
                                    at = k * 4 * C + (2 * q + j) * P
                                    last = mm(PS[:, 2 * (q % 2) + j, :], fc1[:, at:at + P], chunk_of(img1, k, c),
                                              k == 0, k == KC - 1)
                            last.then_inc(sem("gH"), 1)

                        def down(q):
                            done(pe, "gB", n * 4 + q)
                            if q == 0:
                                room(pe, "gX", n)
                            hb = i2[6 + q % 2]
                            for j in range(2):
                                for oc in range(KC):
                                    at = (2 * q + j) * C + oc * P
                                    last = mm(PS[:, 4 + 2 * h + oc, :], fc2[:, at:at + P], hb[:, j * CHUNK:(j + 1) * CHUNK],
                                              q == 0 and j == 0, q == 3 and j == 1)
                            last.then_inc(sem("gD"), 1)

                        up(0)
                        up(1)
                        down(0)
                        up(2)
                        down(1)
                        up(3)
                        down(2)
                        down(3)
                loop(f2)
                barrier()

            def L1(b):
                loaded("wa")
                group_average()
                pe.wait_ge(sem("pooled"), b + 1)
                for j, at in enumerate((R_AP1, R_ME1)):
                    for k in range(KC):
                        last = mm(PS[0:64, 6, j:j + 1], wa_sb[:, at + k * 64:at + (k + 1) * 64], pooled[:, k:k + 1],
                                  k == 0, k == KC - 1)
                last.then_inc(sem("l1_hidden"), 1)
                pe.wait_ge(sem("l1_relu"), b + 1)
                for j, (at, hid) in enumerate(((R_AP2, a_hid), (R_ME2, m_hid))):
                    for oc in range(KC):
                        last = mm(PS[:, 5, 2 * j + oc:2 * j + oc + 1], wa_sb[0:64, at + oc * P:at + (oc + 1) * P], hid[0:64, :],
                                  True, True)
                last.then_inc(sem("l1_heads"), 1)
                barrier()

                def l1(i):
                    for h in range(2):
                        n, c = i * 2 + (b * CHUNKS + h), i * 2 + h
                        room(pe, "lX", n)
                        for k in range(KC):
                            for tap in range(K2):
                                at = R_SIZE + (k * K2 + tap) * P
                                last = mm(PS[:, 2 * h + k, :].rearrange("p (r x) -> p r x", x=W), wseg(wa_sb, at, P),
                                          padded(k, c, tap // 3, tap % 3), tap == 0, tap == K2 - 1)
                        last.then_inc(sem("lC"), 1)
                loop(l1)
                barrier()

            def L2(b):
                loaded("wb")
                group_average()
                barrier()
                wq_, wk_ = wseg(wb_sb, Q_Q, KC * HID), wseg(wb_sb, Q_K, KC * HID)
                wv_, wo_ = wseg(wb_sb, Q_V, KC * HID), wseg(wb_sb, Q_O, KH * C)
                kx = wseg(wb_sb, Q_SIZE, 1024)
                kxt, bd, mt = wseg(wb_sb, Q_SIZE + 1024, 1024), wseg(wb_sb, Q_SIZE + 3072, 512), wseg(wb_sb, Q_SIZE + 2048, 1024)
                E_, QS = img2[:, 2048:4096], img2[:, 4096:6144]

                def la(i):
                    for h in range(2):
                        n = i * 2 + (b * CHUNKS + h)
                        xn = i2[h]
                        pe.wait_ge(sem("cXN"), n + 1)
                        pe.wait_ge(sem("cQC"), n + 1)
                        for m in range(KH):
                            for k in range(KC):
                                last = mm(PS[:, m, :], wk_[:, k * HID + m * P:k * HID + (m + 1) * P],
                                          xn[:, k * CHUNK:(k + 1) * CHUNK], k == 0, k == KC - 1)
                        last.then_inc(sem("cK"), 1)
                        pe.wait_ge(sem("cE"), n + 1)
                        for s in range(SUBS):
                            for k in range(KC):
                                last = mm(PS[:, s, :], xn[:, k * CHUNK + s * P:k * CHUNK + (s + 1) * P],
                                          wq_[:, k * HID:(k + 1) * HID], k == 0, k == KC - 1)
                        last.then_inc(sem("cQ"), 1)

                        def turn_(s):
                            pe.wait_ge(sem("cET"), n * 4 + (s + 1))
                            for m in range(KH):
                                nc.tensor.transpose(PS[:, 6, m * P:(m + 1) * P],
                                                    E_[:, m * CHUNK + s * P:m * CHUNK + (s + 1) * P], v("ident"))
                            pe.wait_ge(sem("cXT"), n * 4 + (s + 1))
                            for k in range(KC):
                                last = nc.tensor.transpose(PS[:, 7, k * P:(k + 1) * P],
                                                           xn[:, k * CHUNK + s * P:k * CHUNK + (s + 1) * P], v("ident"))
                            last.then_inc(sem("cTT"), 1)

                        def product(s):
                            pe.wait_ge(sem("cET"), n * 4 + (s + 2))
                            pe.wait_ge(sem("cXT"), n * 4 + (s + 2))
                            if s == 0:
                                pe.wait_ge(sem("cS"), n + 1)
                            et, xt = i2[8][:, (s % 2) * 512:(s % 2 + 1) * 512], cb[:, (s % 2) * C:(s % 2 + 1) * C]
                            for m in range(KH):
                                last = mm(PS[:, 4 + m // 2, (m % 2) * C:(m % 2 + 1) * C], et[:, m * P:(m + 1) * P], xt,
                                          s == 0 and m % 2 == 0, s == SUBS - 1, skip_group_check=True)
                            last.then_inc(sem("cKs"), 1)

                        turn_(0)
                        for s in range(SUBS):
                            if s + 1 < SUBS:
                                turn_(s + 1)
                            product(s)
                        pe.wait_ge(sem("cQn"), n + 1)
                        for m in range(KH):
                            for s in range(SUBS):
                                last = nc.tensor.transpose(PS[:, m, s * P:(s + 1) * P],
                                                           QS[:, s * HID + m * P:s * HID + (m + 1) * P], v("ident"))
                        last.then_inc(sem("cQT"), 1)
                loop(la)
                barrier()
                pe.wait_ge(sem("kx_scaled"), b + 1)
                for k in range(KC):
                    for m in range(KH):
                        last = nc.tensor.transpose(PS[:, k, m * P:(m + 1) * P], kx[:, m * C + k * P:m * C + (k + 1) * P],
                                                   v("ident"))
                last.then_inc(sem("kx_turned"), 1)
                pe.wait_ge(sem("kxt_ready"), b + 1)
                for m in range(KH):
                    for k in range(KC):
                        last = mm(PS[:, 2, m * P:(m + 1) * P], wv_[:, k * HID + m * P:k * HID + (m + 1) * P],
                                  kxt[:, k * HID + m * P:k * HID + (m + 1) * P], k == 0, k == KC - 1)
                last.then_inc(sem("ctx_ready"), 1)
                pe.wait_ge(sem("ctx_diagonal"), b + 1)
                for m in range(KH):
                    last = mm(PS[:, 3 + m // 2, (m % 2) * C:(m % 2 + 1) * C], bd[:, m * P:(m + 1) * P],
                              wo_[:, m * C:(m + 1) * C], True, True)
                last.then_inc(sem("mt_ready"), 1)
                barrier()

                def lb(i):
                    for h in range(2):
                        n, m_ = i * 2 + (b * CHUNKS + h), i + b * PAIRS
                        pe.wait_ge(sem(f"q_loaded{h}"), m_ * 16 + 16)
                        room(pe, "bO", n)
                        for oc in range(KC):
                            for m in range(KH):
                                last = mm(PS[:, 2 * h + oc, :], mt[:, m * C + oc * P:m * C + (oc + 1) * P],
                                          img2[:, h * 2048 + m * CHUNK:h * 2048 + (m + 1) * CHUNK], m == 0, m == KH - 1)
                        last.then_inc(sem("bP"), 1)
                loop(lb)
                barrier()

            def L3():
                loaded("wb")
                barrier()
                for b in range(B):
                    group_average()
                    barrier()

                    def conv(i):
                        for h in range(2):
                            n, c = i * 2 + (b * CHUNKS + h), i * 2 + h
                            room(pe, "eX", n)
                            at = 0
                            for k, taps in enumerate((L3_TAPS0, L3_TAPS1)):
                                for j, (dy, dx) in enumerate(taps):
                                    src = padded3(k, c, dy + (5, 1)[k], dx + (0, 5)[k])
                                    last = mm(PS[:, 2 * h + k, :].rearrange("p (r x) -> p r x", x=W), wseg(wb_sb, at * P, P),
                                              src, j == 0, j == len(taps) - 1)
                                    at += 1
                            last.then_inc(sem("eC"), 1)
                    loop(conv)
                    barrier()

            for phase, b, gi in plan:
                if phase == "REST":
                    barrier()
                elif phase == "L3":
                    L3()
                else:
                    {"A": A, "F": F, "L1": L1, "L2": L2}[phase](b)

        @block.scalar
        def _(act):
            barrier = Barrier(act, "act")
            count = {"gn": 0}

            def A_(o, i, f, **kw):
                return nc.scalar.activation(o, i, f, **kw)

            def loop(func, body):
                nc.scalar.preload_act_table(func)
                with act.Fori(0, PAIRS) as i:
                    body(i)

            def deviation():
                count["gn"] += 1
                act.wait_ge(sem("gn_var"), count["gn"])
                A_(gsd, gvar, ACT.Sqrt, bias=eps_c).then_inc(sem("gn_sd"), 1)

            def A(b):
                if b == 0:
                    act.wait_ge(sem("bn_var"), 1)
                    A_(bnv, bnv, ACT.Sqrt, bias=eps_c).then_inc(sem("bn_sd"), 1)
                deviation()
                barrier()

                def a1(i):
                    for h in range(2):
                        n = i * 2 + (b * CHUNKS + h)
                        m = i + b * PAIRS
                        done(act, "aC", n)
                        room(act, "aX", n)
                        room(act, "aP", n)
                        act.wait_ge(sem(f"y_stored{h}"), m * (16 * KC) + 16)
                        for oc in range(KC):
                            last = A_(ych[h][:, oc * CHUNK:(oc + 1) * CHUNK], PS[:, 2 * h + oc, :], ACT.Identity,
                                      bias=cb1[:, oc:oc + 1], scale=bninv[:, oc:oc + 1])
                        last.then_inc(sem("aZ"), 1)
                    for h in range(2):
                        n, c = i * 2 + (b * CHUNKS + h), i * 2 + h
                        done(act, "aY", n)
                        for k in range(KC):
                            last = A_(padded(k, c, 1, 1), rows(ych[h][:, k * CHUNK:(k + 1) * CHUNK]), ACT.Copy)
                        last.then_inc(sem("aP"), 1)
                loop(ACT.Identity, a1)
                barrier()

                def a2(i):
                    for h in range(2):
                        n = i * 2 + (b * CHUNKS + h)
                        done(act, "dD", n)
                        room(act, "dO", n)
                        for oc in range(KC):
                            last = A_(ych[h][:, oc * CHUNK:(oc + 1) * CHUNK], PS[:, 2 * h + oc, :], ACT.Identity,
                                      bias=bnsh[:, 2 + oc:3 + oc], scale=bninv[:, 2 + oc:3 + oc])
                        last.then_inc(sem("dZ"), 1)
                loop(ACT.Identity, a2)
                barrier()
                T = lambda j: img1[:, 3456 + j * 1152:3456 + (j + 1) * 1152] if j < 4 else \
                    img2[:, 4608 + (j - 4) * 1152:4608 + (j - 3) * 1152]
                act.wait_ge(sem("logit_less"), b + 1)
                A_(T(6), T(6), ACT.Exp).then_inc(sem("mask_exp"), 1)
                act.wait_ge(sem("dx_dy"), b + 1)
                A_(T(2), T(0), ACT.Abs, bias=nhalf)
                A_(T(3), T(1), ACT.Abs, bias=nhalf)
                A_(T(0), T(0), ACT.Abs)
                A_(T(1), T(1), ACT.Abs).then_inc(sem("act_own"), 1)
                act.wait_ge(sem("act_own"), b * 1 + 1)
                for j in (0, 1, 2, 3):
                    last = A_(T(j), T(j), ACT.Relu, bias=one_c, scale=-1.0)
                last.then_inc(sem("hats"), 1)
                barrier()

            def F(b):
                def f1(i):
                    for h in range(2):
                        n = i * 2 + (b * CHUNKS + h)
                        done(act, "fT", n)
                        room(act, "fO", n)
                        A_(i2[4 + h], PS[:, 2 * h:2 * h + 2, :].rearrange("p k n -> p (k n)"), ACT.Copy)\
                            .then_inc(sem("fC"), 1)
                loop(ACT.Copy, f1)
                barrier()
                for k in range(KC):
                    last = A_(img1[:, k * HW:(k + 1) * HW], img1[:, k * HW:(k + 1) * HW], ACT.Identity,
                              accum_out=rsum[:, k:k + 1])
                last.then_inc(sem("r_summed"), 1)
                act.wait_ge(sem("se_z"), b + 1)
                A_(s_e, s_z, ACT.Exp, scale=-1.0).then_inc(sem("se_exp"), 1)
                barrier()

                def f2(i):
                    for h in range(2):
                        n = i * 2 + (b * CHUNKS + h)
                        for q in range(4):
                            done(act, "gH", n * 4 + q)
                            room(act, "gB", n * 4 + q)
                            for j in range(2):
                                last = A_(i2[4 + q % 2][:, j * CHUNK:(j + 1) * CHUNK], PS[:, 2 * (q % 2) + j, :], ACT.Identity,
                                          bias=fb[:, 2 * q + j:2 * q + j + 1])
                            last.then_inc(sem("gZ"), 1)
                loop(ACT.Identity, f2)
                barrier()

            def L1(b):
                deviation()
                act.wait_ge(sem("gn_ready"), count["gn"])
                for k in range(KC):
                    last = A_(img2[:, k * YPLANE:(k + 1) * YPLANE].rearrange("p (r x) -> p r x", x=YPITCH)[:, 1:H + 1, 1:W + 1],
                              rows(img1[:, k * HW:(k + 1) * HW]), ACT.Identity, bias=gn_t[:, k:k + 1], scale=gn_s[:, k:k + 1])
                act.wait_ge(sem("l1_z"), b + 1)
                A_(ang, ang, ACT.Tanh)
                A_(mz, mz, ACT.Exp, scale=-1.0).then_inc(sem("l1_tanh"), 1)
                act.wait_ge(sem("l1_angle"), b + 1)
                A_(sin_c, ang, ACT.Sin)
                A_(cos_c, cos_c, ACT.Sin).then_inc(sem("l1_sincos"), 1)
                act.wait_ge(sem("l1_uv"), b + 1)
                for src, dst in ((U, BX), (V_, AY)):
                    A_(dst[:, 0:18], src, ACT.Relu, scale=-1.0)
                    A_(dst[:, 36:54], src, ACT.Relu)
                    last = A_(dst[:, 18:36], src, ACT.Abs)
                last.then_inc(sem("l1_hats"), 1)
                barrier()
                barrier()

            def L2(b):
                deviation()
                barrier()
                E_, QS, QC = img2[:, 2048:4096], img2[:, 4096:6144], img2[:, 6144:8192]

                def la(i):
                    for h in range(2):
                        n, c = i * 2 + (b * CHUNKS + h), i * 2 + h
                        act.wait_ge(sem("cQT"), n + 1)
                        for k in range(KC):
                            last = A_(i2[h][:, k * CHUNK:(k + 1) * CHUNK], chunk_of(img1, k, c), ACT.Identity,
                                      bias=gn_t[:, k:k + 1], scale=gn_s[:, k:k + 1])
                        last.then_inc(sem("cXN"), 1)
                        act.wait_ge(sem("cM"), n + 1)
                        act.wait_ge(sem("cS"), n + 1)
                        A_(kalpha, kdif, ACT.Exp)
                        for m in range(KH):
                            last = A_(E_[:, m * CHUNK:(m + 1) * CHUNK], PS[:, m, :], ACT.Exp, bias=kneg[:, m:m + 1],
                                      accum_out=esum[:, m:m + 1])
                        last.then_inc(sem("cE"), 1)
                        act.wait_ge(sem("cQs"), n + 1)
                        A_(QS, QS, ACT.Exp).then_inc(sem("cQe"), 1)
                        for s in range(SUBS):
                            act.wait_ge(sem("cTT"), n * 4 + (s + 1))
                            room(act, "cKs", n * 4 + s)
                            A_(i2[8][:, (s % 2) * 512:(s % 2 + 1) * 512], PS[:, 6, :], ACT.Copy).then_inc(sem("cET"), 1)
                        act.wait_ge(sem("cQT"), n + 2)
                        act.wait_ge(sem("q_stored"), n * 16 + 16)
                        A_(QC, PS[:, 0:4, :].rearrange("p m n -> p (m n)"), ACT.Copy).then_inc(sem("cQC"), 1)
                loop(ACT.Exp, la)
                barrier()
                kxt, mt = wseg(wb_sb, Q_SIZE + 1024, 1024), wseg(wb_sb, Q_SIZE + 2048, 1024)
                act.wait_ge(sem("kx_turned"), b + 1)
                A_(kxt, PS[:, 0:2, :].rearrange("p m n -> p (m n)"), ACT.Copy).then_inc(sem("kxt_ready"), 1)
                act.wait_ge(sem("mt_ready"), b + 1)
                A_(mt, PS[:, 3:5, :].rearrange("p m n -> p (m n)"), ACT.Copy)
                barrier()

                def lb(i):
                    for h in range(2):
                        n, m_ = i * 2 + (b * CHUNKS + h), i + b * PAIRS
                        done(act, "bP", n)
                        act.wait_ge(sem(f"o_stored{h}"), m_ * 16 + 16)
                        room(act, "bS", n)
                        for oc in range(KC):
                            last = A_(i2[4 + h][:, oc * CHUNK:(oc + 1) * CHUNK], PS[:, 2 * h + oc, :], ACT.Identity,
                                      bias=v("b_out", oc))
                        last.then_inc(sem("bO"), 1)
                loop(ACT.Identity, lb)
                barrier()

            def L3():
                rf = ring[:].rearrange("p g c -> p (g c)")
                act.wait_ge(sem("o_var"), 1)
                A_(o_sd, o_mv.rearrange("p (k s) -> p s k", s=2)[:, 1, :], ACT.Sqrt, bias=eps_c).then_inc(sem("o_sd_ready"), 1)
                barrier()
                for b in range(B):
                    act.wait_ge(sem("e_loaded"), 32 * (b + 1))
                    for k in range(KC):
                        last = A_(rf[:, k * HW:(k + 1) * HW], rf[:, k * HW:(k + 1) * HW], ACT.Identity,
                                  bias=o_sh[:, k:k + 1], scale=o_sc[:, k:k + 1])
                    last.then_inc(sem("e_bn"), 1)
                    deviation()
                    act.wait_ge(sem("gn_ready"), count["gn"])
                    for k, (base, pitch, nr, top, left) in enumerate(((0, P0_PITCH, P0_ROWS, 5, 0), (P1_BASE, P1_PITCH, P1_ROWS, 1, 5))):
                        A_(img2[:, base:base + pitch * nr].rearrange("p (r x) -> p r x", x=pitch)[:, top:top + H, left:left + W],
                           rows(img1[:, k * HW:(k + 1) * HW]), ACT.Identity, bias=gn_t[:, k:k + 1], scale=gn_s[:, k:k + 1])
                    barrier()
                    barrier()

            for phase, b, gi in plan:
                if phase == "REST":
                    barrier()
                elif phase == "L3":
                    L3()
                else:
                    {"A": A, "F": F, "L1": L1, "L2": L2}[phase](b)

        @block.vector
        def _(dve):
            vec = nc.vector
            barrier = Barrier(dve, "dve")
            own = Own(dve, sem("dve_own"))
            link = own.link
            count = {"gn": 0, "wa": 0, "wb": 0}

            def loaded(region):
                count[region] += 1
                dve.wait_ge(sem(region + "_loaded"), 16 * count[region])

            def unit(b, t, g, j):
                dve.wait_ge(sem(f"gathered{g}"), t * (16 * K2) + 16 * K2 * (b * TILES + 1))
                rg = ring[:, g, :].rearrange("p (k c) -> p k c", c=GC)
                weights = seg(wt, t * (PTS * CORNERS) + g * K2 * CORNERS, K2 * CORNERS)
                vec.tensor_tensor(rg, rg, weights.unsqueeze(2).to_broadcast([P, K2 * CORNERS, GC]), ALU.mult)\
                    .then_inc(sem("weighted"), 1)
                dve.wait_ge(sem("weighted"), t * G + (b * TILES * G + g + 1))
                if g == 0:
                    dve.wait_ge(sem("d_stored"), t * 16 + (16 * b * TILES + 16 - 16 * j))
                vec.tensor_reduce(dbuf[:, j, g * GC:(g + 1) * GC], ring[:, g, :].rearrange("p (k c) -> p c k", c=GC),
                                  AX_X, ALU.add).then_inc(sem("ring_free"), 1)

            stream = Stream(unit)

            def chunks(part, gi, per, body):
                if gi is not None:
                    dve.wait_ge(sem("wt_loaded"), 16 * (gi + 1))
                with dve.Fori(0, PAIRS) as i:
                    own.settle()
                    own.enter(i, per)
                    stream.begin(part, gi, i)
                    body(i)
                    stream.finish()
                own.leave(PAIRS)
                stream.ended(part, gi)

            def moments_from(stats_):
                count["gn"] += 1
                q = count["gn"]
                for k in range(KC):
                    last = vec.bn_aggr(mv[:, 2 * k:2 * k + 2], stats_[:, k * 48:(k + 1) * 48].rearrange("p (c s) -> p c s", s=6))
                link(last)
                m_, va = mv.rearrange("p (k s) -> p s k", s=2)[:, 0, :], mv.rearrange("p (k s) -> p s k", s=2)[:, 1, :]
                ms2 = ms.rearrange("p (s k) -> p s k", s=2)
                link(vec.tensor_tensor(ms2[:, 1, :], m_, m_, ALU.mult))
                vec.tensor_copy(ms2[:, 0, :], m_)
                vec.tensor_tensor(ms2[:, 1, :], ms2[:, 1, :], va, ALU.add).then_inc(sem("gn_moments"), 1)
                dve.wait_ge(sem("gn_grouped"), q)
                link(vec.tensor_copy(gm, PS[:, 7, 0:4]))
                link(vec.tensor_tensor(gsq[:, 0:2], gm[:, 0:2], gm[:, 0:2], ALU.mult))
                link(vec.tensor_tensor(gvar, gm[:, 2:4], gsq[:, 0:2], ALU.subtract))
                vec.tensor_scalar(gvar, gvar, 0.0, None, ALU.max).then_inc(sem("gn_var"), 1)
                dve.wait_ge(sem("gn_sd"), q)
                link(vec.reciprocal(gn_s, gsd))
                vec.scalar_tensor_tensor(out=gn_t, in0=gm[:, 0:2], scalar=-1.0, in1=gn_s, op0=ALU.mult, op1=ALU.mult)\
                    .then_inc(sem("gn_ready"), 1)
                dve.wait_ge(sem("gn_ready"), q)

            def image_stats():
                for k in range(KC):
                    for c in range(CHUNKS):
                        last = vec.bn_stats(stats[:, (k * CHUNKS + c) * 6:(k * CHUNKS + c + 1) * 6],
                                            img1[:, k * HW + c * CHUNK:k * HW + (c + 1) * CHUNK])
                link(last)

            def leaky(o, i):
                return vec.scalar_tensor_tensor(out=o, in0=i, scalar=SLOPE, in1=i, op0=ALU.mult, op1=ALU.max)

            def clear_borders():
                for k in range(KC):
                    pl = img2[:, k * YPLANE:(k + 1) * YPLANE]
                    vec.memset(pl[:, 0:YPITCH + 1], 0.0)
                    vec.memset(pl[:, 2 * YPITCH - 1:(H + 1) * YPITCH - 1].rearrange("p (r x) -> p r x", x=YPITCH)[:, :, 0:2], 0.0)
                    vec.memset(pl[:, (H + 1) * YPITCH - 1:YPLANE], 0.0)

            def setup():
                vec.memset(dbuf[:, 0, :], 0.0).then_inc(sem("zeros"), 1)
                vec.memset(eps_c, EPS)
                vec.memset(one_c, 1.0)
                vec.memset(nhalf, -1.0)
                dve.wait_ge(sem("par_loaded"), 16)
                for j, nm in enumerate(("bn1", "dwbn", "bn2")):
                    last = vec.tensor_copy(bnv[:, 2 * j:2 * j + 2], v(nm + "_v"))
                last.then_inc(sem("bn_var"), 1)
                dve.wait_ge(sem("bn_sd"), 1)
                link(vec.reciprocal(bninv, bnv))
                for j, nm in enumerate(("bn1", "dwbn", "bn2")):
                    last = vec.tensor_tensor(bninv[:, 2 * j:2 * j + 2], bninv[:, 2 * j:2 * j + 2], v(nm + "_g"), ALU.mult)
                link(last)
                for j, nm in enumerate(("bn1", "dwbn", "bn2")):
                    last = vec.tensor_tensor(bnsh[:, 2 * j:2 * j + 2], bninv[:, 2 * j:2 * j + 2], v(nm + "_m"), ALU.mult)
                link(last)
                for j, nm in enumerate(("bn1", "dwbn", "bn2")):
                    last = vec.tensor_tensor(bnsh[:, 2 * j:2 * j + 2], v(nm + "_b"), bnsh[:, 2 * j:2 * j + 2], ALU.subtract)
                link(last)
                link(vec.tensor_tensor(gsq[:, 0:2], bninv[:, 2:4], v("dw_b"), ALU.mult))
                link(vec.tensor_tensor(bnsh[:, 2:4], bnsh[:, 2:4], gsq[:, 0:2], ALU.add))

            def A(b, gi):
                if b == 0:
                    setup()
                dve.wait_ge(sem("x_loaded"), 32 * (b + 1))
                image_stats()
                clear_borders()
                moments_from(stats)
                loaded("wa")
                dve.wait_ge(sem("a_bias"), b + 1)
                link(vec.tensor_tensor(cb1, PS[:, 6, 0:2], bninv[:, 0:2], ALU.mult))
                vec.tensor_tensor(cb1, cb1, bnsh[:, 0:2], ALU.add)
                for k in range(KC):
                    w_ = wa_sb[:, A_CONV + k * C:A_CONV + (k + 1) * C]
                    last = vec.tensor_scalar(w_, w_, gn_s[:, k:k + 1], None, ALU.mult)
                link(last)
                barrier()

                def a1(i):
                    for h in range(2):
                        n = i * 2 + (b * CHUNKS + h)
                        done(dve, "aZ", n)
                        leaky(ych[h], ych[h]).then_inc(sem("aY"), 1)
                        stream.give(1, 4)
                    for h in range(2):
                        n, m = i * 2 + (b * CHUNKS + h), i + b * PAIRS
                        done(dve, "aX", n)
                        dve.wait_ge(sem(f"t_stored{h}"), m * 256 + 16)
                        vec.tensor_tensor(xpt[h].rearrange("p (s c) -> p s c", s=SUBS),
                                          PS[:, 4 + 2 * h:6 + 2 * h, :].rearrange("p a (s c) -> p (a s) c", s=2),
                                          v("inproj_row").unsqueeze(1).to_broadcast([P, SUBS, C]), ALU.add)\
                            .then_inc(sem("aXE"), 1)
                chunks("A1", gi, 0, a1)
                barrier()
                OM = img1[:, 0:TILES * 3 * PTS]

                def a2(i):
                    for h in range(2):
                        n = i * 2 + (b * CHUNKS + h)
                        done(dve, "dZ", n)
                        leaky(ych[h], ych[h]).then_inc(sem("dT"), 1)
                        stream.give(1, 4)
                    for h in range(2):
                        n, c = i * 2 + (b * CHUNKS + h), i * 2 + h
                        done(dve, "dO", n)
                        vec.tensor_tensor(seg(OM, c * (SUBS * 3 * PTS), SUBS * 3 * PTS).rearrange("p (s c) -> p s c", s=SUBS),
                                          PS[:, 4 + h, 0:SUBS * 3 * PTS].rearrange("p (s c) -> p s c", s=SUBS),
                                          v("om_row").unsqueeze(1).to_broadcast([P, SUBS, 3 * PTS]), ALU.add)\
                            .then_inc(sem("dE"), 1)
                chunks("A2", gi, 0, a2)
                barrier()

                T = lambda j: img1[:, 3456 + j * 1152:3456 + (j + 1) * 1152] if j < 4 else \
                    img2[:, 4608 + (j - 4) * 1152:4608 + (j - 3) * 1152]
                om3 = OM.rearrange("p (t c) -> p t c", c=3 * PTS)
                ox, oy, ml = (om3[:, :, j * PTS:(j + 1) * PTS] for j in range(3))
                tp = lambda a: a.rearrange("p (t c) -> p t c", c=PTS)
                t9 = lambda a: a.rearrange("p (t k) -> p t k", k=K2)
                link(vec.tensor_reduce(stats8(0), ml4(ml), AX_X, ALU.max))
                vec.tensor_tensor(t9(T(6)).rearrange("p (t g) k -> p t g k", g=G), ml4(ml),
                                  stats8(0).unsqueeze(3).to_broadcast([P, TILES, G, K2]), ALU.subtract)\
                    .then_inc(sem("logit_less"), 1)
                vec.tensor_tensor(tp(T(0)), ox, v("gx_base").unsqueeze(1).to_broadcast([P, TILES, PTS]), ALU.add)
                link(vec.tensor_tensor(T(1).rearrange("p (t g k) -> p t g k", g=G, k=K2), oy.rearrange("p t (g k) -> p t g k", k=K2),
                                       v("gy_base").rearrange("p (t k) -> p t k", k=K2).unsqueeze(2).to_broadcast([P, TILES, G, K2]),
                                       ALU.add))
                for a, t in ((0, 4), (1, 5)):
                    last = vec.tensor_scalar(T(t), T(a), 0.0, float(W - 2), ALU.max, ALU.min)
                link(last)
                for t in (4, 5):
                    last = vec.tensor_scalar(T(t), T(t), -0.5, MAGIC, ALU.add, ALU.add)
                link(last)
                for t in (4, 5):
                    last = vec.tensor_scalar(T(t), T(t), -MAGIC, None, ALU.add)
                link(last)
                for a, t in ((0, 4), (1, 5)):
                    last = vec.tensor_tensor(T(a), T(a), T(t), ALU.subtract)
                last.then_inc(sem("dx_dy"), 1)
                link(vec.scalar_tensor_tensor(out=T(7), in0=T(5), scalar=float(W), in1=T(4), op0=ALU.mult, op1=ALU.add))
                vec.tensor_tensor(img1[:, 0:TILES * PTS].bitcast(U32).rearrange("p (t g k) -> p t g k", g=G, k=K2),
                                  T(7).rearrange("p (t g k) -> p t g k", g=G, k=K2),
                                  v("g_base").unsqueeze(1).unsqueeze(3).to_broadcast([P, TILES, G, K2]), ALU.add)\
                    .then_inc(sem("idx_made"), 1)
                dve.wait_ge(sem("mask_exp"), b + 1)
                link(vec.tensor_reduce(stats8(0), T(6).rearrange("p (t g k) -> p t g k", g=G, k=K2), AX_X, ALU.add))
                link(vec.reciprocal(stats8(1), stats8(0)))
                link(vec.tensor_tensor(T(6).rearrange("p (t g k) -> p t g k", g=G, k=K2), T(6).rearrange("p (t g k) -> p t g k", g=G, k=K2),
                                       stats8(1).unsqueeze(3).to_broadcast([P, TILES, G, K2]), ALU.mult))
                dve.wait_ge(sem("hats"), b + 1)
                vec.tensor_tensor(T(4), T(1), T(6), ALU.mult)
                link(vec.tensor_tensor(T(5), T(3), T(6), ALU.mult))
                Wt = img2[:, 0:4608].rearrange("p (n j) -> p j n", j=CORNERS)
                for j, (my, wx) in enumerate(((4, 0), (4, 2), (5, 0), (5, 2))):
                    last = vec.tensor_tensor(Wt[:, j, :], T(my), T(wx), ALU.mult)
                last.then_inc(sem("w_made"), 1)
                barrier()

            def stats8(j):
                return cb[:, j * 128:(j + 1) * 128].rearrange("p (t g) -> p t g", g=G)

            def ml4(ml):
                return ml.rearrange("p t (g k) -> p t g k", k=K2)

            def F(b, gi):
                loaded("wb")

                def f1(i):
                    for h in range(2):
                        n, m, c = i * 2 + (b * CHUNKS + h), i + b * PAIRS, i * 2 + h
                        done(dve, "fO", n)
                        dve.wait_ge(sem(f"fY{h}"), m * 16 + 16)
                        for oc in range(KC):
                            last = vec.scalar_tensor_tensor(out=chunk_of(img1, oc, c), in0=PS[:, 4 + 2 * h + oc, :],
                                                            scalar=v("outproj_b", oc),
                                                            in1=i2[2 + h][:, oc * CHUNK:(oc + 1) * CHUNK],
                                                            op0=ALU.add, op1=ALU.add)
                        last.then_inc(sem("fR"), 1)
                        stream.give(1, 2)
                chunks("F1", gi, 0, f1)
                barrier()
                dve.wait_ge(sem("r_summed"), b + 1)
                link(vec.tensor_scalar(xmean, rsum, 1.0 / HW, None, ALU.mult))
                link(vec.tensor_tensor(xmean, xmean, bninv[:, 4:6], ALU.mult))
                vec.tensor_tensor(xmean, xmean, bnsh[:, 4:6], ALU.add).then_inc(sem("se_mean"), 1)
                dve.wait_ge(sem("se_down"), b + 1)
                vec.tensor_scalar(s_hid[0:64, 0:1], PS[0:64, 7, 0:1], v("se_down_b", 0, 64), 0.0, ALU.add, ALU.max)\
                    .then_inc(sem("se_hidden"), 1)
                dve.wait_ge(sem("se_up"), b + 1)
                vec.tensor_tensor(s_z, PS[:, 6, 0:2], v("se_up_b"), ALU.add).then_inc(sem("se_z"), 1)
                dve.wait_ge(sem("se_exp"), b + 1)
                link(vec.tensor_scalar(s_g, s_e, 1.0, None, ALU.add))
                link(vec.reciprocal(s_g, s_g))
                vec.tensor_tensor(s_ga, s_g, bninv[:, 4:6], ALU.mult)
                vec.tensor_tensor(s_gc, s_g, bnsh[:, 4:6], ALU.mult).then_inc(sem("se_gate"), 1)
                dve.wait_ge(sem("fc1_shift"), b + 1)
                vec.tensor_tensor(fb, PS[:, 5, 0:FC], v("fc1_b"), ALU.add)
                for k in range(KC):
                    w_ = wb_sb[:, F_FC1 + k * 4 * C:F_FC1 + (k + 1) * 4 * C]
                    last = vec.tensor_scalar(w_, w_, s_ga[:, k:k + 1], None, ALU.mult)
                link(last)
                barrier()

                def f2(i):
                    for h in range(2):
                        n, m, c = i * 2 + (b * CHUNKS + h), i + b * PAIRS, i * 2 + h
                        for q in range(4):
                            done(dve, "gZ", n * 4 + q)
                            room(dve, "gD", n * 4 + q)
                            leaky(i2[6 + q % 2], i2[4 + q % 2]).then_inc(sem("gB"), 1)
                            stream.give(1, 8)
                        done(dve, "gD", n * 4 + 3)
                        dve.wait_ge(sem(f"gYl{h}"), m * 16 + 16)
                        for oc in range(KC):
                            last = vec.scalar_tensor_tensor(out=i2[8][:, oc * CHUNK:(oc + 1) * CHUNK], in0=PS[:, 4 + 2 * h + oc, :],
                                                            scalar=v("fc2_b", oc), in1=i2[h][:, oc * CHUNK:(oc + 1) * CHUNK],
                                                            op0=ALU.add, op1=ALU.add)
                        link(last)
                        dve.wait_ge(sem(f"gXl{h}"), m * 16 + 16)
                        for oc in range(KC):
                            last = vec.tensor_tensor(chunk_of(img1, oc, c), i2[8][:, oc * CHUNK:(oc + 1) * CHUNK],
                                                     i2[2 + h][:, oc * CHUNK:(oc + 1) * CHUNK], ALU.add)
                        last.then_inc(sem("gX"), 1)
                        done(dve, "gX", n)
                        for k in range(KC):
                            vec.bn_stats(seg(stats, c * 6 + k * 48, 6), chunk_of(img1, k, c))
                chunks("F2", gi, 2, f2)
                barrier()

            def L1(b, gi):
                clear_borders()
                moments_from(stats)
                link(vec.tensor_tensor(pooled, mv.rearrange("p (k s) -> p s k", s=2)[:, 0, :], gn_s, ALU.mult))
                vec.tensor_tensor(pooled, pooled, gn_t, ALU.add).then_inc(sem("pooled"), 1)
                loaded("wa")
                dve.wait_ge(sem("l1_hidden"), b + 1)
                vec.tensor_scalar(a_hid[0:64, :], PS[0:64, 6, 0:1], v("ap_b1", 0, 64), 0.0, ALU.add, ALU.max)
                vec.tensor_scalar(m_hid[0:64, :], PS[0:64, 6, 1:2], v("meta_b1", 0, 64), 0.0, ALU.add, ALU.max)\
                    .then_inc(sem("l1_relu"), 1)
                dve.wait_ge(sem("l1_heads"), b + 1)
                vec.tensor_tensor(ang, PS[:, 5, 0:2], v("ap_b2"), ALU.add)
                vec.tensor_tensor(mz, PS[:, 5, 2:4], v("meta_b2"), ALU.add).then_inc(sem("l1_z"), 1)
                dve.wait_ge(sem("l1_tanh"), b + 1)
                link(vec.tensor_scalar(ang, ang, 0.7853981633974483, None, ALU.mult))
                vec.tensor_scalar(cos_c, ang, 1.5707963267948966, None, ALU.add).then_inc(sem("l1_angle"), 1)
                link(vec.tensor_scalar(mod, mz, 1.0, None, ALU.add))
                link(vec.reciprocal(mod, mod))
                lt = wseg(wa_sb, R_SIZE, KC * K2 * P)
                link(vec.memset(lt, 0.0))
                dve.wait_ge(sem("l1_sincos"), b + 1)
                for k in range(KC):
                    for tap in range(K2):
                        yy, xx = tap // 3 - 1, tap % 3 - 1
                        at = k * K2 + tap
                        vec.tensor_scalar(U[:, at:at + 1], cos_c[:, k:k + 1], float(xx), None, ALU.mult)
                        last = vec.tensor_scalar(V_[:, at:at + 1], cos_c[:, k:k + 1], float(yy), None, ALU.mult)
                link(last)
                for k in range(KC):
                    for tap in range(K2):
                        yy, xx = tap // 3 - 1, tap % 3 - 1
                        at = k * K2 + tap
                        vec.scalar_tensor_tensor(out=U[:, at:at + 1], in0=sin_c[:, k:k + 1], scalar=float(yy),
                                                 in1=U[:, at:at + 1], op0=ALU.mult, op1=ALU.add)
                        last = vec.scalar_tensor_tensor(out=V_[:, at:at + 1], in0=sin_c[:, k:k + 1], scalar=float(-xx),
                                                        in1=V_[:, at:at + 1], op0=ALU.mult, op1=ALU.add)
                last.then_inc(sem("l1_uv"), 1)
                dve.wait_ge(sem("l1_hats"), b + 1)
                for t in (BX, AY):
                    last = vec.tensor_scalar(t[:, 18:36], t[:, 18:36], -1.0, 1.0, ALU.mult, ALU.add)
                link(last)
                cf = coef.rearrange("p (n q) -> p n q", n=K2)
                for j in range(3):
                    for i in range(3):
                        last = vec.tensor_tensor(cf[:, j * 3 + i, :], AY[:, j * 18:(j + 1) * 18], BX[:, i * 18:(i + 1) * 18], ALU.mult)
                link(last)
                acc = cb[:, KC * K2 * K2:KC * K2 * (K2 + CG)].rearrange("p (k t o) -> p k t o", k=KC, t=K2)
                prod = cb[:, KC * K2 * (K2 + CG):KC * K2 * (K2 + 2 * CG)].rearrange("p (k t o) -> p k t o", k=KC, t=K2)
                base = wseg(wa_sb, R_BASE, KC * K2 * CG).rearrange("p (k t o) -> p k t o", k=KC, t=K2)
                for n in range(K2):
                    dst = acc if n == 0 else prod
                    for k in range(KC):
                        last = vec.tensor_tensor(dst[:, k], base[:, k, n, :].unsqueeze(1).to_broadcast([P, K2, CG]),
                                                 cf[:, n, k * K2:(k + 1) * K2].unsqueeze(2).to_broadcast([P, K2, CG]), ALU.mult)
                    link(last)
                    if n:
                        link(vec.tensor_tensor(acc, acc, prod, ALU.add))
                lt4 = lt.rearrange("p (k t o) -> p k t o", k=KC, t=K2)
                for q in range(P // CG):
                    for k in range(KC):
                        last = vec.tensor_copy(lt4[q * CG:(q + 1) * CG, k, :, q * CG:(q + 1) * CG], acc[q * CG:(q + 1) * CG, k])
                link(last)
                barrier()

                def l1(i):
                    for h in range(2):
                        n, c = i * 2 + (b * CHUNKS + h), i * 2 + h
                        done(dve, "lC", n)
                        for k in range(KC):
                            last = vec.scalar_tensor_tensor(out=chunk_of(img1, k, c), in0=PS[:, 2 * h + k, :], scalar=mod[:, k:k + 1],
                                                            in1=chunk_of(img1, k, c), op0=ALU.mult, op1=ALU.add)
                        last.then_inc(sem("lX"), 1)
                        done(dve, "lX", n)
                        for k in range(KC):
                            vec.bn_stats(seg(stats, c * 6 + k * 48, 6), chunk_of(img1, k, c))
                        stream.give(1, 2)
                chunks("L1", gi, 0, l1)
                barrier()

            def L2(b, gi):
                kx = wseg(wb_sb, Q_SIZE, 1024)
                bd = wseg(wb_sb, Q_SIZE + 3072, 512)
                loaded("wb")
                vec.memset(kmax, -3.0e38)
                vec.memset(ksum, 0.0)
                vec.memset(kx, 0.0)
                vec.memset(bd, 0.0)
                moments_from(stats)
                barrier()
                QS = img2[:, 4096:6144]
                qs3 = QS.rearrange("p (a d) -> p a d", d=DH)

                def la(i):
                    for h in range(2):
                        n = i * 2 + (b * CHUNKS + h)
                        dve.wait_ge(sem("cK"), n + 1)
                        link(vec.tensor_reduce(cmax, PS[:, 0:4, :], AX_X, ALU.max))
                        link(vec.tensor_tensor(knew, kmax, cmax, ALU.max))
                        vec.tensor_tensor(kdif, kmax, knew, ALU.subtract)
                        vec.tensor_scalar(kneg, knew, -1.0, None, ALU.mult).then_inc(sem("cM"), 1)
                        dve.wait_ge(sem("cM"), n + 1)
                        vec.tensor_copy(kmax, knew)
                        dve.wait_ge(sem("cQ"), n + 1)
                        link(vec.tensor_reduce(qmax, PS[:, 0:4, :].rearrange("p s (a d) -> p (s a) d", d=DH), AX_X, ALU.max))
                        dve.wait_ge(sem("cQT"), n + 1)
                        vec.tensor_tensor(qs3, PS[:, 0:4, :].rearrange("p s (a d) -> p (s a) d", d=DH),
                                          qmax.unsqueeze(2).to_broadcast([P, 32, DH]), ALU.subtract).then_inc(sem("cQs"), 1)
                        for s in range(SUBS):
                            dve.wait_ge(sem("cTT"), n * 4 + (s + 1))
                            room(dve, "cKs", n * 4 + s)
                            vec.tensor_copy(cb[:, (s % 2) * C:(s % 2 + 1) * C], PS[:, 7, 0:C]).then_inc(sem("cXT"), 1)
                        dve.wait_ge(sem("cQe"), n + 1)
                        link(vec.tensor_reduce(qsum, qs3, AX_X, ALU.add))
                        link(vec.reciprocal(qsum, qsum))
                        vec.tensor_tensor(qs3, qs3, qsum.unsqueeze(2).to_broadcast([P, 32, DH]), ALU.mult).then_inc(sem("cQn"), 1)
                        done(dve, "cKs", n * 4 + 3)
                        link(vec.tensor_tensor(ksum, ksum, kalpha, ALU.mult))
                        vec.tensor_tensor(ksum, ksum, esum, ALU.add)
                        for m in range(KH):
                            last = vec.scalar_tensor_tensor(out=kx[:, m * C:(m + 1) * C], in0=kx[:, m * C:(m + 1) * C],
                                                            scalar=kalpha[:, m:m + 1],
                                                            in1=PS[:, 4 + m // 2, (m % 2) * C:(m % 2 + 1) * C],
                                                            op0=ALU.mult, op1=ALU.add)
                        last.then_inc(sem("cS"), 1)
                        dve.wait_ge(sem("cS"), n + 2)
                chunks("L2a", gi, 12, la)
                barrier()
                link(vec.reciprocal(ksum, ksum))
                link(vec.tensor_scalar(ksum, ksum, DH ** -0.5 / HW, None, ALU.mult))
                for m in range(KH):
                    last = vec.tensor_scalar(kx[:, m * C:(m + 1) * C], kx[:, m * C:(m + 1) * C], ksum[:, m:m + 1], None, ALU.mult)
                last.then_inc(sem("kx_scaled"), 1)
                dve.wait_ge(sem("ctx_ready"), b + 1)
                for q in range(2):
                    r = slice(q * DH, (q + 1) * DH)
                    last = vec.tensor_copy(bd.rearrange("p (m d) -> p m d", m=KH)[r, :, r],
                                           PS[:, 2, :].rearrange("p (m d) -> p m d", m=KH)[r, :, r])
                last.then_inc(sem("ctx_diagonal"), 1)
                barrier()

                def lb(i):
                    for h in range(2):
                        n, c = i * 2 + (b * CHUNKS + h), i * 2 + h
                        done(dve, "bO", n)
                        for k in range(KC):
                            last = vec.bn_stats(seg(ostats, c * 6 + (k * B + b) * CHUNKS * 6, 6), i2[4 + h][:, k * CHUNK:(k + 1) * CHUNK])
                        last.then_inc(sem("bS"), 1)
                        stream.give(1, 2)
                chunks("L2b", gi, 0, lb)
                barrier()

            def L3():
                rf = ring[:].rearrange("p g c -> p (g c)")
                for k in range(KC):
                    last = vec.bn_aggr(o_mv[:, 2 * k:2 * k + 2],
                                       ostats[:, k * B * 48:(k + 1) * B * 48].rearrange("p (c s) -> p c s", s=6))
                last.then_inc(sem("o_var"), 1)
                dve.wait_ge(sem("o_sd_ready"), 1)
                link(vec.reciprocal(o_sc, o_sd))
                link(vec.tensor_tensor(o_sc, o_sc, v("gamma"), ALU.mult))
                link(vec.tensor_tensor(o_sh, o_mv.rearrange("p (k s) -> p s k", s=2)[:, 0, :], o_sc, ALU.mult))
                vec.tensor_tensor(o_sh, v("beta"), o_sh, ALU.subtract)
                loaded("wb")
                n0 = len(L3_TAPS0) * P
                for k, (a, e) in enumerate(((0, n0), (n0, L3_TAPS * P))):
                    w_ = wb_sb[:, a:e]
                    s_ = v("l3_s", k)
                    link(vec.reciprocal(o_rs, s_))
                    link(vec.tensor_scalar(w_, w_, o_rs, MAGIC, ALU.mult, ALU.add))
                    link(vec.tensor_scalar(w_, w_, -MAGIC, -8.0, ALU.add, ALU.max))
                    link(vec.tensor_scalar(w_, w_, 7.0, s_, ALU.min, ALU.mult))
                mid = wb_sb[:, 5 * P:6 * P]
                vec.tensor_copy(wb_sb[0:64, 5 * P:5 * P + 64], params[0:64, COL["ident"][0]:COL["ident"][0] + 64])
                vec.memset(img2[:], 0.0)
                barrier()
                for b in range(B):
                    dve.wait_ge(sem("e_loaded"), 32 * (b + 1))
                    dve.wait_ge(sem("e_bn"), b + 1)
                    link(vec.tensor_tensor(img1[:], img1[:], rf[:, 0:KC * HW], ALU.add))
                    image_stats()
                    moments_from(stats)
                    barrier()
                    with dve.Fori(0, PAIRS) as i:
                        for h in range(2):
                            n, c, m = i * 2 + (b * CHUNKS + h), i * 2 + h, i + b * PAIRS
                            done(dve, "eC", n)
                            dve.wait_ge(sem(f"out_stored{h}"), m * 16 + 16)
                            for k in range(KC):
                                last = vec.scalar_tensor_tensor(out=ych[h][:, k * CHUNK:(k + 1) * CHUNK], in0=PS[:, 2 * h + k, :],
                                                                scalar=v("l3_b", k), in1=chunk_of(img1, k, c),
                                                                op0=ALU.add, op1=ALU.add)
                            last.then_inc(sem("eX"), 1)
                    barrier()

            for phase, b, gi in plan:
                if phase == "REST":
                    stream.rest(dve, gi)
                    barrier()
                elif phase == "L3":
                    L3()
                else:
                    {"A": A, "F": F, "L1": L1, "L2": L2}[phase](b, gi)


def _lay_out(i):
    import numpy as np
    f = np.float32
    a = {k: np.asarray(x) for k, x in i.items()}

    def g(name):
        return a[name]

    def turned(w):
        o, n = w.shape
        return np.ascontiguousarray(w.T.reshape(n // P, P, o).transpose(1, 0, 2)).reshape(P, -1)

    def low(w):
        z = np.zeros((P, w.shape[0]), f)
        z[:w.shape[1]] = w.T
        return z

    par = np.zeros((P, NPAR), f)

    def put(name, value):
        c, w = COL[name]
        par[:value.shape[0], c:c + w] = value

    def vec(name, value):
        n = value.shape[0]
        put(name, value.reshape(n // P, P).T if n >= P else value[:, None])

    L = "L0_conv_"
    for nm in ("bn1_g", "bn1_b", "bn1_m", "bn1_v", "dwbn_g", "dwbn_b", "dwbn_m", "dwbn_v", "dw_b",
               "bn2_g", "bn2_b", "bn2_m", "bn2_v", "outproj_b", "fc1_b", "fc2_b", "se_down_b", "se_up_b"):
        vec(nm, g(L + nm))
    vec("ap_b1", g("L1_conv_ap_b1"))
    vec("ap_b2", np.repeat(g("L1_conv_ap_b2"), CG))
    vec("meta_b1", g("L1_conv_meta_b1"))
    vec("meta_b2", g("L1_conv_meta_b2"))
    vec("b_out", g("L2_conv_b_out"))
    vec("gamma", g("L2_conv_gamma"))
    vec("beta", g("L2_conv_beta"))
    z64 = np.zeros(64, f)
    vec("l3_b", np.concatenate([z64, g("L3_conv_b_h"), g("L3_conv_b_w"), g("L3_conv_b_hw")]))
    full = lambda s, n: np.broadcast_to(np.asarray(s, f).reshape(1), (n,))
    vec("l3_s", np.concatenate([full(g("L3_conv_s_h"), 128), full(g("L3_conv_s_w"), 64), full(g("L3_conv_s_hw"), 64)]))
    put("inproj_row", np.broadcast_to(g(L + "inproj_b"), (P, C)))
    ob = g(L + "off_b")
    put("om_row", np.broadcast_to(np.concatenate([ob[0::2], ob[1::2], g(L + "mask_b")]), (P, 3 * PTS)))
    put("ident", np.eye(P, dtype=f))
    put("gavg", np.kron(np.eye(P // 8, dtype=f), np.full((8, 8), 0.125, f)))
    pix = np.arange(P)
    put("gx_base", (pix % W)[:, None] + (DIL * (np.arange(PTS) % K2 // 3 - 1))[None, :].astype(f))
    hy = (pix // W)[:, None, None] + (2 * np.arange(TILES))[None, :, None] + (DIL * (np.arange(K2) % 3 - 1))[None, None, :]
    put("gy_base", hy.reshape(P, -1).astype(f))
    put("g_base", np.broadcast_to(np.arange(G) * TAB_ROWS + TAB_FRONT, (P, G)).astype(f))

    ow = g(L + "off_w")
    om = np.concatenate([ow[0::2], ow[1::2], g(L + "mask_w")])
    dw = np.zeros((P, KC, K2, P), f)
    taps = g(L + "dw_w").reshape(KC, P, K2)
    for k in range(KC):
        for t in range(K2):
            dw[pix, k, t, pix] = taps[k, :, t]
    wa = np.concatenate([turned(g(L + "conv_w")), turned(g(L + "inproj_w")), turned(om), dw.reshape(P, -1)], 1)
    wf = np.concatenate([turned(g(L + "outproj_w")), turned(g(L + "fc1_w")), turned(g(L + "fc2_w")),
                         turned(g(L + "se_down_w")), low(g(L + "se_up_w"))], 1)
    bk = g("L1_conv_base_kernel").reshape(KC, P // CG, CG, CG, K2)
    bk = bk.transpose(1, 3, 0, 4, 2).reshape(P, -1)
    wr = np.concatenate([bk, turned(g("L1_conv_ap_w1")), turned(g("L1_conv_meta_w1")),
                         low(np.repeat(g("L1_conv_ap_w2"), CG, axis=0)), low(g("L1_conv_meta_w2"))], 1)
    qkv = g("L2_conv_w_qkv")
    wq = np.concatenate([turned(qkv[0:HID]), turned(qkv[HID:2 * HID]), turned(qkv[2 * HID:]), turned(g("L2_conv_w_out"))], 1)

    w3 = np.zeros((P, L3_TAPS, P), f)

    def place(t, base, w, ky, kx):
        for q in range(16):
            w3[base + 4 * q:base + 4 * q + 4, t, base + 4 * q:base + 4 * q + 4] = w[4 * q:4 * q + 4, :, ky, kx].T

    for t, (dy, dx) in enumerate(L3_TAPS0):
        place(t, 64, g("L3_conv_w_h"), dy + 5, 0)
    for t, (dy, dx) in enumerate(L3_TAPS1, len(L3_TAPS0)):
        if dy == 0:
            place(t, 0, g("L3_conv_w_w"), 0, dx + 5)
        if abs(dx) <= 1:
            place(t, 64, g("L3_conv_w_hw"), dy + 1, dx + 1)
    return dict(x=a["x"], par=par, wa=wa, wr=wr, wf=wf, wq=wq, w3=w3.reshape(P, -1))


def kernel(**inputs):
    import numpy as _np
    import concourse.bacc as _bacc
    from concourse import mybir as _mybir
    from concourse.bass_utils import run_bass_kernel_spmd as _run

    nc = _bacc.Bacc("TRN2", target_bir_lowering=False, num_devices=1)
    arrays, args = {}, []
    for name, a in _lay_out(inputs).items():
        a = _np.ascontiguousarray(a)
        arrays[f"in_{name}"] = a
        args.append(nc.dram_tensor(f"in_{name}", a.shape, _mybir.dt.from_np(a.dtype), kind="ExternalInput").ap())
    args.append(nc.dram_tensor("out", (B, C, H, W), F32, kind="ExternalOutput").ap())
    network_kernel(nc, *args)
    r = _run(nc, [arrays], core_ids=[0])
    return r.results[0]["out"]
```

```python
from contextlib import ExitStack

import concourse.bass as bass
from concourse import mybir

ALU = mybir.AluOpType
ACT = mybir.ActivationFunctionType
AX_X = mybir.AxisListType.X
F32 = mybir.dt.float32
F16 = mybir.dt.float16
U32 = mybir.dt.uint32

B, C, H, W = 4, 256, 64, 64
P = 128
KC = C // P
HW = H * W
CHUNK = 512
ROWS = CHUNK // W
CHUNKS = HW // CHUNK
PAIRS = CHUNKS // 2
SUBS = CHUNK // P
TILES = HW // P
G, K2 = 4, 9
GC = C // G
PTS = G * K2
CORNERS = 4
DIL = 6
FC = 4 * C // P
HEADS, DH = 8, 64
HID = HEADS * DH
KH = HID // P
CG = 32
EPS = 1e-5
SLOPE = 0.01
MAGIC = 12582912.0
TAB_FRONT = W + 1
TAB_ROWS = HW + P
YPITCH = W + 2
YPLANE = (H + 2) * YPITCH
SETS, SC = 4, 64
HALFP = HW // 2
L3_STEPS = 4
PAIR_ROWS = H // 2 // L3_STEPS
PH_PITCH, PH_SIZE = W, (H // 2 + 5) * W
PW_PITCH, PW_SIZE = W + 5, (H // 2) * (W + 5) + 16
PX_PITCH, PX_SIZE = W + 1, (H // 2 + 1) * (W + 1) + 8
IMG2 = 9 * 1024
L3_TAPS_H = [(d, 0) for d in range(-2, 4)]
L3_TAPS_W = [(0, dx) for dx in range(-5, 6)]
L3_TAPS_X = [(d, dx) for d in (0, 1) for dx in (-1, 0, 1)]
L3_TAPS = len(L3_TAPS_H) + len(L3_TAPS_W) + len(L3_TAPS_X)
START = 2

VECS = [("bn1_g", 2), ("bn1_b", 2), ("bn1_m", 2), ("bn1_v", 2),
        ("dwbn_g", 2), ("dwbn_b", 2), ("dwbn_m", 2), ("dwbn_v", 2), ("dw_b", 2),
        ("bn2_g", 2), ("bn2_b", 2), ("bn2_m", 2), ("bn2_v", 2),
        ("outproj_b", 2), ("fc1_b", 8), ("fc2_b", 2), ("se_down_b", 1), ("se_up_b", 2),
        ("ap_b1", 1), ("ap_b2", 2), ("meta_b1", 1), ("meta_b2", 2),
        ("b_out", 2), ("gamma", 2), ("beta", 2), ("l3_b", 4), ("l3_s", 3),
        ("inproj_row", 256), ("om_row", 3 * PTS), ("ident", P), ("gavg", P), ("gavg2", P), ("dw_taps", K2), ("tap_x", K2), ("tap_y", K2), ("tap_nx", K2),
        ("gx_base", PTS), ("gy_base", TILES * K2), ("g_base", PTS)]
COL, _at = {}, 0
for _name, _width in VECS:
    COL[_name] = (_at, _width)
    _at += _width
NPAR = _at

A_CONV, A_INP, A_OM, A_DW = 0, 512, 1024, 1024 + 2 * 3 * PTS
A_SIZE = A_DW + K2 * P
F_OUT, F_FC1, F_FC2 = 0, 512, 512 + KC * 4 * C
F_DOWN = F_FC2 + FC * C
F_UP = F_DOWN + KC * 64
F_SIZE = F_UP + C
R_BASE = 0
R_AP1 = KC * K2 * CG
R_ME1 = R_AP1 + KC * 64
R_AP2 = R_ME1 + KC * 64
R_ME2 = R_AP2 + C
R_SIZE = R_ME2 + C
Q_Q, Q_K, Q_V, Q_O = 0, KC * HID, 2 * KC * HID, 3 * KC * HID
Q_SIZE = Q_O + KH * C
WA_SIZE = R_SIZE + KC * K2 * P
WB_SIZE = Q_SIZE + 3 * 1024 + 512
assert A_SIZE <= WA_SIZE and F_SIZE <= WB_SIZE


class Own:

    def __init__(self, eng, sem):
        self.eng, self.sem, self.n, self.at, self.k = eng, sem, 0, 0, 0

    def enter(self, it, per):
        self.at, self.per, self.k = it * per, per, 0

    def leave(self, times):
        assert self.k == self.per, (self.k, self.per)
        self.n += self.per * times
        self.at, self.k = 0, 0

    def link(self, ins):
        self.k += 1
        ins.then_inc(self.sem, 1)
        self.eng.wait_ge(self.sem, self.at + (self.n + self.k))

    def settle(self):
        self.n, self.k = self.n + self.k, 0


def network_kernel(nc, x, par, wa, wr, wf, wq, w3, out):
    ctx = ExitStack()
    with ctx:
        def sb(name, shape, dt=F32):
            return ctx.enter_context(nc.sbuf_tensor(name, shape, dt))

        def dram(name, shape):
            return nc.dram_tensor(name, shape, F32, kind="Internal").ap()

        sems = {}

        def sem(name):
            if name not in sems:
                sems[name] = ctx.enter_context(nc.semaphore(name))
            return sems[name]

        y_dram = dram("y_dram", [B, P, KC, HW])
        tab = [dram(f"table{b}", [G * TAB_ROWS, CORNERS * GC]) for b in range(B)]
        w_dram = dram("w_dram", [B, P, TILES * PTS * CORNERS])
        idx_dram = nc.dram_tensor("idx_dram", [B, P, TILES * PTS], U32, kind="Internal").ap()
        d_dram = dram("d_dram", [B, TILES, P, C])
        q_dram = dram("q_dram", [B, P, CHUNKS, KH, CHUNK])
        o_dram = dram("o_dram", [B, P, KC, 2, HALFP])
        x2_dram = dram("x2_dram", [B, P, KC, 2, HALFP])

        params = sb("params", [P, NPAR])
        wa_sb = sb("wa_sb", [P, WA_SIZE])
        wb_sb = sb("wb_sb", [P, WB_SIZE])
        ring = sb("ring", [P, G, K2 * CORNERS * GC])
        idx = sb("idx", [P, 2, TILES * PTS], U32)
        idx_stage = sb("idx_stage", [P, 2, 2 * PTS], U32)
        wt = sb("wt", [P, TILES * PTS * CORNERS])
        dbuf = sb("dbuf", [P, 4, C])
        img1 = sb("img1", [P, KC * HW])
        img2 = sb("img2", [P, IMG2])
        cb = sb("cb", [P, 4 * 1024])
        stats = sb("stats", [P, KC * CHUNKS * 6])
        ostats = sb("ostats", [P, KC * B * CHUNKS * 6])
        sm = sb("sm", [P, 496])
        PS = ctx.enter_context(nc.psum_tensor("PS", [P, 8, 512], F32))

        def v(name, k=None, rows=P):
            a, w = COL[name]
            return params[0:rows, a:a + w] if k is None else params[0:rows, a + k:a + k + 1]

        used = [0]

        def small(n):
            a = used[0]
            used[0] += n
            return sm[:, a:a + n]

        mv, ms, gm = small(4), small(4), small(4)
        gvar, gsd, gn_s, gn_t, gsq = small(2), small(2), small(2), small(2), small(4)
        eps_c, one_c, neg_one = small(1), small(1), small(1)
        bnv, bninv, bnsh = small(6), small(6), small(6)
        cb1 = small(2)
        rsum, xmean, s_hid, s_z, s_e, s_g, s_ga, s_gc = (small(2) for _ in range(8))
        rsums = small(KC * CHUNKS)
        fb = small(8)
        a_hid, m_hid, ang, sin_c, cos_c, mod = small(1), small(1), small(2), small(2), small(2), small(2)
        mz = small(2)
        U, V_ = small(18), small(18)
        BX, AY = small(54), small(54)
        kmax, cmax, knew, kneg, kdif, kalpha, ksum, esum = (small(KH) for _ in range(8))
        qmax, qsum = small(32), small(32)
        pooled = small(2)
        o_mv, o_sd, o_rs = small(4), small(2), small(1)
        e_mv, e_ms, e_gm = small(8), small(8), small(8)
        e_sq, e_var, e_sd, e_s, e_t, e_s1 = (small(SETS) for _ in range(6))
        o_bn = small(2 * KC)
        obn4 = small(2 * SETS)
        assert used[0] <= 496, used[0]

        coef = cb[:, 0:KC * K2 * K2]

        ych = [cb[:, h * 1024:(h + 1) * 1024] for h in range(2)]
        xpt = [cb[:, (2 + h) * 1024:(3 + h) * 1024] for h in range(2)]
        dwacc = [img1[:, TILES * 3 * PTS + h * CHUNK:TILES * 3 * PTS + (h + 1) * CHUNK] for h in range(2)]
        i2 = [img2[:, j * 1024:(j + 1) * 1024] for j in range(9)]

        def seg(t, start, n):
            return t[:, bass.ds(start, n)]

        def chunk_of(t, k, c):
            return seg(t, c * CHUNK + k * HW, CHUNK)

        def padded(k, c, dy, dx):
            return seg(img2, c * (ROWS * YPITCH) + (k * YPLANE + dy * YPITCH + dx), ROWS * YPITCH)\
                .rearrange("p (r x) -> p r x", x=YPITCH)[:, :, 0:W]

        x3 = [ring[:].rearrange("p g c -> p (g c)")[:, 0:KC * HW], img1[:]]
        SIZES = (PH_SIZE, PW_SIZE, PX_SIZE)
        FIRST = [sum(SIZES[:f]) for f in range(4)]
        padf = [img2[:, FIRST[f]:FIRST[f + 1]] for f in range(3)]
        hold = [[wb_sb[:, FIRST[f]:FIRST[f + 1]] for f in range(3)],
                [wt[:, FIRST[f]:FIRST[f + 1]] for f in range(2)] + [img2[:, FIRST[3]:FIRST[3] + PX_SIZE]]]
        pads = [[(hold[j][f].bitcast(F16)[:, 0:SIZES[f]], hold[j][f].bitcast(F16)[:, SIZES[f]:2 * SIZES[f]])
                 for f in range(3)] for j in range(2)]
        ring_end = ring[:].rearrange("p g c -> p (g c)")[:, KC * HW:].bitcast(F16)
        wa_end = wa_sb[:, L3_TAPS * P:].bitcast(F16)
        nh, nw, nx = len(L3_TAPS_H) * P, len(L3_TAPS_W) * P, len(L3_TAPS_X) * P
        w_int = [ring_end[:, 0:nh], wa_end[:, 0:nw], ring_end[:, nh:nh + nx]]
        obuf = [cb[:, j * HALFP:(j + 1) * HALFP] for j in range(2)]
        PAD_FORM = ((PH_PITCH, 2, 0), (PW_PITCH, 0, 5), (PX_PITCH, 0, 1))

        def pair_rows(s, j, form, part, d, dx):
            pitch, top, left = PAD_FORM[form]
            return seg(pads[j][form][part], s * (PAIR_ROWS * pitch) + ((top + d) * pitch + left + dx), PAIR_ROWS * pitch)\
                .rearrange("p (r x) -> p r x", x=pitch)[:, :, 0:W]

        def interior(form, late=0):
            pitch, top, left = PAD_FORM[form]
            at = (top + late) * pitch + left
            return padf[form][:, at:at + H // 2 * pitch].rearrange("p (r x) -> p r x", x=pitch)[:, :, 0:W]

        def by_parity(ap):
            return ap.rearrange("p (two r x) -> p two r x", two=2, x=W)

        def from_rows(ap):
            return ap.rearrange("p (r two x) -> p two r x", two=2, x=W)

        def rows(ap):
            return ap.rearrange("p (r x) -> p r x", x=W)

        def wseg(region, a, n):
            return region[:, a:a + n]

        x_img = x.rearrange("b (k p) h w -> b p k (h w)", p=P)
        out_img = out.rearrange("b (k p) h w -> b p k (h w)", p=P)

        def done(eng, name, n):
            eng.wait_ge(sem(name), n + (START + 1))

        def room(eng, name, n):
            eng.wait_ge(sem(name), n + 1)

        two_deep = ["aZ", "aY", "aC", "aP", "aX", "aXE", "dZ", "dT", "dD", "dO", "dE",
                    "fT", "fC", "fO", "fR", "gH", "gZ", "gB", "gD", "gX", "lC", "lX",
                    "cKs", "cET", "cQC", "bP", "bO", "bS"]
        store_sems = [f"{name}{h}" for name in ("y_stored", "t_stored", "o_stored") for h in range(2)] \
            + ["d_stored", "q_stored"]
        block = ctx.enter_context(nc.Block())
        ENG = ("sp", "pe", "act", "dve")

        class Barrier:

            def __init__(self, eng, me):
                self.eng, self.me, self.n = eng, me, 0

            def __call__(self):
                self.n += 1
                if self.me == "sp":
                    self.eng.sem_inc(sem("sp_phase"), 1)
                else:
                    self.eng.drain().then_inc(sem(self.me + "_phase"), 1)
                for e in ENG:
                    if e != self.me:
                        self.eng.wait_ge(sem(e + "_phase"), self.n)

        plan = [("A", 0, None)] + [("A", b, 0) for b in range(1, B)] + [("REST", None, 0)]
        for k in range(1, B):
            plan += [("F", k - 1, k), ("L1", k - 1, k), ("L2", k - 1, k)] + [("REST", None, k)] * (k < B - 1)
        plan += [("F", B - 1, B - 1), ("L1", B - 1, None), ("L2", B - 1, None), ("L3", None, None)]
        TURNS = {"A1": 1, "A2": 1, "F1": 1, "F2": 2, "L1": 2, "L2a": 2, "L2b": 1,
                 "L1 last": 1}

        class Stream:

            def __init__(self, unit, turned=None):
                self.unit, self.turned, self.taken, self.left = unit, turned, {}, []

            def begin(self, part, gi, i):
                self.left = []
                if gi is not None:
                    n = TURNS[part]
                    self.left = [(gi, i * n + (self.taken.get(gi, 0) + j), g, j) for j in range(n) for g in range(G)]
                self.share = len(self.left)

            def give(self, part_of=1, whole=1):
                for _ in range(min(len(self.left), -(-self.share * part_of // whole))):
                    self.unit(*self.left.pop(0))

            def finish(self):
                while self.left:
                    self.unit(*self.left.pop(0))

            def ended(self, part, gi, turns=PAIRS):
                if gi is not None:
                    self.taken[gi] = self.taken.get(gi, 0) + TURNS[part] * turns

            def extra(self, gi, after=None):
                t = self.taken.get(gi, 0)
                for g in range(G):
                    self.unit(gi, t, g, 0)
                if after:
                    after(gi, t, 1)
                self.taken[gi] = t + 1

            def rest(self, eng, gi, after=None):
                first = self.taken.get(gi, 0)
                if first < TILES:
                    with eng.Fori(0, TILES - first) as i:
                        for g in range(G):
                            self.unit(gi, i + first, g, 0)
                        if after:
                            after(gi, i + first, 1)
                self.taken[gi] = TILES

        @block.gpsimd
        def _(pool):
            def unit(b, t, g, stage, at):
                pool.wait_ge(sem("ring_free"), t * G + (b * TILES * G + g + 1))
                pool.sem_inc(sem("unit_begun"), 1)
                for p in range(K2):
                    nc.gpsimd.indirect_dma_start(
                        out=ring[:, g, p * CORNERS * GC:(p + 1) * CORNERS * GC], out_offset=None,
                        in_=tab[b], in_offset=bass.IndirectOffsetOnAxis(
                            ap=idx_stage[:, stage, at + g * K2 + p:at + g * K2 + p + 1], axis=0),
                    ).then_inc(sem(f"gathered{g}"), 16)

            def quad(b, i, last):
                for stage in range(2):
                    pool.wait_ge(sem("idx_staged"), i * 2 + (b * TILES // 2 + stage + 1))
                    for h in range(2):
                        t = i * 4 + (2 * stage + h)
                        for g in range(G):
                            if h == 1 and g == G - 1 and not (last and stage == 1):
                                pool.wait_ge(sem("ring_free"), t * G + (b * TILES * G + g + 1))
                                nc.gpsimd.tensor_copy(idx_stage[:, 1 - stage, :], seg(idx[:, b % 2, :], t * PTS + PTS, 2 * PTS))\
                                    .then_inc(sem("idx_staged"), 1)
                            unit(b, t, g, stage, h * PTS)

            for b in range(B):
                pool.wait_ge(sem("idx_loaded"), 16 * (b + 1))
                nc.gpsimd.tensor_copy(idx_stage[:, 0, :], idx[:, b % 2, 0:2 * PTS]).then_inc(sem("idx_staged"), 1)
                with pool.Fori(0, TILES // 4 - 1) as i:
                    quad(b, i, False)
                quad(b, TILES // 4 - 1, True)

        @block.sync
        def _(sp):
            for name in two_deep:
                sp.sem_inc(sem(name), START)
            for name in ("cS", "cQT"):
                sp.sem_inc(sem(name), 1)
            sp.sem_inc(sem("ring_free"), G)
            barrier = Barrier(sp, "sp")
            loads = {"wa": 0, "wb": 0}

            def store_sums(b, first, n):
                for j in range(n):
                    t = first + j
                    sp.wait_ge(sem("ring_free"), t * G + ((b * TILES + 1) * G + G))
                    sp.dma_start(d_dram[b][bass.ds(t, 1)].rearrange("a p c -> (a p) c"), dbuf[:, j, :])\
                        .then_inc(sem("d_stored"), 16)

            stream = Stream(lambda *u: None)

            def load_indices(b):
                sp.dma_start(idx[:, b % 2, :], idx_dram[b]).then_inc(sem("idx_loaded"), 16)

            def load_weights(b):
                sp.dma_start(wt[:], w_dram[b]).then_inc(sem("wt_loaded"), 16)

            def load_pack(region, tile_, pack):
                loads[region] += 1
                sp.dma_start(tile_[:, 0:pack.shape[1]], pack).then_inc(sem(region + "_loaded"), 16)

            def chunks(part, gi, body, last_body=None, sums_first=False):
                def turn(i, run, streaming=True):
                    if not sums_first:
                        run(i)
                    if gi is not None and streaming:
                        store_sums(gi, i * TURNS[part] + stream.taken.get(gi, 0), TURNS[part])
                    if sums_first:
                        run(i)

                turns = PAIRS - 1 if last_body else PAIRS
                with sp.Fori(0, turns) as i:
                    turn(i, body)
                if last_body:
                    turn(turns, last_body, part != "L2b")
                stream.ended(part, gi, turns if part == "L2b" else PAIRS)

            def A(b, gi):
                if b == 0:
                    sp.dma_start(params[:], par).then_inc(sem("par_loaded"), 16)
                for k in range(KC):
                    sp.dma_start(img1[:, k * HW:(k + 1) * HW], x_img[b][:, k, :]).then_inc(sem(f"x_loaded{k}"), 16)
                load_pack("wa", wa_sb, wa)
                if b == B - 1:
                    load_pack("wb", wb_sb, wf)
                if gi is not None:
                    for _ in range(1 if b == B - 1 else 2):
                        stream.extra(gi, store_sums)
                if b == 0:
                    sp.wait_ge(sem("zeros"), 1)
                    pieces = [(t, first) for t in tab for first in (0, P // 2, HW, HW + P // 2)]
                    for (t, first), name in zip(pieces, store_sems + ["pads_stored"] * (len(pieces) - len(store_sems))):
                        sp.dma_start(t.rearrange("(r g) c -> r g c", g=G)[first:first + P // 2],
                                     dbuf[0:P // 2, 0, :].unsqueeze(1).to_broadcast([P // 2, G, C])).then_inc(sem(name), 16)
                    for name in store_sems:
                        sp.wait_ge(sem(name), 16)
                    sp.wait_ge(sem("pads_stored"), 16 * (len(pieces) - len(store_sems)))
                barrier()
                def body(i):
                    for h in range(2):
                        n, c = i * 2 + (b * CHUNKS + h), i * 2 + h
                        done(sp, "aY", n)
                        for k in range(KC):
                            sp.dma_start(y_dram[b][:, k, bass.ds(c * CHUNK, CHUNK)], ych[h][:, k * CHUNK:(k + 1) * CHUNK])\
                                .then_inc(sem(f"y_stored{h}"), 16)
                    for h in range(2):
                        n, c = i * 2 + (b * CHUNKS + h), i * 2 + h
                        done(sp, "aXE", n)
                        src = xpt[h].rearrange("p (q c) -> p q c", q=SUBS * G)
                        for j, back in enumerate((0, 1, W, W + 1)):
                            first = c * (CHUNK * G) + (TAB_FRONT - back) * G
                            sp.dma_start(tab[b][bass.ds(first, CHUNK * G), :].rearrange("(p q) c -> p q c", q=SUBS * G)
                                         [:, :, j * GC:(j + 1) * GC], src).then_inc(sem(f"t_stored{h}"), 16)
                chunks("A1", gi, body)
                barrier()
                chunks("A2", gi, lambda i: None)
                for h in range(2):
                    sp.wait_ge(sem(f"y_stored{h}"), 16 * KC * PAIRS * (b + 1) + 16)
                    sp.wait_ge(sem(f"t_stored{h}"), 16 * CORNERS * PAIRS * (b + 1) + 16)
                barrier()
                if b == 0:
                    barrier()
                    return
                sp.wait_ge(sem("idx_made"), b + 1)
                sp.wait_ge(sem("w_made"), b + 1)
                sp.dma_start(w_dram[b], img2[:, 0:TILES * PTS * CORNERS]).then_inc(sem("w_stored"), 16)
                sp.dma_start(idx_dram[b], img1[:, 0:TILES * PTS].bitcast(U32)).then_inc(sem("w_stored"), 16)
                sp.wait_ge(sem("w_stored"), 32 * b)
                if b == 1:
                    load_indices(b)
                if gi is not None:
                    stream.extra(gi, store_sums)
                barrier()

            def F(b, gi):
                load_pack("wa", wa_sb, wr)
                if b == B - 1:
                    load_pack("wb", wb_sb, wf)

                def f1(i):
                    for h in range(2):
                        n, c = i * 2 + (b * CHUNKS + h), i * 2 + h
                        room(sp, "fT", n)
                        sp.dma_start(i2[h].rearrange("p (s c) -> p s c", s=SUBS),
                                     d_dram[b][bass.ds(c * SUBS, SUBS)].rearrange("s p c -> p s c"))\
                            .then_inc(sem(f"fD{h}"), 16)
                        room(sp, "fR", n)
                        sp.dma_start(i2[2 + h].rearrange("p (k n) -> p k n", k=KC), y_dram[b][:, :, bass.ds(c * CHUNK, CHUNK)])\
                            .then_inc(sem(f"fY{h}"), 16)

                def f1_last(i):
                    sp.wait_ge(sem("d_stored"), 16 * B * TILES + 16)
                    f1(i)

                if b < B - 1:
                    chunks("F1", gi, f1)
                else:
                    assert stream.taken[gi] == TILES - PAIRS
                    sp.wait_ge(sem("d_stored"), 16 * (B * TILES - PAIRS) + 16)
                    chunks("F1", gi, f1, f1_last, sums_first=True)
                    gi = None
                barrier()
                barrier()

                def f2(i):
                    for h in range(2):
                        n, c = i * 2 + (b * CHUNKS + h), i * 2 + h
                        room(sp, "gX", n)
                        sp.dma_start(i2[h].rearrange("p (k n) -> p k n", k=KC), y_dram[b][:, :, bass.ds(c * CHUNK, CHUNK)])\
                            .then_inc(sem(f"gYl{h}"), 16)
                        sp.dma_start(i2[2 + h].rearrange("p (k n) -> p k n", k=KC), x_img[b][:, :, bass.ds(c * CHUNK, CHUNK)])\
                            .then_inc(sem(f"gXl{h}"), 16)
                chunks("F2", gi, f2)
                barrier()

            def L1(b, gi):
                load_pack("wb", wb_sb, wq)
                if gi is not None:
                    stream.extra(gi, store_sums)
                barrier()
                chunks("L1" if gi != B - 1 else "L1 last", gi, lambda i: None)
                barrier()

            def L2(b, gi):
                barrier()
                if b == B - 1:
                    load_pack("wa", wa_sb, w3)
                    load_x(0)

                def a(i):
                    for h in range(2):
                        n, c = i * 2 + (b * CHUNKS + h), i * 2 + h
                        sp.wait_ge(sem("cQC"), n * 2 + 4)
                        sp.dma_start(q_dram[b][:, bass.ds(c, 1)].rearrange("p a m n -> p (a m n)"), img2[:, 6144:8192])\
                            .then_inc(sem("q_stored"), 16)
                chunks("L2a", gi, a)
                sp.wait_ge(sem("q_stored"), 16 * CHUNKS * (b + 1) + 16)
                barrier()
                barrier()

                def load_queries(c, h):
                    sp.dma_start(img2[:, h * 2048:(h + 1) * 2048], q_dram[b][:, bass.ds(c, 1)].rearrange("p a m n -> p (a m n)"))\
                        .then_inc(sem(f"q_loaded{h}"), 16)

                def o(i, last_pair=False):
                    for h in range(2):
                        n, c = i * 2 + (b * CHUNKS + h), i * 2 + h
                        if not last_pair:
                            done(sp, "bP", n)
                            load_queries(c + 2, h)
                        done(sp, "bO", n)
                        for store, src in ((x2_dram, i2[6 + h]), (o_dram, i2[4 + h])):
                            sp.dma_start(store[b].rearrange("p k two n -> p (k two) n")
                                         [:, :, bass.ds(c * (CHUNK // 2), CHUNK // 2)],
                                         src.rearrange("p (a n) -> p a n", a=KC * 2)).then_inc(sem(f"o_stored{h}"), 16)
                load_queries(0, 0)
                load_queries(1, 1)
                if b == B - 1:
                    load_o(0, (0, 1))
                chunks("L2b", gi, o, lambda i: o(i, True))
                for h in range(2):
                    sp.wait_ge(sem(f"o_stored{h}"), 32 * PAIRS * (b + 1) + 16)
                barrier()

            def set_of(store, b, q):
                return store[b].rearrange("(j c) k two n -> k j two c n", j=2)[q // 2][q % 2]

            def load_x(b, sets=range(SETS)):
                for q in sets:
                    sp.dma_start(x3[b % 2][:, q * HALFP:(q + 1) * HALFP], set_of(x2_dram, b, q))\
                        .then_inc(sem(f"e_x{b % 2}{q}"), 16)

            def load_o(b, sets=range(SETS)):
                for q in sets:
                    if b * SETS + q >= 2:
                        sp.wait_ge(sem("eA"), b * SETS + q - 1)
                    sp.dma_start(obuf[q % 2], set_of(o_dram, b, q)).then_inc(sem(f"e_o{q % 2}"), 16)

            def L3():
                sp.wait_ge(sem("o_bn_ready"), 1)
                for par in range(2):
                    for j in range(2):
                        sp.dma_start(obn4[par * SC:(par + 1) * SC, :].rearrange("p (s j k) -> p j s k", k=KC, j=2)[:, j],
                                     o_bn[j * SC:(j + 1) * SC, :].rearrange("p (s k) -> p s k", k=KC))\
                            .then_inc(sem("o_bn_moved"), 16)
                load_x(1)
                load_o(0, (2, 3))
                if B > 1:
                    load_o(1, (0, 1))

                def store(b, q, first, n):
                    for par in range(2):
                        dst = out[b][q * SC:(q + 1) * SC].rearrange("c (r two) x -> two c r x", two=2)[par]
                        src = x3[b % 2][par * SC:(par + 1) * SC, q * HALFP + first * W:q * HALFP + (first + n) * W]
                        sp.dma_start(dst[:, first:first + n, :], rows(src)).then_inc(sem(f"out_stored{q}"), 16)

                def reload(b, q):
                    sp.wait_ge(sem(f"out_stored{q}"), (b + 1) * (32 if q == 0 else 64))
                    if b + 2 < B:
                        load_x(b + 2, (q,))

                for b in range(B):
                    sp.wait_ge(sem("eI"), b + 1)
                    store(b, 0, 0, H // 2)
                    for form in range(3):
                        if b + 1 < B and form < 2:
                            load_o(b + 1, (form + 2,))
                        sp.wait_ge(sem("eX"), b * 12 + form * 2 + 2)
                        store(b, form + 1, 0, 2 * PAIR_ROWS)
                    reload(b, 0)
                    for form in range(3):
                        sp.wait_ge(sem("eX"), b * 12 + form * 2 + 8)
                        store(b, form + 1, 2 * PAIR_ROWS, 2 * PAIR_ROWS)
                        if form == 0 and b + 2 < B:
                            load_o(b + 2, (0, 1))
                        if form:
                            reload(b, form)
                    reload(b, 3)
                barrier()

            for phase, b, gi in plan:
                if phase == "REST":
                    if gi:
                        load_pack("wb", wb_sb, wf)
                    stream.rest(sp, gi, store_sums)
                    sp.wait_ge(sem("d_stored"), 16 * TILES * (gi + 1) + 16)
                    if gi + 1 < B:
                        load_weights(gi + 1)
                    if gi + 2 < B:
                        load_indices(gi + 2)
                    barrier()
                elif phase == "L3":
                    L3()
                else:
                    {"A": A, "F": F, "L1": L1, "L2": L2}[phase](b, gi)

        @block.tensor
        def _(pe):
            barrier = Barrier(pe, "pe")
            count = {"wa": 0, "wb": 0, "gn": 0}

            def mm(o, l, r, start, stop, **kw):
                return nc.tensor.matmul(o, l, r, start=start, stop=stop, **kw)

            def loaded(region):
                count[region] += 1
                pe.wait_ge(sem(region + "_loaded"), 16 * count[region])

            def group_average():
                count["gn"] += 1
                pe.wait_ge(sem("gn_moments"), count["gn"])
                mm(PS[:, 7, 0:4], v("gavg"), ms, True, True).then_inc(sem("gn_grouped"), 1)

            def loop(body):
                with pe.Fori(0, PAIRS) as i:
                    body(i)

            def A(b):
                loaded("wa")
                conv = wseg(wa_sb, A_CONV, 512)
                inp, om = wseg(wa_sb, A_INP, 512), wseg(wa_sb, A_OM, 6 * PTS)
                if b == 0:
                    pe.wait_ge(sem("par_loaded"), 16)
                group_average()
                pe.wait_ge(sem("gn_ready"), count["gn"])
                for oc in range(KC):
                    for k in range(KC):
                        last = mm(PS[:, 6, oc:oc + 1], conv[:, k * C + oc * P:k * C + (oc + 1) * P], gn_t[:, k:k + 1],
                                  k == 0, k == KC - 1)
                last.then_inc(sem("a_bias"), 1)
                barrier()

                def a1(i):
                    for h in range(2):
                        n, c = i * 2 + (b * CHUNKS + h), i * 2 + h
                        room(pe, "aZ", n)
                        for oc in range(KC):
                            for k in range(KC):
                                last = mm(PS[:, 2 * h + oc, :], conv[:, k * C + oc * P:k * C + (oc + 1) * P],
                                          chunk_of(img1, k, c), k == 0, k == KC - 1)
                        last.then_inc(sem("aC"), 1)
                    for h in range(2):
                        n = i * 2 + (b * CHUNKS + h)
                        done(pe, "aY", n)
                        room(pe, "aXE", n)
                        for s in range(SUBS):
                            for k in range(KC):
                                last = mm(PS[:, 4 + 2 * h + s // 2, (s % 2) * C:(s % 2 + 1) * C],
                                          ych[h][:, k * CHUNK:(k + 1) * CHUNK].rearrange("p (x s) -> p s x", s=SUBS)[:, s, :],
                                          inp[:, k * C:(k + 1) * C],
                                          k == 0, k == KC - 1)
                        last.then_inc(sem("aX"), 1)
                loop(a1)
                barrier()

                def depthwise(c, h):
                    for tap in range(K2):
                        last = mm(rows(PS[:, 2 * h, :]), wseg(wa_sb, A_DW + tap * P, P),
                                  padded(0, c, tap // 3, tap % 3), tap == 0, tap == K2 - 1)
                    last.then_inc(sem("dD"), 1)

                def a2(i, last_pair=False):
                    for h in range(2):
                        n, c = i * 2 + (b * CHUNKS + h), i * 2 + h
                        if not last_pair:
                            done(pe, "dZ", n)
                            depthwise(c + 2, h)
                        done(pe, "dT", n)
                        room(pe, "dE", n)
                        for s in range(SUBS):
                            for k in range(KC):
                                last = mm(PS[:, 4 + h, s * 3 * PTS:(s + 1) * 3 * PTS],
                                          ych[h][:, k * CHUNK + s * P:k * CHUNK + (s + 1) * P],
                                          om[:, k * 3 * PTS:(k + 1) * 3 * PTS], k == 0, k == KC - 1)
                        last.then_inc(sem("dO"), 1)
                for h in range(2):
                    depthwise(h, h)
                with pe.Fori(0, PAIRS - 1) as i:
                    a2(i)
                a2(PAIRS - 1, True)
                barrier()
                barrier()

            def F(b):
                loaded("wb")
                outp, fc1, fc2 = wseg(wb_sb, F_OUT, 512), wseg(wb_sb, F_FC1, KC * 4 * C), wseg(wb_sb, F_FC2, FC * C)

                def f1(i):
                    for h in range(2):
                        n, m = i * 2 + (b * CHUNKS + h), i + b * PAIRS
                        pe.wait_ge(sem(f"fD{h}"), m * 16 + 16)
                        room(pe, "fC", n)
                        for k in range(KC):
                            for s in range(SUBS):
                                last = nc.tensor.transpose(PS[:, 2 * h + k, s * P:(s + 1) * P],
                                                           i2[h][:, s * C + k * P:s * C + (k + 1) * P], v("ident"))
                        last.then_inc(sem("fT"), 1)
                    for h in range(2):
                        n = i * 2 + (b * CHUNKS + h)
                        done(pe, "fC", n)
                        room(pe, "fR", n)
                        for oc in range(KC):
                            for k in range(KC):
                                last = mm(PS[:, 4 + 2 * h + oc, :], outp[:, k * C + oc * P:k * C + (oc + 1) * P],
                                          i2[4 + h][:, k * CHUNK:(k + 1) * CHUNK], k == 0, k == KC - 1)
                        last.then_inc(sem("fO"), 1)
                loop(f1)
                barrier()
                pe.wait_ge(sem("se_mean"), b + 1)
                for k in range(KC):
                    last = mm(PS[0:64, 7, 0:1], wseg(wb_sb, F_DOWN, KC * 64)[:, k * 64:(k + 1) * 64], xmean[:, k:k + 1],
                              k == 0, k == KC - 1)
                last.then_inc(sem("se_down"), 1)
                pe.wait_ge(sem("se_hidden"), b + 1)
                for oc in range(KC):
                    last = mm(PS[:, 6, oc:oc + 1], wb_sb[0:64, F_UP + oc * P:F_UP + (oc + 1) * P], s_hid[0:64, 0:1], True, True)
                last.then_inc(sem("se_up"), 1)
                pe.wait_ge(sem("se_gate"), b + 1)
                for hc in range(FC):
                    for k in range(KC):
                        last = mm(PS[:, 5, hc:hc + 1], fc1[:, k * 4 * C + hc * P:k * 4 * C + (hc + 1) * P], s_gc[:, k:k + 1],
                                  k == 0, k == KC - 1)
                last.then_inc(sem("fc1_shift"), 1)
                barrier()

                def f2(i):
                    for h in range(2):
                        n, c = i * 2 + (b * CHUNKS + h), i * 2 + h

                        def up(q):
                            room(pe, "gZ", n * 4 + q)
                            for j in range(2):
                                for k in range(KC):
                                    at = k * 4 * C + (2 * q + j) * P
                                    last = mm(PS[:, 2 * (q % 2) + j, :], fc1[:, at:at + P], chunk_of(img1, k, c),
                                              k == 0, k == KC - 1)
                            last.then_inc(sem("gH"), 1)

                        def down(q):
                            done(pe, "gB", n * 4 + q)
                            if q == 0:
                                room(pe, "gX", n)
                            hb = i2[6 + q % 2]
                            for j in range(2):
                                for oc in range(KC):
                                    at = (2 * q + j) * C + oc * P
                                    last = mm(PS[:, 4 + 2 * h + oc, :], fc2[:, at:at + P], hb[:, j * CHUNK:(j + 1) * CHUNK],
                                              q == 0 and j == 0, q == 3 and j == 1)
                            last.then_inc(sem("gD"), 1)

                        up(0)
                        up(1)
                        down(0)
                        up(2)
                        down(1)
                        up(3)
                        down(2)
                        down(3)
                loop(f2)
                barrier()

            def L1(b):
                loaded("wa")
                group_average()
                pe.wait_ge(sem("pooled"), b + 1)
                for j, at in enumerate((R_AP1, R_ME1)):
                    for k in range(KC):
                        last = mm(PS[0:64, 6, j:j + 1], wa_sb[:, at + k * 64:at + (k + 1) * 64], pooled[:, k:k + 1],
                                  k == 0, k == KC - 1)
                last.then_inc(sem("l1_hidden"), 1)
                pe.wait_ge(sem("l1_relu"), b + 1)
                for j, (at, hid) in enumerate(((R_AP2, a_hid), (R_ME2, m_hid))):
                    for oc in range(KC):
                        last = mm(PS[:, 5, 2 * j + oc:2 * j + oc + 1], wa_sb[0:64, at + oc * P:at + (oc + 1) * P], hid[0:64, :],
                                  True, True)
                last.then_inc(sem("l1_heads"), 1)
                barrier()

                def l1(i):
                    for h in range(2):
                        n, c = i * 2 + (b * CHUNKS + h), i * 2 + h
                        room(pe, "lX", n)
                        for k in range(KC):
                            for tap in range(K2):
                                at = R_SIZE + (k * K2 + tap) * P
                                last = mm(PS[:, 2 * h + k, :].rearrange("p (r x) -> p r x", x=W), wseg(wa_sb, at, P),
                                          padded(k, c, tap // 3, tap % 3), tap == 0, tap == K2 - 1)
                        last.then_inc(sem("lC"), 1)
                loop(l1)
                barrier()

            def L2(b):
                loaded("wb")
                group_average()
                barrier()
                wq_, wk_ = wseg(wb_sb, Q_Q, KC * HID), wseg(wb_sb, Q_K, KC * HID)
                wv_, wo_ = wseg(wb_sb, Q_V, KC * HID), wseg(wb_sb, Q_O, KH * C)
                kx = wseg(wb_sb, Q_SIZE, 1024)
                kxt, bd, mt = wseg(wb_sb, Q_SIZE + 1024, 1024), wseg(wb_sb, Q_SIZE + 3072, 512), wseg(wb_sb, Q_SIZE + 2048, 1024)
                E_, QS = img2[:, 2048:4096], img2[:, 4096:6144]

                def keys(n, h, first=False):
                    pe.wait_ge(sem("cXN"), n + 1)
                    if not first:
                        pe.wait_ge(sem("cQs"), n * 2)
                    for half in range(2):
                        for m in (2 * half, 2 * half + 1):
                            for k in range(KC):
                                last = mm(PS[:, m, :], wk_[:, k * HID + m * P:k * HID + (m + 1) * P],
                                          i2[h][:, k * CHUNK:(k + 1) * CHUNK], k == 0, k == KC - 1)
                        last.then_inc(sem("cK"), 1)

                def la(i, last_pair=False):
                    for h in range(2):
                        n = i * 2 + (b * CHUNKS + h)
                        xn = i2[h]
                        final = last_pair and h == 1
                        pe.wait_ge(sem("cE"), n * 2 + 1)
                        pe.wait_ge(sem("cQC"), n * 2 + 1)
                        for s in range(SUBS):
                            for k in range(KC):
                                last = nc.tensor.transpose(PS[:, s // 2, (s % 2) * C + k * P:(s % 2) * C + (k + 1) * P],
                                                           xn[:, k * CHUNK + s * P:k * CHUNK + (s + 1) * P], v("ident"))
                        last.then_inc(sem("cX"), 1)
                        for half in range(2):
                            if half == 0:
                                pe.wait_ge(sem("cE"), n * 2 + 2)
                                pe.wait_ge(sem("cQC"), n * 2 + 2)
                            else:
                                pe.wait_ge(sem("cXT"), n + 1)
                            for s in (2 * half, 2 * half + 1):
                                for k in range(KC):
                                    last = mm(PS[:, (s + 2) % 4, :], xn[:, k * CHUNK + s * P:k * CHUNK + (s + 1) * P],
                                              wq_[:, k * HID:(k + 1) * HID], k == 0, k == KC - 1)
                            last.then_inc(sem("cQ"), 1)

                        def turn_(s):
                            pe.wait_ge(sem("cET"), n * 4 + (s + 1))
                            for m in range(KH):
                                last = nc.tensor.transpose(PS[:, 6 + s % 2, m * P:(m + 1) * P],
                                                           E_[:, m * CHUNK + s * P:m * CHUNK + (s + 1) * P], v("ident"))
                            last.then_inc(sem("cTT"), 1)

                        def product(s):
                            done(pe, "cET", n * 4 + s)
                            if s == 0:
                                pe.wait_ge(sem("cS"), n + 1)
                            et = i2[8][:, (s % 2) * 512:(s % 2 + 1) * 512]
                            for m in range(KH):
                                last = mm(PS[:, 4 + m // 2, (m % 2) * C:(m % 2 + 1) * C], et[:, m * P:(m + 1) * P],
                                          cb[:, s * C:(s + 1) * C],
                                          s == 0 and m % 2 == 0, s == SUBS - 1, skip_group_check=True)
                            last.then_inc(sem("cKs"), 1)

                        turn_(0)
                        for s in range(SUBS):
                            if s + 1 < SUBS:
                                turn_(s + 1)
                            product(s)
                        if not final:
                            keys(n + 1, 1 - h)
                        pe.wait_ge(sem("cQn"), n + 1)
                        for half in range(2):
                            if not final:
                                pe.wait_ge(sem("cE"), n * 2 + (3 + half))
                            for m in (2 * half, 2 * half + 1):
                                for s in range(SUBS):
                                    last = nc.tensor.transpose(PS[:, m, s * P:(s + 1) * P],
                                                               QS[:, s * HID + m * P:s * HID + (m + 1) * P], v("ident"))
                            last.then_inc(sem("cQT"), 1)
                keys(b * CHUNKS, 0, first=True)
                with pe.Fori(0, PAIRS - 1) as i:
                    la(i)
                la(PAIRS - 1, True)
                barrier()
                pe.wait_ge(sem("kx_scaled"), b + 1)
                for k in range(KC):
                    for m in range(KH):
                        last = nc.tensor.transpose(PS[:, k, m * P:(m + 1) * P], kx[:, m * C + k * P:m * C + (k + 1) * P],
                                                   v("ident"))
                last.then_inc(sem("kx_turned"), 1)
                pe.wait_ge(sem("kxt_ready"), b + 1)
                for m in range(KH):
                    for k in range(KC):
                        last = mm(PS[:, 2, m * P:(m + 1) * P], wv_[:, k * HID + m * P:k * HID + (m + 1) * P],
                                  kxt[:, k * HID + m * P:k * HID + (m + 1) * P], k == 0, k == KC - 1)
                last.then_inc(sem("ctx_ready"), 1)
                pe.wait_ge(sem("ctx_diagonal"), b + 1)
                for m in range(KH):
                    last = mm(PS[:, 3 + m // 2, (m % 2) * C:(m % 2 + 1) * C], bd[:, m * P:(m + 1) * P],
                              wo_[:, m * C:(m + 1) * C], True, True)
                last.then_inc(sem("mt_ready"), 1)
                barrier()

                def lb(i):
                    for h in range(2):
                        n, m_ = i * 2 + (b * CHUNKS + h), i + b * PAIRS
                        pe.wait_ge(sem(f"q_loaded{h}"), m_ * 16 + 16)
                        room(pe, "bO", n)
                        for oc in range(KC):
                            for m in range(KH):
                                last = mm(PS[:, 2 * h + oc, :], mt[:, m * C + oc * P:m * C + (oc + 1) * P],
                                          img2[:, h * 2048 + m * CHUNK:h * 2048 + (m + 1) * CHUNK], m == 0, m == KH - 1)
                        last.then_inc(sem("bP"), 1)
                loop(lb)
                barrier()

            def L3():
                flat = PS[:].rearrange("p a n -> p (a n)")

                def average(b):
                    pe.wait_ge(sem("e_moments"), b + 1)
                    mm(PS[:, 7, 0:2 * SETS], v("gavg2"), e_ms, True, True).then_inc(sem("e_grouped"), 1)

                def convolve(b, half, form):
                    if half == 0:
                        pe.wait_ge(sem("eN"), b * 3 + form + 1)
                    taps = (L3_TAPS_H, L3_TAPS_W, L3_TAPS_X)[form]
                    with pe.Fori(0, 2) as i:
                        if b or half:
                            pe.wait_ge(sem("eX"), i + (b * 12 + half * 6 + form * 2 - 5))
                        dst = rows(seg(flat, i * CHUNK + form * 2 * CHUNK, CHUNK))
                        for part in range(2):
                            for j, (d, dx) in enumerate(taps):
                                last = mm(dst, w_int[form][:, j * P:(j + 1) * P], pair_rows(i + half * 2, b % 2, form, part, d, dx),
                                          part == 0 and j == 0, part == 1 and j == len(taps) - 1)
                        last.then_inc(sem("eC"), 1)

                average(0)
                for b in range(B):
                    for form in range(3):
                        convolve(b, 0, form)
                    convolve(b, 1, 0)
                    if b + 1 < B:
                        average(b + 1)
                    convolve(b, 1, 1)
                    convolve(b, 1, 2)
                barrier()

            for phase, b, gi in plan:
                if phase == "REST":
                    barrier()
                elif phase == "L3":
                    L3()
                else:
                    {"A": A, "F": F, "L1": L1, "L2": L2}[phase](b)

        @block.scalar
        def _(act):
            barrier = Barrier(act, "act")
            count = {"gn": 0}

            def A_(o, i, f, **kw):
                return nc.scalar.activation(o, i, f, **kw)

            def loop(func, body):
                nc.scalar.preload_act_table(func)
                with act.Fori(0, PAIRS) as i:
                    body(i)

            def deviation():
                count["gn"] += 1
                act.wait_ge(sem("gn_var"), count["gn"])
                A_(gsd, gvar, ACT.Sqrt, bias=eps_c).then_inc(sem("gn_sd"), 1)

            def A(b):
                if b == 0:
                    act.wait_ge(sem("bn_var"), 1)
                    A_(bnv, bnv, ACT.Sqrt, bias=eps_c).then_inc(sem("bn_sd"), 1)
                deviation()
                barrier()

                def a1(i):
                    for h in range(2):
                        n = i * 2 + (b * CHUNKS + h)
                        m = i + b * PAIRS
                        done(act, "aC", n)
                        room(act, "aX", n)
                        room(act, "aP", n)
                        act.wait_ge(sem(f"y_stored{h}"), m * (16 * KC) + 16)
                        for oc in range(KC):
                            last = A_(ych[h][:, oc * CHUNK:(oc + 1) * CHUNK], PS[:, 2 * h + oc, :], ACT.Identity,
                                      bias=cb1[:, oc:oc + 1], scale=bninv[:, oc:oc + 1])
                        last.then_inc(sem("aZ"), 1)
                    for h in range(2):
                        n, c = i * 2 + (b * CHUNKS + h), i * 2 + h
                        done(act, "aY", n)
                        for k in range(KC):
                            last = A_(padded(k, c, 1, 1), rows(ych[h][:, k * CHUNK:(k + 1) * CHUNK]), ACT.Copy)
                        last.then_inc(sem("aP"), 1)
                loop(ACT.Identity, a1)
                barrier()

                for h in range(2):
                    act.wait_ge(sem(f"y_stored{h}"), 16 * KC * PAIRS * (b + 1) + 16)

                def a2(i):
                    for h in range(2):
                        n = i * 2 + (b * CHUNKS + h)
                        done(act, "dD", n)
                        room(act, "dO", n)
                        A_(ych[h][:, 0:CHUNK], PS[:, 2 * h, :], ACT.Identity, bias=bnsh[:, 2:3], scale=bninv[:, 2:3])
                        act.wait_ge(sem("dW"), i + (b * PAIRS + 1))
                        A_(ych[h][:, CHUNK:], dwacc[h], ACT.Identity, bias=bnsh[:, 3:4], scale=bninv[:, 3:4])\
                            .then_inc(sem("dZ"), 1)
                loop(ACT.Identity, a2)
                barrier()
                T = lambda j: img1[:, 3456 + j * 1152:3456 + (j + 1) * 1152] if j < 4 else \
                    img2[:, 4608 + (j - 4) * 1152:4608 + (j - 3) * 1152]
                act.wait_ge(sem("dx_dy"), b + 1)
                A_(T(2), T(0), ACT.Abs, bias=neg_one)
                A_(T(3), T(1), ACT.Abs, bias=neg_one)
                A_(T(0), T(0), ACT.Abs)
                A_(T(1), T(1), ACT.Abs).then_inc(sem("act_own"), 1)
                act.wait_ge(sem("act_own"), b * 1 + 1)
                for j in (0, 1, 2, 3):
                    last = A_(T(j), T(j), ACT.Relu, bias=one_c, scale=-1.0)
                last.then_inc(sem("hats"), 1)
                act.wait_ge(sem("logit_less"), b + 1)
                A_(T(6), T(6), ACT.Exp).then_inc(sem("mask_exp"), 1)
                barrier()

            def F(b):
                def f1(i):
                    for h in range(2):
                        n = i * 2 + (b * CHUNKS + h)
                        done(act, "fT", n)
                        room(act, "fO", n)
                        A_(i2[4 + h], PS[:, 2 * h:2 * h + 2, :].rearrange("p k n -> p (k n)"), ACT.Copy)\
                            .then_inc(sem("fC"), 1)
                    for h in range(2):
                        n, c = i * 2 + (b * CHUNKS + h), i * 2 + h
                        done(act, "fR", n)
                        for k in range(KC):
                            A_(chunk_of(img1, k, c), chunk_of(img1, k, c), ACT.Identity,
                               accum_out=seg(rsums, c + k * CHUNKS, 1))
                loop(ACT.Identity, f1)
                barrier()
                act.wait_ge(sem("se_z"), b + 1)
                A_(s_e, s_z, ACT.Exp, scale=-1.0).then_inc(sem("se_exp"), 1)
                barrier()

                def f2(i):
                    for h in range(2):
                        n = i * 2 + (b * CHUNKS + h)
                        for q in range(4):
                            done(act, "gH", n * 4 + q)
                            room(act, "gB", n * 4 + q)
                            for j in range(2):
                                last = A_(i2[4 + q % 2][:, j * CHUNK:(j + 1) * CHUNK], PS[:, 2 * (q % 2) + j, :], ACT.Identity,
                                          bias=fb[:, 2 * q + j:2 * q + j + 1])
                            last.then_inc(sem("gZ"), 1)
                loop(ACT.Identity, f2)
                barrier()

            def L1(b):
                deviation()
                act.wait_ge(sem("l1_z"), b + 1)
                A_(ang, ang, ACT.Tanh)
                A_(mz, mz, ACT.Exp, scale=-1.0).then_inc(sem("l1_tanh"), 1)
                act.wait_ge(sem("l1_angle"), b + 1)
                A_(sin_c, ang, ACT.Sin)
                A_(cos_c, cos_c, ACT.Sin).then_inc(sem("l1_sincos"), 1)
                act.wait_ge(sem("l1_uv"), b + 1)
                for src, dst in ((U, BX), (V_, AY)):
                    A_(dst[:, 0:18], src, ACT.Relu, scale=-1.0)
                    A_(dst[:, 36:54], src, ACT.Relu)
                    last = A_(dst[:, 18:36], src, ACT.Abs)
                last.then_inc(sem("l1_hats"), 1)
                act.wait_ge(sem("gn_ready"), count["gn"])
                for k in range(KC):
                    last = A_(img2[:, k * YPLANE:(k + 1) * YPLANE].rearrange("p (r x) -> p r x", x=YPITCH)[:, 1:H + 1, 1:W + 1],
                              rows(img1[:, k * HW:(k + 1) * HW]), ACT.Identity, bias=gn_t[:, k:k + 1], scale=gn_s[:, k:k + 1])
                barrier()
                barrier()

            def L2(b):
                deviation()
                barrier()
                E_, QS, QC = img2[:, 2048:4096], img2[:, 4096:6144], img2[:, 6144:8192]

                def normalised(c, h):
                    for k in range(KC):
                        last = A_(i2[h][:, k * CHUNK:(k + 1) * CHUNK], chunk_of(img1, k, c), ACT.Identity,
                                  bias=gn_t[:, k:k + 1], scale=gn_s[:, k:k + 1])
                    last.then_inc(sem("cXN"), 1)

                def exponentials(n):
                    act.wait_ge(sem("cS"), n + 1)
                    for half in range(2):
                        act.wait_ge(sem("cM"), n * 2 + (1 + half))
                        A_(kalpha[:, 2 * half:2 * half + 2], kdif[:, 2 * half:2 * half + 2], ACT.Exp)
                        for m in (2 * half, 2 * half + 1):
                            last = A_(E_[:, m * CHUNK:(m + 1) * CHUNK], PS[:, m, :], ACT.Exp, bias=kneg[:, m:m + 1],
                                      accum_out=esum[:, m:m + 1])
                        last.then_inc(sem("cE"), 1)

                def la(i, last_pair=False):
                    for h in range(2):
                        n, c = i * 2 + (b * CHUNKS + h), i * 2 + h
                        act.wait_ge(sem("cX"), n + 1)
                        A_(cb[:, 0:SUBS * C], PS[:, 0:2, :].rearrange("p a n -> p (a n)"), ACT.Copy).then_inc(sem("cXT"), 1)
                        for s in range(SUBS):
                            act.wait_ge(sem("cTT"), n * 4 + (s + 1))
                            room(act, "cKs", n * 4 + s)
                            A_(i2[8][:, (s % 2) * 512:(s % 2 + 1) * 512], PS[:, 6 + s % 2, :], ACT.Copy).then_inc(sem("cET"), 1)
                            if s < 2:
                                act.wait_ge(sem("cQs"), n * 2 + (1 + s))
                                A_(QS[:, s * 1024:(s + 1) * 1024], QS[:, s * 1024:(s + 1) * 1024], ACT.Exp).then_inc(sem("cQe"), 1)
                        if not last_pair:
                            normalised(c + 2, h)
                        if not (last_pair and h == 1):
                            exponentials(n + 1)
                        act.wait_ge(sem("q_stored"), n * 16 + 16)
                        for half in range(2):
                            act.wait_ge(sem("cQT"), n * 2 + (2 + half))
                            A_(QC[:, half * 1024:(half + 1) * 1024], PS[:, 2 * half:2 * half + 2, :].rearrange("p m n -> p (m n)"),
                               ACT.Copy).then_inc(sem("cQC"), 1)
                nc.scalar.preload_act_table(ACT.Exp)
                normalised(0, 0)
                normalised(1, 1)
                exponentials(b * CHUNKS)
                with act.Fori(0, PAIRS - 1) as i:
                    la(i)
                la(PAIRS - 1, True)
                barrier()
                kxt, mt = wseg(wb_sb, Q_SIZE + 1024, 1024), wseg(wb_sb, Q_SIZE + 2048, 1024)
                act.wait_ge(sem("kx_turned"), b + 1)
                A_(kxt, PS[:, 0:2, :].rearrange("p m n -> p (m n)"), ACT.Copy).then_inc(sem("kxt_ready"), 1)
                act.wait_ge(sem("mt_ready"), b + 1)
                A_(mt, PS[:, 3:5, :].rearrange("p m n -> p (m n)"), ACT.Copy)
                barrier()

                def lb(i):
                    for h in range(2):
                        n, m_, c = i * 2 + (b * CHUNKS + h), i + b * PAIRS, i * 2 + h
                        done(act, "bP", n)
                        act.wait_ge(sem(f"o_stored{h}"), m_ * 32 + 16)
                        room(act, "bS", n)
                        for oc in range(KC):
                            A_(by_parity(i2[6 + h][:, oc * CHUNK:(oc + 1) * CHUNK]), from_rows(chunk_of(img1, oc, c)), ACT.Copy)
                            last = A_(by_parity(i2[4 + h][:, oc * CHUNK:(oc + 1) * CHUNK]), from_rows(PS[:, 2 * h + oc, :]),
                                      ACT.Identity, bias=v("b_out", oc))
                        last.then_inc(sem("bO"), 1)
                loop(ACT.Identity, lb)
                barrier()

            def L3():
                act.wait_ge(sem("o_var"), 1)
                A_(o_sd, o_mv.rearrange("p (k s) -> p s k", s=2)[:, 1, :], ACT.Sqrt, bias=eps_c).then_inc(sem("o_sd_ready"), 1)
                act.wait_ge(sem("o_bn_biased"), 1)

                def scaled(b):
                    for q in range(SETS):
                        act.wait_ge(sem(f"e_o{q % 2}"), 16 * (b * 2 + q // 2 + 1))
                        at = q % 2 * KC + q // 2
                        A_(obuf[q % 2], obuf[q % 2], ACT.Identity, bias=obn4[:, SETS + at:SETS + at + 1], scale=obn4[:, at:at + 1])\
                            .then_inc(sem("eB"), 1)

                def normalised(b):
                    act.wait_ge(sem("e_var_ready"), b + 1)
                    A_(e_sd, e_var, ACT.Sqrt, bias=eps_c).then_inc(sem("e_sd_ready"), 1)
                    act.wait_ge(sem("e_ready"), b + 1)
                    for form in range(3):
                        q = form + 1
                        if b:
                            act.wait_ge(sem("eN"), b * 3 - 2 + form)
                        for lo, hi, late in (((0, P, 0),) if form == 1 else ((0, SC, 0), (SC, P, 1))):
                            last = A_(interior(form, late)[lo:hi], rows(x3[b % 2][lo:hi, q * HALFP:(q + 1) * HALFP]),
                                      ACT.Identity, bias=e_t[lo:hi, q:q + 1], scale=e_s[lo:hi, q:q + 1])
                        last.then_inc(sem("eT"), 1)
                        if b >= 2 and form == 0:
                            act.wait_ge(sem("eC"), 12 * (b - 1))
                        act.wait_ge(sem("eT"), b * 3 + form + 1)
                        A_(pads[b % 2][form][0], padf[form], ACT.Copy).then_inc(sem("eP"), 1)
                    A_(x3[b % 2][:, 0:HALFP], x3[b % 2][:, 0:HALFP], ACT.Identity, bias=e_t[:, 0:1], scale=e_s1[:, 0:1])\
                        .then_inc(sem("eI"), 1)

                scaled(0)
                act.wait_ge(sem("e_cleared"), 1)
                normalised(0)
                for b in range(1, B):
                    scaled(b)
                    normalised(b)
                barrier()

            for phase, b, gi in plan:
                if phase == "REST":
                    barrier()
                elif phase == "L3":
                    L3()
                else:
                    {"A": A, "F": F, "L1": L1, "L2": L2}[phase](b)

        @block.vector
        def _(dve):
            vec = nc.vector
            barrier = Barrier(dve, "dve")
            own = Own(dve, sem("dve_own"))
            link = own.link
            count = {"gn": 0, "wa": 0, "wb": 0}

            def loaded(region):
                count[region] += 1
                dve.wait_ge(sem(region + "_loaded"), 16 * count[region])

            def unit(b, t, g, j):
                dve.wait_ge(sem(f"gathered{g}"), t * (16 * K2) + 16 * K2 * (b * TILES + 1))
                rg = ring[:, g, :].rearrange("p (k c) -> p k c", c=GC)
                weights = seg(wt, t * (PTS * CORNERS) + g * K2 * CORNERS, K2 * CORNERS)
                vec.tensor_tensor(rg, rg, weights.unsqueeze(2).to_broadcast([P, K2 * CORNERS, GC]), ALU.mult)\
                    .then_inc(sem("weighted"), 1)
                dve.wait_ge(sem("weighted"), t * G + (b * TILES * G + g + 1))
                if g == 0:
                    dve.wait_ge(sem("d_stored"), t * 16 + (16 * b * TILES + 16 - 16 * j))
                vec.tensor_reduce(dbuf[:, j, g * GC:(g + 1) * GC], ring[:, g, :].rearrange("p (k c) -> p c k", c=GC),
                                  AX_X, ALU.add).then_inc(sem("ring_free"), 1)

            stream = Stream(unit)

            def chunks(part, gi, per, body, last_body=None, sums_first=False):
                if gi is not None:
                    dve.wait_ge(sem("wt_loaded"), 16 * (gi + 1))
                turns = PAIRS - 1 if last_body else PAIRS
                own.settle()
                with dve.Fori(0, turns) as i:
                    own.enter(i, per)
                    stream.begin(part, gi, i)
                    if sums_first:
                        stream.finish()
                    body(i)
                    stream.finish()
                own.leave(turns)
                if last_body:
                    stream.begin(part, None if part == "L2b" else gi, turns)
                    last_body(turns)
                    stream.finish()
                stream.ended(part, gi, turns if part == "L2b" else PAIRS)

            def moments_from(stats_):
                count["gn"] += 1
                q = count["gn"]
                for k in range(KC):
                    last = vec.bn_aggr(mv[:, 2 * k:2 * k + 2], stats_[:, k * 48:(k + 1) * 48].rearrange("p (c s) -> p c s", s=6))
                link(last)
                m_, va = mv.rearrange("p (k s) -> p s k", s=2)[:, 0, :], mv.rearrange("p (k s) -> p s k", s=2)[:, 1, :]
                ms2 = ms.rearrange("p (s k) -> p s k", s=2)
                link(vec.tensor_tensor(ms2[:, 1, :], m_, m_, ALU.mult))
                vec.tensor_copy(ms2[:, 0, :], m_)
                vec.tensor_tensor(ms2[:, 1, :], ms2[:, 1, :], va, ALU.add).then_inc(sem("gn_moments"), 1)
                dve.wait_ge(sem("gn_grouped"), q)
                link(vec.tensor_copy(gm, PS[:, 7, 0:4]))
                link(vec.tensor_tensor(gsq[:, 0:2], gm[:, 0:2], gm[:, 0:2], ALU.mult))
                link(vec.tensor_tensor(gvar, gm[:, 2:4], gsq[:, 0:2], ALU.subtract))
                vec.tensor_scalar(gvar, gvar, 0.0, None, ALU.max).then_inc(sem("gn_var"), 1)
                dve.wait_ge(sem("gn_sd"), q)
                link(vec.reciprocal(gn_s, gsd))
                vec.scalar_tensor_tensor(out=gn_t, in0=gm[:, 0:2], scalar=-1.0, in1=gn_s, op0=ALU.mult, op1=ALU.mult)\
                    .then_inc(sem("gn_ready"), 1)
                dve.wait_ge(sem("gn_ready"), q)

            def image_stats(b):
                for k in range(KC):
                    dve.wait_ge(sem(f"x_loaded{k}"), 16 * (b + 1))
                    for c in range(CHUNKS):
                        last = vec.bn_stats(stats[:, (k * CHUNKS + c) * 6:(k * CHUNKS + c + 1) * 6],
                                            img1[:, k * HW + c * CHUNK:k * HW + (c + 1) * CHUNK])
                link(last)

            def leaky(o, i):
                return vec.scalar_tensor_tensor(out=o, in0=i, scalar=SLOPE, in1=i, op0=ALU.mult, op1=ALU.max)

            def clear_borders():
                for k in range(KC):
                    pl = img2[:, k * YPLANE:(k + 1) * YPLANE]
                    vec.memset(pl[:, 0:YPITCH + 1], 0.0)
                    vec.memset(pl[:, 2 * YPITCH - 1:(H + 1) * YPITCH - 1].rearrange("p (r x) -> p r x", x=YPITCH)[:, :, 0:2], 0.0)
                    vec.memset(pl[:, (H + 1) * YPITCH - 1:YPLANE], 0.0)

            def setup():
                vec.memset(dbuf[:, 0, :], 0.0).then_inc(sem("zeros"), 1)
                vec.memset(eps_c, EPS)
                vec.memset(one_c, 1.0)
                vec.memset(neg_one, -1.0)
                dve.wait_ge(sem("par_loaded"), 16)
                for j, nm in enumerate(("bn1", "dwbn", "bn2")):
                    last = vec.tensor_copy(bnv[:, 2 * j:2 * j + 2], v(nm + "_v"))
                last.then_inc(sem("bn_var"), 1)
                dve.wait_ge(sem("bn_sd"), 1)
                link(vec.reciprocal(bninv, bnv))
                for j, nm in enumerate(("bn1", "dwbn", "bn2")):
                    last = vec.tensor_tensor(bninv[:, 2 * j:2 * j + 2], bninv[:, 2 * j:2 * j + 2], v(nm + "_g"), ALU.mult)
                link(last)
                for j, nm in enumerate(("bn1", "dwbn", "bn2")):
                    last = vec.tensor_tensor(bnsh[:, 2 * j:2 * j + 2], bninv[:, 2 * j:2 * j + 2], v(nm + "_m"), ALU.mult)
                link(last)
                for j, nm in enumerate(("bn1", "dwbn", "bn2")):
                    last = vec.tensor_tensor(bnsh[:, 2 * j:2 * j + 2], v(nm + "_b"), bnsh[:, 2 * j:2 * j + 2], ALU.subtract)
                link(last)
                link(vec.tensor_tensor(gsq[:, 0:2], bninv[:, 2:4], v("dw_b"), ALU.mult))
                link(vec.tensor_tensor(bnsh[:, 2:4], bnsh[:, 2:4], gsq[:, 0:2], ALU.add))

            def A(b, gi):
                if b == 0:
                    setup()
                clear_borders()
                if gi is not None:
                    dve.wait_ge(sem("wt_loaded"), 16 * (gi + 1))
                    stream.extra(gi)
                image_stats(b)
                if gi is not None and b < B - 1:
                    stream.extra(gi)
                moments_from(stats)
                loaded("wa")
                dve.wait_ge(sem("a_bias"), b + 1)
                link(vec.tensor_tensor(cb1, PS[:, 6, 0:2], bninv[:, 0:2], ALU.mult))
                vec.tensor_tensor(cb1, cb1, bnsh[:, 0:2], ALU.add)
                for k in range(KC):
                    w_ = wa_sb[:, A_CONV + k * C:A_CONV + (k + 1) * C]
                    last = vec.tensor_scalar(w_, w_, gn_s[:, k:k + 1], None, ALU.mult)
                link(last)
                barrier()

                def a1(i):
                    for h in range(2):
                        n = i * 2 + (b * CHUNKS + h)
                        stream.give(1, 4)
                        done(dve, "aZ", n)
                        leaky(ych[h], ych[h]).then_inc(sem("aY"), 1)
                    for h in range(2):
                        n, m = i * 2 + (b * CHUNKS + h), i + b * PAIRS
                        done(dve, "aX", n)
                        dve.wait_ge(sem(f"t_stored{h}"), m * (16 * CORNERS) + 16)
                        vec.tensor_tensor(xpt[h].rearrange("p (s c) -> p s c", s=SUBS),
                                          PS[:, 4 + 2 * h:6 + 2 * h, :].rearrange("p a (s c) -> p (a s) c", s=2),
                                          v("inproj_row").unsqueeze(1).to_broadcast([P, SUBS, C]), ALU.add)\
                            .then_inc(sem("aXE"), 1)
                chunks("A1", gi, 0, a1)
                barrier()
                OM = img1[:, 0:TILES * 3 * PTS]

                def depthwise(i, streaming=True):
                    for tap in range(K2):
                        w_ = v("dw_taps", tap)
                        for h in range(2):
                            acc, src = rows(dwacc[h]), padded(1, i * 2 + h, tap // 3, tap % 3)
                            if tap == 0:
                                last = vec.tensor_scalar(acc, src, w_, None, ALU.mult)
                            else:
                                last = vec.scalar_tensor_tensor(out=acc, in0=src, scalar=w_, in1=acc, op0=ALU.mult, op1=ALU.add)
                        if tap < K2 - 1:
                            link(last)
                        if streaming and tap % 4 == 3:
                            stream.give(1, 16)
                    last.then_inc(sem("dW"), 1)

                def a2(i, last_pair=False):
                    for h in range(2):
                        n = i * 2 + (b * CHUNKS + h)
                        done(dve, "dZ", n)
                        leaky(ych[h], ych[h]).then_inc(sem("dT"), 1)
                        stream.give(1, 16)
                    if not last_pair:
                        depthwise(i + 1)
                    for h in range(2):
                        n, c = i * 2 + (b * CHUNKS + h), i * 2 + h
                        done(dve, "dO", n)
                        vec.tensor_tensor(seg(OM, c * (SUBS * 3 * PTS), SUBS * 3 * PTS).rearrange("p (s c) -> p s c", s=SUBS),
                                          PS[:, 4 + h, 0:SUBS * 3 * PTS].rearrange("p (s c) -> p s c", s=SUBS),
                                          v("om_row").unsqueeze(1).to_broadcast([P, SUBS, 3 * PTS]), ALU.add)\
                            .then_inc(sem("dE"), 1)
                depthwise(0, False)
                chunks("A2", gi, K2 - 1, a2, lambda i: a2(i, True))
                barrier()

                T = lambda j: img1[:, 3456 + j * 1152:3456 + (j + 1) * 1152] if j < 4 else \
                    img2[:, 4608 + (j - 4) * 1152:4608 + (j - 3) * 1152]
                om3 = OM.rearrange("p (t c) -> p t c", c=3 * PTS)
                ox, oy, ml = (om3[:, :, j * PTS:(j + 1) * PTS] for j in range(3))
                tp = lambda a: a.rearrange("p (t c) -> p t c", c=PTS)
                t9 = lambda a: a.rearrange("p (t k) -> p t k", k=K2)

                def less_maximum():
                    link(vec.tensor_reduce(stats8(0), ml4(ml), AX_X, ALU.max))
                    vec.tensor_tensor(t9(T(6)).rearrange("p (t g) k -> p t g k", g=G), ml4(ml),
                                      stats8(0).unsqueeze(3).to_broadcast([P, TILES, G, K2]), ALU.subtract)\
                        .then_inc(sem("logit_less"), 1)

                if b:
                    less_maximum()
                vec.tensor_tensor(tp(T(0)), ox, v("gx_base").unsqueeze(1).to_broadcast([P, TILES, PTS]), ALU.add)
                link(vec.tensor_tensor(T(1).rearrange("p (t g k) -> p t g k", g=G, k=K2), oy.rearrange("p t (g k) -> p t g k", k=K2),
                                       v("gy_base").rearrange("p (t k) -> p t k", k=K2).unsqueeze(2).to_broadcast([P, TILES, G, K2]),
                                       ALU.add))
                for a, t in ((0, 4), (1, 5)):
                    last = vec.tensor_scalar(T(t), T(a), 0.0, float(W - 2), ALU.max, ALU.min)
                link(last)
                for t in (4, 5):
                    last = vec.tensor_scalar(T(t), T(t), -0.5, MAGIC, ALU.add, ALU.add)
                link(last)
                for t in (4, 5):
                    last = vec.tensor_scalar(T(t), T(t), -MAGIC, None, ALU.add)
                link(last)
                for a, t in ((0, 4), (1, 5)):
                    last = vec.tensor_tensor(T(a), T(a), T(t), ALU.subtract)
                last.then_inc(sem("dx_dy"), 1)
                link(vec.scalar_tensor_tensor(out=T(7), in0=T(5), scalar=float(W), in1=T(4), op0=ALU.mult, op1=ALU.add))
                made = idx[:, 0, :] if b == 0 else img1[:, 0:TILES * PTS].bitcast(U32)
                vec.scalar_tensor_tensor(out=tp(made), in0=tp(T(7)), scalar=float(G),
                                         in1=v("g_base").unsqueeze(1).to_broadcast([P, TILES, PTS]),
                                         op0=ALU.mult, op1=ALU.add)\
                    .then_inc(sem("idx_made"), 1)
                if b == 0:
                    dve.wait_ge(sem("idx_made"), 1)
                    dve.sem_inc(sem("idx_loaded"), 16)
                    less_maximum()
                else:
                    stream.extra(gi)
                dve.wait_ge(sem("mask_exp"), b + 1)
                link(vec.tensor_reduce(stats8(0), T(6).rearrange("p (t g k) -> p t g k", g=G, k=K2), AX_X, ALU.add))
                link(vec.reciprocal(stats8(1), stats8(0)))
                link(vec.tensor_tensor(T(6).rearrange("p (t g k) -> p t g k", g=G, k=K2), T(6).rearrange("p (t g k) -> p t g k", g=G, k=K2),
                                       stats8(1).unsqueeze(3).to_broadcast([P, TILES, G, K2]), ALU.mult))
                dve.wait_ge(sem("hats"), b + 1)
                vec.tensor_tensor(T(4), T(1), T(6), ALU.mult)
                link(vec.tensor_tensor(T(5), T(3), T(6), ALU.mult))
                Wt = (wt[:] if b == 0 else img2[:, 0:4608]).rearrange("p (n j) -> p j n", j=CORNERS)
                for j, (my, wx) in enumerate(((4, 0), (4, 2), (5, 0), (5, 2))):
                    last = vec.tensor_tensor(Wt[:, j, :], T(my), T(wx), ALU.mult)
                last.then_inc(sem("w_made"), 1)
                if b == 0:
                    dve.wait_ge(sem("w_made"), 1)
                    dve.sem_inc(sem("wt_loaded"), 16)
                barrier()

            def stats8(j):
                return cb[:, j * 128:(j + 1) * 128].rearrange("p (t g) -> p t g", g=G)

            def ml4(ml):
                return ml.rearrange("p t (g k) -> p t g k", k=K2)

            def F(b, gi):
                loaded("wb")

                def f1(i):
                    for h in range(2):
                        n, m, c = i * 2 + (b * CHUNKS + h), i + b * PAIRS, i * 2 + h
                        stream.give(1, 4)
                        done(dve, "fO", n)
                        dve.wait_ge(sem(f"fY{h}"), m * 16 + 16)
                        for oc in range(KC):
                            last = vec.scalar_tensor_tensor(out=chunk_of(img1, oc, c), in0=PS[:, 4 + 2 * h + oc, :],
                                                            scalar=v("outproj_b", oc),
                                                            in1=i2[2 + h][:, oc * CHUNK:(oc + 1) * CHUNK],
                                                            op0=ALU.add, op1=ALU.add)
                        last.then_inc(sem("fR"), 1)
                        stream.give(1, 4)
                chunks("F1", gi, 0, f1, sums_first=b == B - 1)
                if b == B - 1:
                    gi = None
                barrier()
                link(vec.tensor_reduce(rsum, rsums.rearrange("p (k c) -> p k c", k=KC), AX_X, ALU.add))
                link(vec.tensor_scalar(xmean, rsum, 1.0 / HW, None, ALU.mult))
                link(vec.tensor_tensor(xmean, xmean, bninv[:, 4:6], ALU.mult))
                vec.tensor_tensor(xmean, xmean, bnsh[:, 4:6], ALU.add).then_inc(sem("se_mean"), 1)
                dve.wait_ge(sem("se_down"), b + 1)
                vec.tensor_scalar(s_hid[0:64, 0:1], PS[0:64, 7, 0:1], v("se_down_b", 0, 64), 0.0, ALU.add, ALU.max)\
                    .then_inc(sem("se_hidden"), 1)
                dve.wait_ge(sem("se_up"), b + 1)
                vec.tensor_tensor(s_z, PS[:, 6, 0:2], v("se_up_b"), ALU.add).then_inc(sem("se_z"), 1)
                dve.wait_ge(sem("se_exp"), b + 1)
                link(vec.tensor_scalar(s_g, s_e, 1.0, None, ALU.add))
                link(vec.reciprocal(s_g, s_g))
                vec.tensor_tensor(s_ga, s_g, bninv[:, 4:6], ALU.mult)
                vec.tensor_tensor(s_gc, s_g, bnsh[:, 4:6], ALU.mult).then_inc(sem("se_gate"), 1)
                dve.wait_ge(sem("fc1_shift"), b + 1)
                vec.tensor_tensor(fb, PS[:, 5, 0:FC], v("fc1_b"), ALU.add)
                for k in range(KC):
                    w_ = wb_sb[:, F_FC1 + k * 4 * C:F_FC1 + (k + 1) * 4 * C]
                    last = vec.tensor_scalar(w_, w_, s_ga[:, k:k + 1], None, ALU.mult)
                link(last)
                barrier()

                def f2(i):
                    for h in range(2):
                        n, m, c = i * 2 + (b * CHUNKS + h), i + b * PAIRS, i * 2 + h
                        for q in range(4):
                            done(dve, "gZ", n * 4 + q)
                            room(dve, "gD", n * 4 + q)
                            leaky(i2[6 + q % 2], i2[4 + q % 2]).then_inc(sem("gB"), 1)
                            stream.give(1, 8)
                        done(dve, "gD", n * 4 + 3)
                        dve.wait_ge(sem(f"gYl{h}"), m * 16 + 16)
                        for oc in range(KC):
                            last = vec.scalar_tensor_tensor(out=i2[8][:, oc * CHUNK:(oc + 1) * CHUNK], in0=PS[:, 4 + 2 * h + oc, :],
                                                            scalar=v("fc2_b", oc), in1=i2[h][:, oc * CHUNK:(oc + 1) * CHUNK],
                                                            op0=ALU.add, op1=ALU.add)
                        link(last)
                        dve.wait_ge(sem(f"gXl{h}"), m * 16 + 16)
                        for oc in range(KC):
                            last = vec.tensor_tensor(chunk_of(img1, oc, c), i2[8][:, oc * CHUNK:(oc + 1) * CHUNK],
                                                     i2[2 + h][:, oc * CHUNK:(oc + 1) * CHUNK], ALU.add)
                        last.then_inc(sem("gX"), 1)
                        done(dve, "gX", n)
                        for k in range(KC):
                            vec.bn_stats(seg(stats, c * 6 + k * 48, 6), chunk_of(img1, k, c))
                chunks("F2", gi, 2, f2)
                barrier()

            def L1(b, gi):
                clear_borders()
                moments_from(stats)
                link(vec.tensor_tensor(pooled, mv.rearrange("p (k s) -> p s k", s=2)[:, 0, :], gn_s, ALU.mult))
                vec.tensor_tensor(pooled, pooled, gn_t, ALU.add).then_inc(sem("pooled"), 1)
                loaded("wa")
                dve.wait_ge(sem("l1_hidden"), b + 1)
                vec.tensor_scalar(a_hid[0:64, :], PS[0:64, 6, 0:1], v("ap_b1", 0, 64), 0.0, ALU.add, ALU.max)
                vec.tensor_scalar(m_hid[0:64, :], PS[0:64, 6, 1:2], v("meta_b1", 0, 64), 0.0, ALU.add, ALU.max)\
                    .then_inc(sem("l1_relu"), 1)
                dve.wait_ge(sem("l1_heads"), b + 1)
                vec.tensor_tensor(ang, PS[:, 5, 0:2], v("ap_b2"), ALU.add)
                vec.tensor_tensor(mz, PS[:, 5, 2:4], v("meta_b2"), ALU.add).then_inc(sem("l1_z"), 1)
                dve.wait_ge(sem("l1_tanh"), b + 1)
                link(vec.tensor_scalar(ang, ang, 0.7853981633974483, None, ALU.mult))
                vec.tensor_scalar(cos_c, ang, 1.5707963267948966, None, ALU.add).then_inc(sem("l1_angle"), 1)
                link(vec.tensor_scalar(mod, mz, 1.0, None, ALU.add))
                link(vec.reciprocal(mod, mod))
                lt = wseg(wa_sb, R_SIZE, KC * K2 * P)
                if b == 0:
                    link(vec.memset(lt, 0.0))
                if gi is not None:
                    stream.extra(gi)
                dve.wait_ge(sem("l1_sincos"), b + 1)
                tx, ty, tnx = v("tap_x"), v("tap_y"), v("tap_nx")
                kk = [slice(k * K2, (k + 1) * K2) for k in range(KC)]
                for k in range(KC):
                    vec.tensor_scalar(U[:, kk[k]], tx, cos_c[:, k:k + 1], None, ALU.mult)
                    last = vec.tensor_scalar(V_[:, kk[k]], ty, cos_c[:, k:k + 1], None, ALU.mult)
                link(last)
                for k in range(KC):
                    vec.scalar_tensor_tensor(out=U[:, kk[k]], in0=ty, scalar=sin_c[:, k:k + 1], in1=U[:, kk[k]],
                                             op0=ALU.mult, op1=ALU.add)
                    last = vec.scalar_tensor_tensor(out=V_[:, kk[k]], in0=tnx, scalar=sin_c[:, k:k + 1], in1=V_[:, kk[k]],
                                                    op0=ALU.mult, op1=ALU.add)
                last.then_inc(sem("l1_uv"), 1)
                dve.wait_ge(sem("l1_hats"), b + 1)
                for t in (BX, AY):
                    last = vec.tensor_scalar(t[:, 18:36], t[:, 18:36], -1.0, 1.0, ALU.mult, ALU.add)
                link(last)
                cf = coef.rearrange("p (n q) -> p n q", n=K2)
                for j in range(3):
                    for i in range(3):
                        last = vec.tensor_tensor(cf[:, j * 3 + i, :], AY[:, j * 18:(j + 1) * 18], BX[:, i * 18:(i + 1) * 18], ALU.mult)
                link(last)
                acc = cb[:, KC * K2 * K2:KC * K2 * (K2 + CG)].rearrange("p (k t o) -> p k t o", k=KC, t=K2)
                prod = cb[:, KC * K2 * (K2 + CG):KC * K2 * (K2 + 2 * CG)].rearrange("p (k t o) -> p k t o", k=KC, t=K2)
                base = wseg(wa_sb, R_BASE, KC * K2 * CG).rearrange("p (k t o) -> p k t o", k=KC, t=K2)
                lt4 = lt.rearrange("p (k t o) -> p k t o", k=KC, t=K2)
                for n in range(K2):
                    dst = acc if n == 0 else prod
                    for k in range(KC):
                        last = vec.tensor_tensor(dst[:, k], base[:, k, n, :].unsqueeze(1).to_broadcast([P, K2, CG]),
                                                 cf[:, n, k * K2:(k + 1) * K2].unsqueeze(2).to_broadcast([P, K2, CG]), ALU.mult)
                    link(last)
                    if 0 < n < K2 - 1:
                        link(vec.tensor_tensor(acc, acc, prod, ALU.add))
                for q in range(P // CG):
                    r_ = slice(q * CG, (q + 1) * CG)
                    last = vec.tensor_tensor(lt4[r_, :, :, r_], acc[r_], prod[r_], ALU.add)
                link(last)
                barrier()

                def l1(i):
                    for h in range(2):
                        n, c = i * 2 + (b * CHUNKS + h), i * 2 + h
                        stream.give(1, 4)
                        done(dve, "lC", n)
                        for k in range(KC):
                            last = vec.scalar_tensor_tensor(out=chunk_of(img1, k, c), in0=PS[:, 2 * h + k, :], scalar=mod[:, k:k + 1],
                                                            in1=chunk_of(img1, k, c), op0=ALU.mult, op1=ALU.add)
                        last.then_inc(sem("lX"), 1)
                        done(dve, "lX", n)
                        for k in range(KC):
                            vec.bn_stats(seg(stats, c * 6 + k * 48, 6), chunk_of(img1, k, c))
                        stream.give(1, 4)
                chunks("L1" if gi != B - 1 else "L1 last", gi, 0, l1)
                barrier()

            def L2(b, gi):
                kx = wseg(wb_sb, Q_SIZE, 1024)
                bd = wseg(wb_sb, Q_SIZE + 3072, 512)
                loaded("wb")
                vec.memset(kmax, -3.0e38)
                vec.memset(ksum, 0.0)
                vec.memset(kx, 0.0)
                vec.memset(bd, 0.0)
                moments_from(stats)
                barrier()
                QS = img2[:, 4096:6144]

                def maximum(n):
                    for half in range(2):
                        s2 = slice(2 * half, 2 * half + 2)
                        dve.wait_ge(sem("cK"), n * 2 + (1 + half))
                        link(vec.tensor_reduce(cmax[:, s2], PS[:, s2, :], AX_X, ALU.max))
                        link(vec.tensor_tensor(knew[:, s2], kmax[:, s2], cmax[:, s2], ALU.max))
                        vec.tensor_tensor(kdif[:, s2], kmax[:, s2], knew[:, s2], ALU.subtract)
                        vec.tensor_scalar(kneg[:, s2], knew[:, s2], -1.0, None, ALU.mult).then_inc(sem("cM"), 1)
                        dve.wait_ge(sem("cM"), n * 2 + (1 + half))
                        last = vec.tensor_copy(kmax[:, s2], knew[:, s2])
                    link(last)

                def la(i, last_pair=False):
                    for h in range(2):
                        n = i * 2 + (b * CHUNKS + h)
                        for half in range(2):
                            q3 = PS[:, 2 - 2 * half:4 - 2 * half, :].rearrange("p s (a d) -> p (s a) d", d=DH)
                            mx = qmax[:, half * 16:(half + 1) * 16]
                            dve.wait_ge(sem("cQ"), n * 2 + (1 + half))
                            link(vec.tensor_reduce(mx, q3, AX_X, ALU.max))
                            dve.wait_ge(sem("cQT"), n * 2 + 1)
                            vec.tensor_tensor(QS[:, half * 1024:(half + 1) * 1024].rearrange("p (a d) -> p a d", d=DH), q3,
                                              mx.unsqueeze(2).to_broadcast([P, 16, DH]), ALU.subtract).then_inc(sem("cQs"), 1)
                        stream.give(1, 4)
                        dve.wait_ge(sem("cQe"), n * 2 + 2)
                        qs3 = QS.rearrange("p (a d) -> p a d", d=DH)
                        link(vec.tensor_reduce(qsum, qs3, AX_X, ALU.add))
                        link(vec.reciprocal(qsum, qsum))
                        vec.tensor_tensor(qs3, qs3, qsum.unsqueeze(2).to_broadcast([P, 32, DH]), ALU.mult).then_inc(sem("cQn"), 1)
                        done(dve, "cKs", n * 4 + 3)
                        link(vec.tensor_tensor(ksum, ksum, kalpha, ALU.mult))
                        vec.tensor_tensor(ksum, ksum, esum, ALU.add)
                        for m in range(KH):
                            last = vec.scalar_tensor_tensor(out=kx[:, m * C:(m + 1) * C], in0=kx[:, m * C:(m + 1) * C],
                                                            scalar=kalpha[:, m:m + 1],
                                                            in1=PS[:, 4 + m // 2, (m % 2) * C:(m % 2 + 1) * C],
                                                            op0=ALU.mult, op1=ALU.add)
                        last.then_inc(sem("cS"), 1)
                        dve.wait_ge(sem("cS"), n + 2)
                        if not (last_pair and h == 1):
                            maximum(n + 1)
                        stream.give(1, 4)
                maximum(b * CHUNKS)
                chunks("L2a", gi, 20, la, lambda i: la(i, True))
                barrier()
                link(vec.reciprocal(ksum, ksum))
                link(vec.tensor_scalar(ksum, ksum, DH ** -0.5 / HW, None, ALU.mult))
                for m in range(KH):
                    last = vec.tensor_scalar(kx[:, m * C:(m + 1) * C], kx[:, m * C:(m + 1) * C], ksum[:, m:m + 1], None, ALU.mult)
                last.then_inc(sem("kx_scaled"), 1)
                dve.wait_ge(sem("ctx_ready"), b + 1)
                for q in range(2):
                    r = slice(q * DH, (q + 1) * DH)
                    last = vec.tensor_copy(bd.rearrange("p (m d) -> p m d", m=KH)[r, :, r],
                                           PS[:, 2, :].rearrange("p (m d) -> p m d", m=KH)[r, :, r])
                last.then_inc(sem("ctx_diagonal"), 1)
                barrier()

                if b == B - 1:
                    quantise()

                def lb(i):
                    for h in range(2):
                        n, c = i * 2 + (b * CHUNKS + h), i * 2 + h
                        stream.give(1, 4)
                        done(dve, "bO", n)
                        for k in range(KC):
                            last = vec.bn_stats(seg(ostats, c * 6 + (k * B + b) * CHUNKS * 6, 6), i2[4 + h][:, k * CHUNK:(k + 1) * CHUNK])
                        last.then_inc(sem("bS"), 1)
                        stream.give(1, 4)
                chunks("L2b", gi, 0, lb, lb)
                barrier()

            def quantise():
                loaded("wa")
                at = 0
                for form, taps in enumerate((L3_TAPS_H, L3_TAPS_W, L3_TAPS_X)):
                    w_ = wa_sb[:, at * P:(at + len(taps)) * P]
                    at += len(taps)
                    s_ = v("l3_s", form)
                    link(vec.reciprocal(o_rs, s_))
                    link(vec.tensor_scalar(w_, w_, o_rs, MAGIC, ALU.mult, ALU.add))
                    link(vec.tensor_scalar(w_, w_, -MAGIC, -8.0, ALU.add, ALU.max))
                    link(vec.tensor_scalar(w_int[form], w_, 7.0, None, ALU.min))

            def L3():
                for k in range(KC):
                    last = vec.bn_aggr(o_mv[:, 2 * k:2 * k + 2],
                                       ostats[:, k * B * 48:(k + 1) * B * 48].rearrange("p (c s) -> p c s", s=6))
                last.then_inc(sem("o_var"), 1)
                dve.wait_ge(sem("o_sd_ready"), 1)
                o_sc, o_sh = o_bn[:, 0:KC], o_bn[:, KC:2 * KC]
                link(vec.reciprocal(o_sc, o_sd))
                link(vec.tensor_tensor(o_sc, o_sc, v("gamma"), ALU.mult))
                link(vec.tensor_tensor(o_sh, o_mv.rearrange("p (k s) -> p s k", s=2)[:, 0, :], o_sc, ALU.mult))
                vec.tensor_tensor(o_sh, v("beta"), o_sh, ALU.subtract).then_inc(sem("o_bn_ready"), 1)
                vec.memset(img2[:, 0:FIRST[3]], 0.0).then_inc(sem("e_cleared"), 1)
                bias = v("l3_b")
                dve.wait_ge(sem("o_bn_moved"), 64)
                shift = obn4[:, SETS:].rearrange("p (j k) -> p j k", j=2)
                vec.tensor_tensor(shift, shift, bias.rearrange("p (k j) -> p j k", j=2), ALU.add).then_inc(sem("o_bn_biased"), 1)

                def summed(b, q):
                    xs = x3[b % 2][:, q * HALFP:(q + 1) * HALFP]
                    dve.wait_ge(sem(f"e_x{b % 2}{q}"), 16 * (b // 2 + 1))
                    dve.wait_ge(sem("eB"), b * SETS + q + 1)
                    vec.tensor_tensor(xs, xs, obuf[q % 2], ALU.add).then_inc(sem("eA"), 1)
                    dve.wait_ge(sem("eA"), b * SETS + q + 1)
                    for j in range(4):
                        last = vec.bn_stats(stats[:, (q * 4 + j) * 6:(q * 4 + j + 1) * 6], xs[:, j * CHUNK:(j + 1) * CHUNK])
                    link(last)

                def moments(b):
                    for q in range(SETS):
                        last = vec.bn_aggr(e_mv[:, 2 * q:2 * q + 2], stats[:, q * 24:(q + 1) * 24].rearrange("p (c s) -> p c s", s=6))
                    link(last)
                    m_, va = (e_mv.rearrange("p (q s) -> p s q", s=2)[:, j, :] for j in range(2))
                    link(vec.tensor_tensor(e_ms[:, 0:SETS], m_, bias, ALU.subtract))
                    link(vec.tensor_tensor(e_ms[:, SETS:], e_ms[:, 0:SETS], e_ms[:, 0:SETS], ALU.mult))
                    vec.tensor_tensor(e_ms[:, SETS:], e_ms[:, SETS:], va, ALU.add).then_inc(sem("e_moments"), 1)

                def factors(b):
                    dve.wait_ge(sem("e_grouped"), b + 1)
                    link(vec.tensor_copy(e_gm, PS[:, 7, 0:2 * SETS]))
                    link(vec.tensor_tensor(e_sq, e_gm[:, 0:SETS], e_gm[:, 0:SETS], ALU.mult))
                    link(vec.tensor_tensor(e_var, e_gm[:, SETS:], e_sq, ALU.subtract))
                    vec.tensor_scalar(e_var, e_var, 0.0, None, ALU.max).then_inc(sem("e_var_ready"), 1)
                    dve.wait_ge(sem("e_sd_ready"), b + 1)
                    link(vec.reciprocal(e_s, e_sd))
                    vec.tensor_scalar(e_s1, e_s, 1.0, None, ALU.add)
                    link(vec.tensor_tensor(e_t, e_gm[:, 0:SETS], bias, ALU.add))
                    vec.scalar_tensor_tensor(out=e_t, in0=e_t, scalar=-1.0, in1=e_s, op0=ALU.mult, op1=ALU.mult)\
                        .then_inc(sem("e_ready"), 1)

                def second_part(b, form):
                    dve.wait_ge(sem("eP"), b * 3 + form + 1)
                    vec.tensor_tensor(pads[b % 2][form][1], padf[form], pads[b % 2][form][0], ALU.subtract)\
                        .then_inc(sem("eN"), 1)

                def finish(b, half, form):
                    for i in range(2):
                        k = b * 12 + half * 6 + form * 2 + i
                        dve.wait_ge(sem("eC"), k + 1)
                        at = (form + 1) * HALFP + (half * 2 + i) * CHUNK
                        xs = x3[b % 2][:, at:at + CHUNK]
                        vec.scalar_tensor_tensor(out=xs, in0=PS[:, form * 2 + i, :], scalar=v("l3_s", form), in1=xs,
                                                 op0=ALU.mult, op1=ALU.add).then_inc(sem("eX"), 1)

                for q in range(SETS):
                    summed(0, q)
                moments(0)
                factors(0)
                for form in range(3):
                    second_part(0, form)
                for b in range(B):
                    more = b + 1 < B
                    for form in range(3):
                        if more:
                            summed(b + 1, form)
                        finish(b, 0, form)
                    if more:
                        summed(b + 1, 3)
                        moments(b + 1)
                    finish(b, 1, 0)
                    if more:
                        factors(b + 1)
                    finish(b, 1, 1)
                    if more:
                        second_part(b + 1, 0)
                    finish(b, 1, 2)
                    if more:
                        second_part(b + 1, 1)
                        second_part(b + 1, 2)
                barrier()

            for phase, b, gi in plan:
                if phase == "REST":
                    stream.rest(dve, gi)
                    barrier()
                elif phase == "L3":
                    L3()
                else:
                    {"A": A, "F": F, "L1": L1, "L2": L2}[phase](b, gi)


def _lay_out(i):
    import numpy as np
    f = np.float32
    a = {k: np.asarray(x) for k, x in i.items()}

    def g(name):
        return a[name]

    def turned(w):
        o, n = w.shape
        return np.ascontiguousarray(w.T.reshape(n // P, P, o).transpose(1, 0, 2)).reshape(P, -1)

    def low(w):
        z = np.zeros((P, w.shape[0]), f)
        z[:w.shape[1]] = w.T
        return z

    par = np.zeros((P, NPAR), f)

    def put(name, value):
        c, w = COL[name]
        par[:value.shape[0], c:c + w] = value

    def vec(name, value):
        n = value.shape[0]
        put(name, value.reshape(n // P, P).T if n >= P else value[:, None])

    L = "L0_conv_"
    for nm in ("bn1_g", "bn1_b", "bn1_m", "bn1_v", "dwbn_g", "dwbn_b", "dwbn_m", "dwbn_v", "dw_b",
               "bn2_g", "bn2_b", "bn2_m", "bn2_v", "outproj_b", "fc1_b", "fc2_b", "se_down_b", "se_up_b"):
        vec(nm, g(L + nm))
    vec("ap_b1", g("L1_conv_ap_b1"))
    vec("ap_b2", np.repeat(g("L1_conv_ap_b2"), CG))
    vec("meta_b1", g("L1_conv_meta_b1"))
    vec("meta_b2", g("L1_conv_meta_b2"))
    vec("b_out", g("L2_conv_b_out"))
    vec("gamma", g("L2_conv_gamma"))
    vec("beta", g("L2_conv_beta"))
    put("l3_b", np.stack([np.zeros(P, f)] + [np.tile(g(n), 2) for n in ("L3_conv_b_h", "L3_conv_b_w", "L3_conv_b_hw")], 1))
    put("l3_s", np.stack([np.broadcast_to(g(n).reshape(1), (P,)) for n in ("L3_conv_s_h", "L3_conv_s_w", "L3_conv_s_hw")], 1))
    put("inproj_row", np.broadcast_to(g(L + "inproj_b"), (P, C)))
    ob = g(L + "off_b")
    put("om_row", np.broadcast_to(np.concatenate([ob[0::2], ob[1::2], g(L + "mask_b")]), (P, 3 * PTS)))
    put("ident", np.eye(P, dtype=f))
    put("gavg", np.kron(np.eye(P // 8, dtype=f), np.full((8, 8), 0.125, f)))
    tap = np.arange(K2)
    for nm, value in (("tap_x", tap % 3 - 1), ("tap_y", tap // 3 - 1), ("tap_nx", 1 - tap % 3)):
        put(nm, np.broadcast_to(value.astype(f), (P, K2)))
    put("gavg2", np.kron(np.ones((2, 2), f), np.kron(np.eye(SC // 8, dtype=f), np.full((8, 8), 0.0625, f))))
    pix = np.arange(P)
    put("gx_base", (pix % W)[:, None] + (DIL * (np.arange(PTS) % K2 // 3 - 1))[None, :].astype(f))
    hy = (pix // W)[:, None, None] + (2 * np.arange(TILES))[None, :, None] + (DIL * (np.arange(K2) % 3 - 1))[None, None, :]
    put("gy_base", hy.reshape(P, -1).astype(f))
    put("g_base", np.broadcast_to(np.arange(PTS) // K2 + TAB_FRONT * G, (P, PTS)).astype(f))

    ow = g(L + "off_w")
    om = np.concatenate([ow[0::2], ow[1::2], g(L + "mask_w")])
    dw = np.zeros((P, K2, P), f)
    taps = g(L + "dw_w").reshape(KC, P, K2)
    for t in range(K2):
        dw[pix, t, pix] = taps[0, :, t]
    put("dw_taps", taps[1])
    wa = np.concatenate([turned(g(L + "conv_w")), turned(g(L + "inproj_w")), turned(om), dw.reshape(P, -1)], 1)
    wf = np.concatenate([turned(g(L + "outproj_w")), turned(g(L + "fc1_w")), turned(g(L + "fc2_w")),
                         turned(g(L + "se_down_w")), low(g(L + "se_up_w"))], 1)
    bk = g("L1_conv_base_kernel").reshape(KC, P // CG, CG, CG, K2)
    bk = bk.transpose(1, 3, 0, 4, 2).reshape(P, -1)
    wr = np.concatenate([bk, turned(g("L1_conv_ap_w1")), turned(g("L1_conv_meta_w1")),
                         low(np.repeat(g("L1_conv_ap_w2"), CG, axis=0)), low(g("L1_conv_meta_w2"))], 1)
    qkv = g("L2_conv_w_qkv")
    wq = np.concatenate([turned(qkv[0:HID]), turned(qkv[HID:2 * HID]), turned(qkv[2 * HID:]), turned(g("L2_conv_w_out"))], 1)

    w3 = np.zeros((P, L3_TAPS, P), f)

    def place(t, pi, po, w, ky, kx):
        for q in range(0, SC, 4):
            w3[pi * SC + q:pi * SC + q + 4, t, po * SC + q:po * SC + q + 4] = w[q:q + 4, :, ky, kx].T

    t = 0
    for taps, nm, up, left in ((L3_TAPS_H, "h", 5, 0), (L3_TAPS_W, "w", 0, 5), (L3_TAPS_X, "hw", 1, 1)):
        for d, dx in taps:
            for pi in range(2):
                for po in range(2):
                    dy = 2 * d + pi - po - (2 * pi if up else 0)
                    if abs(dy) <= up:
                        place(t, pi, po, g("L3_conv_w_" + nm), dy + up, dx + left)
            t += 1
    return dict(x=a["x"], par=par, wa=wa, wr=wr, wf=wf, wq=wq, w3=w3.reshape(P, -1))


def kernel(**inputs):
    import numpy as _np
    import concourse.bacc as _bacc
    from concourse import mybir as _mybir
    from concourse.bass_utils import run_bass_kernel_spmd as _run

    nc = _bacc.Bacc("TRN2", target_bir_lowering=False, num_devices=1)
    arrays, args = {}, []
    for name, a in _lay_out(inputs).items():
        a = _np.ascontiguousarray(a)
        arrays[f"in_{name}"] = a
        args.append(nc.dram_tensor(f"in_{name}", a.shape, _mybir.dt.from_np(a.dtype), kind="ExternalInput").ap())
    args.append(nc.dram_tensor("out", (B, C, H, W), F32, kind="ExternalOutput").ap())
    network_kernel(nc, *args)
    r = _run(nc, [arrays], core_ids=[0])
    return r.results[0]["out"]
```
